# Optimizing a Trainium2 kernel written in Bass

```python
import numpy as np
import jax
import jax.numpy as jnp

def _softmax(x, axis=-1):
    return jax.nn.softmax(x, axis=axis)

def _gelu(x):
    return jax.nn.gelu(x, approximate=True)

def _silu(x):
    return jax.nn.silu(x)

def _sigmoid(x):
    return jax.nn.sigmoid(x)

def _layernorm(x, axis=-1, eps=1e-05):
    m = jnp.mean(x, axis=axis, keepdims=True)
    v = jnp.var(x, axis=axis, keepdims=True)
    return (x - m) / jnp.sqrt(v + eps)

def _scatter_add(tgt, idx, src, axis=0):
    return tgt.at[idx].add(src)

def _segment_sum(src, seg, n):
    return jax.ops.segment_sum(src, seg, n)
kernel_name = 'mk_audio_tower_d1_tok_audfeat768_r4_1a353d'

def setup_inputs(seed: int=0):
    np.random.seed(seed)
    _w = jnp.asarray

    def _rec_inputs():
        import jax
        import jax.numpy as jnp
        _rk = jax.random.key(seed)
        x = -4.65018e-05 + 0.999886 * jax.random.normal(jax.random.fold_in(_rk, 1), (8, 1024, 192), jnp.float32)
        return x
    x = _rec_inputs()

    def _L0_tok_setup():
        import jax, jax.numpy as jnp
        import numpy as np
        HEADS = 12
        DIM = 192
        DIM_OUT = 192
        HEAD_DIM = DIM_OUT // HEADS
        Q_STRIDE = 4
        WINDOW_SIZE = 64
        key = jax.random.key(seed)
        ks = jax.random.split(key, 5)
        B, N = (16, 1024)
        x = jax.random.normal(ks[0], (B, N, DIM), dtype=jnp.float32)
        qkv_w = jax.random.normal(ks[1], (3 * DIM_OUT, DIM), dtype=jnp.float32) * DIM ** (-0.5)
        qkv_b = jax.random.normal(ks[2], (3 * DIM_OUT,), dtype=jnp.float32) * 0.02
        proj_w = jax.random.normal(ks[3], (DIM_OUT, DIM_OUT), dtype=jnp.float32) * DIM_OUT ** (-0.5)
        proj_b = jax.random.normal(ks[4], (DIM_OUT,), dtype=jnp.float32) * 0.02
        return {'x': x, 'qkv_w': qkv_w, 'qkv_b': qkv_b, 'proj_w': proj_w, 'proj_b': proj_b}
    _L0_tok_all = _L0_tok_setup()
    _L0_tok_in = {k: v for k, v in _L0_tok_all.items() if k in ('qkv_w', 'qkv_b', 'proj_w', 'proj_b')}
    del _L0_tok_all

    def _L0_attn_setup():
        import jax, jax.numpy as jnp
        import numpy as np
        D_MODEL = 192
        D_STATE = 64
        D_CONV = 4
        EXPAND = 2
        HEADDIM = 64
        D_INNER = EXPAND * D_MODEL
        NHEADS = D_INNER // HEADDIM
        CONV_DIM = D_INNER + 2 * D_STATE
        D_IN_PROJ = 2 * D_INNER + 2 * D_STATE + NHEADS
        BATCH, SEQLEN = (2, 256)
        EPS = 1e-05

        def _forward(x, ln_w, ln_b, W_in, conv_w, conv_b, dt_bias, A_log, D, rms_w, W_out):
            b, l, _ = x.shape
            mu = jnp.mean(x, -1, keepdims=True)
            var = jnp.mean((x - mu) ** 2, -1, keepdims=True)
            xn = (x - mu) * jax.lax.rsqrt(var + EPS) * ln_w + ln_b
            zxbcdt = xn @ W_in
            z = zxbcdt[..., :D_INNER]
            xBC = zxbcdt[..., D_INNER:D_INNER + CONV_DIM]
            dt_raw = zxbcdt[..., -NHEADS:]
            xp = jnp.pad(xBC, ((0, 0), (D_CONV - 1, 0), (0, 0)))
            xBC = sum((xp[:, k:k + l, :] * conv_w[:, k] for k in range(D_CONV))) + conv_b
            xBC = jax.nn.silu(xBC)
            xh = xBC[..., :D_INNER].reshape(b, l, NHEADS, HEADDIM)
            Bm = xBC[..., D_INNER:D_INNER + D_STATE]
            Cm = xBC[..., D_INNER + D_STATE:]
            dt = jax.nn.softplus(dt_raw + dt_bias)
            A = -jnp.exp(A_log)
            decay = jnp.exp(dt * A)

            def step(h, inp):
                dec_t, dt_t, x_t, B_t, C_t = inp
                h = h * dec_t[..., None, None] + (dt_t[..., None] * x_t)[..., None] * B_t[:, None, None, :]
                y = jnp.einsum('bhpn,bn->bhp', h, C_t)
                return (h, y)
            h0 = jnp.zeros((b, NHEADS, HEADDIM, D_STATE), x.dtype)
            seq = (decay.transpose(1, 0, 2), dt.transpose(1, 0, 2), xh.transpose(1, 0, 2, 3), Bm.transpose(1, 0, 2), Cm.transpose(1, 0, 2))
            _, ys = jax.lax.scan(step, h0, seq)
            y = ys.transpose(1, 0, 2, 3) + D[None, None, :, None] * xh
            y = y.reshape(b, l, D_INNER)
            g = y * jax.nn.silu(z)
            g = g * jax.lax.rsqrt(jnp.mean(g * g, -1, keepdims=True) + EPS) * rms_w
            return g @ W_out + x
        key = jax.random.key(seed)
        ks = jax.random.split(key, 8)
        n = lambda i, shape, s: jax.random.normal(ks[i], shape, jnp.float32) * s
        return {'x': n(0, (BATCH, SEQLEN, D_MODEL), 1.0), 'ln_w': jnp.ones((D_MODEL,), jnp.float32), 'ln_b': jnp.zeros((D_MODEL,), jnp.float32), 'W_in': n(1, (D_MODEL, D_IN_PROJ), 0.02), 'conv_w': n(2, (CONV_DIM, D_CONV), 0.2), 'conv_b': jnp.zeros((CONV_DIM,), jnp.float32), 'dt_bias': n(3, (NHEADS,), 0.5), 'A_log': jnp.log(jnp.linspace(1.0, 16.0, NHEADS, dtype=jnp.float32)), 'D': jnp.ones((NHEADS,), jnp.float32), 'rms_w': jnp.ones((D_INNER,), jnp.float32), 'W_out': n(4, (D_INNER, D_MODEL), 0.02)}
    _L0_attn_all = _L0_attn_setup()
    _L0_attn_in = {k: v for k, v in _L0_attn_all.items() if k in ('ln_w', 'ln_b', 'W_in', 'conv_w', 'conv_b', 'dt_bias', 'A_log', 'D', 'rms_w', 'W_out')}
    del _L0_attn_all

    def _L0_ffn_setup():
        import jax, jax.numpy as jnp
        import numpy as np
        DIM = 192
        NUM_EXPERTS = 4
        NUM_HEADS = 12
        HEAD_DIM = DIM // NUM_HEADS
        MLP_HID = 4 * DIM
        FC1_OUT = MLP_HID + 3 * DIM
        FC2_IN = MLP_HID + DIM
        FC2_OUT = 2 * DIM
        CAP_FACTOR = 0.5
        LN_EPS = 1e-06
        key = jax.random.key(seed)
        ks = jax.random.split(key, 4)
        B, N = (8, 256)
        return {'x': jax.random.normal(ks[0], (B, N, DIM), jnp.float32), 'w_router': jax.random.normal(ks[1], (NUM_EXPERTS, DIM), jnp.float32) * 0.02, 'gamma1': jnp.ones((DIM,), jnp.float32), 'beta1': jnp.zeros((DIM,), jnp.float32), 'w1': jax.random.normal(ks[2], (FC1_OUT, DIM), jnp.float32) * 0.02, 'b1': jnp.zeros((FC1_OUT,), jnp.float32), 'w2': jax.random.normal(ks[3], (FC2_OUT, FC2_IN), jnp.float32) * 0.02, 'b2': jnp.zeros((FC2_OUT,), jnp.float32)}
    _L0_ffn_all = _L0_ffn_setup()
    _L0_ffn_in = {k: v for k, v in _L0_ffn_all.items() if k in ('w_router', 'gamma1', 'beta1', 'w1', 'b1', 'w2', 'b2')}
    del _L0_ffn_all
    return {'x': x, 'L0_tok_qkv_w': _L0_tok_in['qkv_w'], 'L0_tok_qkv_b': _L0_tok_in['qkv_b'], 'L0_tok_proj_w': _L0_tok_in['proj_w'], 'L0_tok_proj_b': _L0_tok_in['proj_b'], 'L0_attn_ln_w': _L0_attn_in['ln_w'], 'L0_attn_ln_b': _L0_attn_in['ln_b'], 'L0_attn_W_in': _L0_attn_in['W_in'], 'L0_attn_conv_w': _L0_attn_in['conv_w'], 'L0_attn_conv_b': _L0_attn_in['conv_b'], 'L0_attn_dt_bias': _L0_attn_in['dt_bias'], 'L0_attn_A_log': _L0_attn_in['A_log'], 'L0_attn_D': _L0_attn_in['D'], 'L0_attn_rms_w': _L0_attn_in['rms_w'], 'L0_attn_W_out': _L0_attn_in['W_out'], 'L0_ffn_w_router': _L0_ffn_in['w_router'], 'L0_ffn_gamma1': _L0_ffn_in['gamma1'], 'L0_ffn_beta1': _L0_ffn_in['beta1'], 'L0_ffn_w1': _L0_ffn_in['w1'], 'L0_ffn_b1': _L0_ffn_in['b1'], 'L0_ffn_w2': _L0_ffn_in['w2'], 'L0_ffn_b2': _L0_ffn_in['b2']}

def reference(x, L0_tok_qkv_w, L0_tok_qkv_b, L0_tok_proj_w, L0_tok_proj_b, L0_attn_ln_w, L0_attn_ln_b, L0_attn_W_in, L0_attn_conv_w, L0_attn_conv_b, L0_attn_dt_bias, L0_attn_A_log, L0_attn_D, L0_attn_rms_w, L0_attn_W_out, L0_ffn_w_router, L0_ffn_gamma1, L0_ffn_beta1, L0_ffn_w1, L0_ffn_b1, L0_ffn_w2, L0_ffn_b2):
    import jax
    import jax.numpy as jnp

    def _L0_tok_ref(x, qkv_w, qkv_b, proj_w, proj_b):
        import jax, jax.numpy as jnp
        import numpy as np
        HEADS = 12
        DIM = 192
        DIM_OUT = 192
        HEAD_DIM = DIM_OUT // HEADS
        Q_STRIDE = 4
        WINDOW_SIZE = 64
        B, N, _ = x.shape
        nw = N // (Q_STRIDE * WINDOW_SIZE)
        L = N // nw
        qkv = (x @ qkv_w.T + qkv_b).reshape(B, L, nw, 3, HEADS, HEAD_DIM)
        qkv = jnp.transpose(qkv, (3, 0, 4, 2, 1, 5))
        q, k, v = (qkv[0], qkv[1], qkv[2])
        q = q.reshape(B, HEADS, nw, Q_STRIDE, L // Q_STRIDE, HEAD_DIM).max(axis=3)
        scale = HEAD_DIM ** (-0.5)
        logits = jnp.einsum('bhwqd,bhwkd->bhwqk', q, k) * scale
        attn = jax.nn.softmax(logits, axis=-1)
        o = jnp.einsum('bhwqk,bhwkd->bhwqd', attn, v)
        o = jnp.transpose(o, (0, 3, 2, 1, 4)).reshape(B, -1, DIM_OUT)
        return o @ proj_w.T + proj_b

    def _L0_attn_ref(x, ln_w, ln_b, W_in, conv_w, conv_b, dt_bias, A_log, D, rms_w, W_out):
        import jax, jax.numpy as jnp
        import numpy as np
        D_MODEL = 192
        D_STATE = 64
        D_CONV = 4
        EXPAND = 2
        HEADDIM = 64
        D_INNER = EXPAND * D_MODEL
        NHEADS = D_INNER // HEADDIM
        CONV_DIM = D_INNER + 2 * D_STATE
        D_IN_PROJ = 2 * D_INNER + 2 * D_STATE + NHEADS
        BATCH, SEQLEN = (2, 256)
        EPS = 1e-05

        def _forward(x, ln_w, ln_b, W_in, conv_w, conv_b, dt_bias, A_log, D, rms_w, W_out):
            b, l, _ = x.shape
            mu = jnp.mean(x, -1, keepdims=True)
            var = jnp.mean((x - mu) ** 2, -1, keepdims=True)
            xn = (x - mu) * jax.lax.rsqrt(var + EPS) * ln_w + ln_b
            zxbcdt = xn @ W_in
            z = zxbcdt[..., :D_INNER]
            xBC = zxbcdt[..., D_INNER:D_INNER + CONV_DIM]
            dt_raw = zxbcdt[..., -NHEADS:]
            xp = jnp.pad(xBC, ((0, 0), (D_CONV - 1, 0), (0, 0)))
            xBC = sum((xp[:, k:k + l, :] * conv_w[:, k] for k in range(D_CONV))) + conv_b
            xBC = jax.nn.silu(xBC)
            xh = xBC[..., :D_INNER].reshape(b, l, NHEADS, HEADDIM)
            Bm = xBC[..., D_INNER:D_INNER + D_STATE]
            Cm = xBC[..., D_INNER + D_STATE:]
            dt = jax.nn.softplus(dt_raw + dt_bias)
            A = -jnp.exp(A_log)
            decay = jnp.exp(dt * A)

            def step(h, inp):
                dec_t, dt_t, x_t, B_t, C_t = inp
                h = h * dec_t[..., None, None] + (dt_t[..., None] * x_t)[..., None] * B_t[:, None, None, :]
                y = jnp.einsum('bhpn,bn->bhp', h, C_t)
                return (h, y)
            h0 = jnp.zeros((b, NHEADS, HEADDIM, D_STATE), x.dtype)
            seq = (decay.transpose(1, 0, 2), dt.transpose(1, 0, 2), xh.transpose(1, 0, 2, 3), Bm.transpose(1, 0, 2), Cm.transpose(1, 0, 2))
            _, ys = jax.lax.scan(step, h0, seq)
            y = ys.transpose(1, 0, 2, 3) + D[None, None, :, None] * xh
            y = y.reshape(b, l, D_INNER)
            g = y * jax.nn.silu(z)
            g = g * jax.lax.rsqrt(jnp.mean(g * g, -1, keepdims=True) + EPS) * rms_w
            return g @ W_out + x
        return _forward(x, ln_w, ln_b, W_in, conv_w, conv_b, dt_bias, A_log, D, rms_w, W_out)

    def _L0_ffn_ref(x, w_router, gamma1, beta1, w1, b1, w2, b2):
        import jax, jax.numpy as jnp
        import numpy as np
        DIM = 192
        NUM_EXPERTS = 4
        NUM_HEADS = 12
        HEAD_DIM = DIM // NUM_HEADS
        MLP_HID = 4 * DIM
        FC1_OUT = MLP_HID + 3 * DIM
        FC2_IN = MLP_HID + DIM
        FC2_OUT = 2 * DIM
        CAP_FACTOR = 0.5
        LN_EPS = 1e-06
        B, N, C = x.shape
        E = NUM_EXPERTS
        cap = int(CAP_FACTOR * N)
        m = np.array([C // 2 ** (E - 1 - e) for e in range(E)])
        in_mask = (np.arange(C)[None, :] < m[:, None]).astype(np.float32)
        in_mask = jnp.asarray(in_mask)
        out_mask = jnp.concatenate([in_mask, in_mask], axis=-1)
        logits = jnp.einsum('bnc,ec->bne', x, w_router)
        probs = jax.nn.softmax(logits, axis=-1)
        gate, idx = jax.lax.top_k(jnp.swapaxes(probs, 1, 2), cap)
        dispatch = jax.nn.one_hot(idx, N, dtype=x.dtype)
        combine = dispatch * gate[..., None]
        mu = jnp.mean(x, -1, keepdims=True)
        var = jnp.var(x, -1, keepdims=True)
        y = (x - mu) * jax.lax.rsqrt(var + LN_EPS) * gamma1 + beta1
        xg = jnp.einsum('becn,bnd->becd', dispatch, y)
        xg = xg * in_mask[None, :, None, :]
        h = jnp.einsum('becd,fd->becf', xg, w1) + b1
        h = jnp.einsum('becn,becf->bnf', dispatch, h)
        x_mlp, x_qkv = (h[..., :MLP_HID], h[..., MLP_HID:])
        qkv = x_qkv.reshape(B, N, 3, NUM_HEADS, HEAD_DIM).transpose(2, 0, 3, 1, 4)
        q, k, v = (qkv[0], qkv[1], qkv[2])
        scale = HEAD_DIM ** (-0.5)
        attn = jax.nn.softmax(jnp.einsum('bhqd,bhkd->bhqk', q, k) * scale, axis=-1)
        x_attn = jnp.einsum('bhqk,bhkd->bhqd', attn, v)
        x_attn = x_attn.transpose(0, 2, 1, 3).reshape(B, N, C)
        x_mlp = jax.nn.gelu(x_mlp, approximate=False)
        y2 = jnp.concatenate([x_mlp, x_attn], axis=-1)
        yg = jnp.einsum('becn,bnf->becf', dispatch, y2)
        o = jnp.einsum('becf,of->beco', yg, w2) + b2
        o = o * out_mask[None, :, None, :]
        z = jnp.einsum('becn,beco->bno', combine, o)
        x_mlp2, x_attn2 = (z[..., :C], z[..., C:])
        return x + x_mlp2 + x_attn2
    h = _L0_tok_ref(x, L0_tok_qkv_w, L0_tok_qkv_b, L0_tok_proj_w, L0_tok_proj_b)
    h = h + _L0_attn_ref(_layernorm(h, axis=-1), L0_attn_ln_w, L0_attn_ln_b, L0_attn_W_in, L0_attn_conv_w, L0_attn_conv_b, L0_attn_dt_bias, L0_attn_A_log, L0_attn_D, L0_attn_rms_w, L0_attn_W_out)
    h = h + _L0_ffn_ref(_layernorm(h, axis=-1), L0_ffn_w_router, L0_ffn_gamma1, L0_ffn_beta1, L0_ffn_w1, L0_ffn_b1, L0_ffn_w2, L0_ffn_b2)
    return h

_drawn_inputs = setup_inputs


def setup_inputs(seed=0):
    import zlib

    import numpy as np

    out = dict(_drawn_inputs(seed))
    spreads = {'L0_attn_ln_w': (1.0, 0.2),
     'L0_attn_ln_b': (0.0, 0.1),
     'L0_attn_conv_b': (0.0, 0.1),
     'L0_attn_D': (1.0, 0.6),
     'L0_attn_rms_w': (1.0, 0.2),
     'L0_ffn_gamma1': (1.0, 0.6),
     'L0_ffn_beta1': (0.0, 0.8),
     'L0_ffn_b1': (0.0, 0.392),
     'L0_ffn_b2': (0.0, 0.396)}
    factors = {'L0_attn_dt_bias': 8.0, 'L0_attn_A_log': 8.0}
    for name, (base, spread) in spreads.items():
        noise = np.random.default_rng([zlib.crc32(name.encode()), seed]).standard_normal(out[name].shape)
        drawn = base * np.exp(spread * noise) if base else spread * noise
        out[name] = jnp.asarray(drawn.astype(out[name].dtype))
    for name, factor in factors.items():
        out[name] = (out[name] * factor).astype(out[name].dtype)
    return out
```

```python
from contextlib import ExitStack

import numpy as np

import concourse.bass as bass
from concourse import mybir
from concourse.alu_op_type import AluOpType as ALU

F32 = mybir.dt.float32
F32R = mybir.dt.float32r
BF16 = mybir.dt.bfloat16
ACT = mybir.ActivationFunctionType
AX = mybir.AxisListType

B = 8
N = 1024
L = 256
C = 192
HC = C // 2
H = 12
D = C // H
HH = H // 2
PAIRS = H // 2
SR = 6 * D
STRIDE = 4
W = 4
QW = 64
KW = 256
E = 4
CAP = L // 2
MLP = 4 * C
F1 = MLP + 3 * C
MJ = MLP // 128
G3 = H // 4
INNER = 2 * C
STATE = 64
SH = INNER // 64
XC = INNER // 128
ZXD = 2 * INNER + 2 * STATE + SH
U = 12
TAPS = 4
T2 = 2
SCALE = float(D) ** -0.5


def audio_tower(nc, x, wqkv_d, wo_d, bo_d, win_d, lnw_d, lnb_d, cw_d, cb_d, dtb_d, alog_d, dd_d, rms_d,
                wout_d, wr_d, gam_d, bet_d, w1_d, w2_d, b2_d, hm_d, later_d, upto_d, eye_d, nest_d,
                row_d, out):
    with ExitStack() as ctx:
        def sb(name, shape, dt=F32):
            return ctx.enter_context(nc.sbuf_tensor(name, shape, dt))

        def sb_phase(*tensors):
            with ExitStack() as phase:
                return [phase.enter_context(nc.sbuf_tensor(*t)) for t in tensors]

        def sem(name):
            return ctx.enter_context(nc.semaphore(name))

        ps = ctx.enter_context(nc.psum_tensor("ps", [128, 8, 512], F32))
        GEN, TR, SC, OB = 0, 2, 4, 6
        psO = ps[:, OB:OB + 2, :].rearrange("p a n -> p (a n)")[:, 0:G3 * L]
        psY = psO
        psDt = ps[:, 7, 256:256 + T2 * SH]
        psSuf = ps[:, 7, 272:272 + SH]
        psLg = ps[:, 7, 288:288 + T2 * E]

        areaX = sb("areaX", [128, 2, 2048])
        xT = [areaX[:, p, :].rearrange("p (a n) -> p a n", a=2) for p in range(2)]

        prob = sb("prob", [128, 3, 512])
        probT = sb("probT", [128, 3, 512])
        nmax = sb("nmax", [128, 4, 2])
        qp = sb("qp", [HC, 2, L])
        qhl = sb("qhl", [HC, 2, 2, L], F32R)
        otA = sb("otA", [128, G3 * L])
        rsum = sb("rsum", [128, G3 * L // 32])
        oT = sb("oT", [128, G3, L])
        h_all = sb("h_all", [128, B * T2, C])
        st6 = sb("st6", [128, T2, 6])
        mv = sb("mv", [128, T2, 2])
        mean_all = sb("mean_all", [128, B * T2])
        ve = sb("ve", [128, T2])
        vu = sb("vu", [128, T2])
        ve2 = sb("ve2", [128, T2])
        r1_all = sb("r1_all", [128, B * T2])
        rr_all = sb("rr_all", [128, B * T2])
        mhalf = sb("mhalf", [128, T2])
        eps5 = sb("eps5", [128, T2])
        eps6 = sb("eps6", [128, T2])

        wqkv = sb("wqkv", [HC + 1, 2, 3 * C])
        wo = sb("wo", [128, G3, C])
        bo = sb("bo", [128, C])
        hm = sb("hm", [HC, 2])
        eye = sb("eye", [128, 128])
        later = sb("later", [128, 128])
        upto = sb("upto", [128, 128])
        ones = sb("ones", [128, 128])
        win = sb("win", [HC, 2, ZXD])
        lnw = sb("lnw", [HC, 2])
        lnb = sb("lnb", [HC, 2])
        cw = sb("cw", [128, TAPS, TAPS])
        cb = sb("cb", [128, TAPS])
        dtb = sb("dtb", [128, SH])
        aneg = sb("aneg", [128, SH])
        dd = sb("dd", [128, XC])
        rms = sb("rms", [128, XC])
        wout = sb("wout", [128, XC, C])
        wr = sb("wr", [HC, 2, E])
        gam = sb("gam", [HC, 2])
        bet = sb("bet", [HC, 2])
        w1 = sb("w1", [HC + 1, 2, F1])
        w2 = sb("w2", [128, MJ + G3, C])
        w2x = areaX[:, 1, 0:(MJ + G3) * C].rearrange("p (j c) -> p j c", c=C)
        b2 = sb("b2", [128, C])
        b2x = sb("b2x", [128, C])
        nestf = sb("nestf", [32, 2 * (HC + 1) + C])
        nest = sb("nest", [32, 2 * (HC + 1)], BF16)
        rowm = sb("rowm", [32, B])

        small = sb("small", [128, 12, T2 * SH])
        dt2 = sb("dt2", [128, 2, T2, SH])
        a2 = sb("a2", [128, 2, T2, SH])
        esuf = sb("esuf", [128, SH])
        ms = sb("ms", [128, T2])
        rt = sb("rt", [128, T2])
        r1 = sb("r1", [128, T2])
        r2 = sb("r2", [128, T2])
        rr = sb("rr", [128, T2])
        s2 = sb("s2", [128, T2])
        lg = sb("lg", [128, T2, B, E])
        lsm = sb("lsm", [128, 4, T2 * B])
        pe_ = sb("pe_", [128, T2 * B, E])
        pr = sb("pr", [32, L])
        pick = sb("pick", [32, 2, L])
        top8 = sb("top8", [32, 8])
        sel = sb("sel", [32, L])
        gsel = sb("gsel", [32, L])
        selb = sb("selb", [32, L], BF16)
        gselb = sb("gselb", [32, 2, L])
        yhat = sb("yhat", [HC + 1, 2, L])
        y2T = [areaX[:, p, 0:MJ * L].rearrange("p (j n) -> p j n", j=MJ) for p in range(2)]
        res = sb("res", [128, T2, C])
        res2 = sb("res2", [128, T2, C])

        kst, qst0, qst1, qm, qmhl, khl, areaV1 = sb_phase(
            ("kst", [SR, PAIRS, N], F32R), ("qst0", [SR, PAIRS, 2 * L], F32R), ("qst1", [SR, PAIRS, 2 * L], F32R),
            ("qm", [HC, 2, W, 2, QW], F32), ("qmhl", [HC, 2, 2, 2 * L], F32R), ("khl", [HC, 2, 2, N], F32R), ("areaV1", [128, 2, 3072], F32))
        qst = [qst0, qst1]
        va = [areaV1[:, p, :].rearrange("p (t h e) -> p t h e", t=N // 128, e=32) for p in range(2)]
        u3_all = sb("u3_all", [128, B * T2, C])
        yT_all = sb("yT_all", [HC + 1, 2, B * L])
        areaQ, areaK, areaV, uu, xnT, bcT, h2, yhT = sb_phase(
            ("areaQ", [128, 6144], F32), ("areaK", [128, 4096], F32), ("areaV", [128, 6144], F32),
            ("uu", [128, T2, C], F32), ("xnT", [HC, 2, L], F32), ("bcT", [STATE, 2, L], F32),
            ("h2", [128, T2, C], F32), ("yhT", [HC, 2, L], F32))
        qst30, qst31, kst30, kst31, khl3, areaV3 = sb_phase(
            ("qst30", [SR, PAIRS, 2, L], F32R), ("qst31", [SR, PAIRS, 2, L], F32R),
            ("kst30", [SR, PAIRS, L], F32R), ("kst31", [SR, PAIRS, L], F32R), ("khl3", [HC, 2, 2, L], F32R),
            ("areaV3", [128, 2, T2 * H * 32], F32))
        qst3, kst3 = [qst30, qst31], [kst30, kst31]
        va3 = [areaV3[:, p, :].rearrange("p (t h e) -> p t h e", t=T2, e=32) for p in range(2)]

        def cut(area, sizes):
            got, at = [], 0
            for n in sizes:
                got.append(area[:, at:at + n])
                at += n
            return got

        qflat, kflat, vflat = areaQ[:, :], areaK[:, :], areaV[:, :]
        m_, a1_, ex0, ex1 = cut(qflat, [3 * 768, 2 * 768, 768, 768])
        mix = m_.rearrange("p (a h t) -> p a h t", a=3, h=SH)
        a1 = a1_.rearrange("p (a h t) -> p a h t", a=2, h=SH)
        dec = [ex0.rearrange("p (h t) -> p h t", h=SH), ex1.rearrange("p (h t) -> p h t", h=SH)]
        xdt_, y_, g_, gsq_, gm_ = cut(kflat, [3 * INNER, XC * L, XC * L, XC * L, 3 * 128])
        xdt = xdt_.rearrange("p (a h q) -> p a h q", a=3, h=SH)
        y2 = y_.rearrange("p (c t) -> p c t", c=XC)
        gt = g_.rearrange("p (c t) -> p c t", c=XC)
        gsq = gsq_.rearrange("p (c t) -> p c t", c=XC)
        gmask = gm_.rearrange("p (a t) -> p a t", a=3)
        xc_, sz_, xpad_, acc_, xh_ = cut(vflat, [2 * XC * L, 2 * XC * L, TAPS * (L + 4), TAPS * L, 2 * T2 * C])
        xh = xh_.rearrange("p (b t c) -> p b t c", b=2, t=T2)
        xc = xc_.rearrange("p (b c t) -> p b c t", b=2, c=XC)
        sz = sz_.rearrange("p (b c t) -> p b c t", b=2, c=XC)
        xpad = xpad_.rearrange("p (c t) -> p c t", c=TAPS)
        acc = acc_.rearrange("p (c t) -> p c t", c=TAPS)
        w_first, w_rest, w2x_loaded = sem("w_first"), sem("w_rest"), sem("w2x_loaded")
        x_loaded = [sem("x_loaded0"), sem("x_loaded1")]
        x_used = sem("x_used")
        consts = sem("consts")
        fills = sem("fills")
        vones = sem("vones")
        s_done, max_done, exp_done = sem("s_done"), sem("max_done"), sem("exp_done")
        t_done, pt_ready, pv_done = sem("t_done"), sem("pt_ready"), sem("pv_done")
        o_read, ot_sum, ot_norm, ot_ready = sem("o_read"), sem("ot_sum"), sem("ot_norm"), sem("ot_ready")
        q_done, k_done, v_done, h_done = sem("q_done"), sem("k_done"), sem("v_done"), sem("h_done")
        q_pooled, k_ready, v_ready, h_ready = sem("q_pooled"), sem("k_ready"), sem("v_ready"), sem("h_ready")
        q_split, q_low, k_split = sem("q_split"), sem("q_low"), sem("k_split")
        q_stacked = [sem("q_stacked0"), sem("q_stacked1")]
        k_stacked = [sem("k_stacked0"), sem("k_stacked1")]
        bn_done, mv_done, ve_done, r1_done = sem("bn_done"), sem("mv_done"), sem("ve_done"), sem("r1_done")
        pow_step = sem("pow_step")
        stat_done = sem("stat_done")
        alog_exp = sem("alog_exp")
        setup, w2_ready = sem("setup"), sem("w2_ready")
        xh_ready, u_done, hu_done = sem("xh_ready"), sem("u_done"), sem("hu_done")
        xt_done, xn_ready = sem("xt_done"), sem("xn_ready")
        dt_done, zx_done, zx_read = sem("dt_done"), sem("zx_done"), sem("zx_read")
        dt_step, dt_exp, dt_log, dt_ready = sem("dt_step"), sem("dt_exp"), sem("dt_log"), sem("dt_ready")
        xp_ready, conv_step, conv_done = sem("xp_ready"), sem("conv_step"), sem("conv_done")
        z_ready, xc_ready = sem("z_ready"), sem("xc_ready")
        a1_ready, tok_done, g_done, suf_done = sem("a1_ready"), sem("tok_done"), sem("g_done"), sem("suf_done")
        seg_done, dec_ready, suf_ready = sem("seg_done"), sem("dec_ready"), sem("suf_ready")
        xdt_ready, gm_ready, mix_ready = sem("xdt_ready"), sem("gm_ready"), sem("mix_ready")
        y_done, y_ready, gt_ready, gsq_ready = sem("y_done"), sem("y_ready"), sem("gt_ready"), sem("gsq_ready")
        o2_done, ms_done, rt_done, h2_ready = sem("o2_done"), sem("ms_done"), sem("rt_done"), sem("h2_ready")
        bn2_done, mv2_done, ve3_done, r3_done = sem("bn2_done"), sem("mv2_done"), sem("ve3_done"), sem("r3_done")
        h2_used = sem("h2_used")
        pow2_step, yh_ready, u3_ready = sem("pow2_step"), sem("yh_ready"), sem("u3_ready")
        yt_done, yhT_ready, yT_ready = sem("yt_done"), sem("yhT_ready"), sem("yT_ready")
        lg_done, lg_ready = sem("lg_done"), sem("lg_ready")
        ch_step, ch_exp, pr_done = sem("ch_step"), sem("ch_exp"), sem("pr_done")
        gates_ready = sem("gates_ready")
        selb_ready, m_done, yhat_ready = sem("selb_ready"), sem("m_done"), sem("yhat_ready")
        q3_done, k3_done, v3_done, m3_done = sem("q3_done"), sem("k3_done"), sem("v3_done"), sem("m3_done")
        q3_ready, k3_ready, v3_ready, m3_read = sem("q3_ready"), sem("k3_ready"), sem("v3_ready"), sem("m3_read")
        gelu_done, q3_split, k3_split = sem("gelu_done"), sem("q3_split"), sem("k3_split")
        zeros3 = sem("zeros3")
        qk3_stacked = [sem("qk3_stacked0"), sem("qk3_stacked1")]
        f_done, f_read, res_step, res_ready = sem("f_done"), sem("f_read"), sem("res_step"), sem("res_ready")
        stored = [sem("stored0"), sem("stored1")]

        block = ctx.enter_context(nc.Block())

        def over_batches(eng, stage):
            stage(0, 0)
            with eng.Fori(0, B // 2 - 1) as i:
                stage(i * 2 + 1, 1)
                stage(i * 2 + 2, 0)
            stage(B - 1, 1)

        def tile(b, t):
            return bass.ds(b * T2 + t, 1)

        @block.sync
        def _(sp):
            sp.dma_start(xT[0][0:HC], x[0]).then_inc(x_loaded[0], 16)
            sp.dma_start(wqkv[:], wqkv_d).then_inc(w_first, 16)
            sp.dma_start(hm[:], hm_d).then_inc(w_first, 16)
            sp.dma_start(eye[:], eye_d).then_inc(w_first, 16)
            sp.dma_start(wo[:], wo_d).then_inc(w_first, 16)
            sp.dma_start(bo[:], bo_d.rearrange("(a n) -> a n", a=1).broadcast_to([128, C])).then_inc(w_first, 16)
            sp.dma_start(xT[1][0:HC], x[1]).then_inc(x_loaded[1], 16)
            for dst, src in ((win, win_d), (lnw, lnw_d), (lnb, lnb_d), (cw, cw_d), (cb, cb_d), (dd, dd_d),
                             (rms, rms_d), (wout, wout_d), (wr, wr_d), (gam, gam_d), (bet, bet_d),
                             (w1, w1_d), (w2, w2_d[0]), (nestf, nest_d), (rowm, row_d), (later, later_d),
                             (upto, upto_d)):
                sp.dma_start(dst[:], src).then_inc(w_rest, 16)
            for dst, src in ((dtb, dtb_d), (aneg, alog_d), (b2, b2_d[0]), (b2x, b2_d[1])):
                n = dst.shape[1]
                sp.dma_start(dst[:], src.rearrange("(a n) -> a n", a=1).broadcast_to([128, n])).then_inc(w_rest, 16)

            def stack_q(c, p):
                sp.wait_ge(q_split, c * 3 + 3)
                for r, part in enumerate((0, 1, 0)):
                    for pair in range(PAIRS // 2):
                        sp.dma_start(qst[p][32 * r:32 * r + 32, pair:PAIRS:PAIRS // 2, :].bitcast(F32),
                                     qmhl[32 * pair:32 * pair + 32, part].bitcast(F32)).then_inc(q_stacked[p], 16)

            def stack_k(c, tb):
                if tb == 0 or isinstance(c, int) and c == 0:
                    sp.wait_ge(k_split, c * 4 + 2 * tb + 2)
                else:
                    sp.wait_ge(s_done, c * U)
                for r, part in enumerate((0, 0, 1)):
                    for pair in range(PAIRS // 2):
                        sp.dma_start(kst[32 * r:32 * r + 32, pair:PAIRS:PAIRS // 2, tb * 512:(tb + 1) * 512].bitcast(F32),
                                     khl[32 * pair:32 * pair + 32, part, :, tb * 512:(tb + 1) * 512].bitcast(F32)
                                     ).then_inc(k_stacked[tb], 16)

            def load_x(c, p):
                sp.wait_ge(x_used, c - 1)
                sp.dma_start(xT[p][0:HC], x[bass.ds(c, 1)].rearrange("b p a n -> p (b a) n")).then_inc(x_loaded[p], 16)

            def stage1(b, p):
                stack_q(b + 1, 1 - p)
                stack_k(b + 1, 0)
                if not isinstance(b, int) or b + 3 < B:
                    load_x(b + 3, 1 - p)
                stack_k(b + 1, 1)

            sp.wait_ge(consts, 7)
            stack_q(0, 0)
            stack_k(0, 0)
            load_x(2, 0)
            stack_k(0, 1)
            stage1(0, 0)
            with sp.Fori(0, B // 2 - 2) as i:
                stage1(i * 2 + 1, 1)
                stage1(i * 2 + 2, 0)
            stage1(B - 3, 1)
            stage1(B - 2, 0)
            sp.wait_ge(x_used, B)
            sp.dma_start(w2x, w2_d[1]).then_inc(w2x_loaded, 16)

            def store(b, p):
                sp.wait_ge(res_ready, b + 1)
                sp.dma_start(out[bass.ds(b, 1)].rearrange("b (t p) c -> p (b t) c", p=128), res2[:]).then_inc(stored[p], 16)

            def stack3(c, p):
                sp.wait_ge(k3_split, c + 1)
                for r, part in enumerate((0, 1, 0)):
                    for h in range(HH):
                        pair, e = divmod(h, 2)
                        sp.dma_start(qst3[p][32 * r + D * e:32 * r + D * (e + 1), pair:PAIRS:PAIRS // 2, e, :].bitcast(F32),
                                     qhl[D * h:D * (h + 1), part].bitcast(F32)).then_inc(qk3_stacked[p], 16)
                for r, part in enumerate((0, 0, 1)):
                    for pair in range(PAIRS // 2):
                        sp.dma_start(kst3[p][32 * r:32 * r + 32, pair:PAIRS:PAIRS // 2, :].bitcast(F32),
                                     khl3[32 * pair:32 * pair + 32, part].bitcast(F32)).then_inc(qk3_stacked[p], 16)

            def stage3(b, p):
                stack3(b + 1, 1 - p)
                if not (isinstance(b, int) and b == 0):
                    store(b - 1, 1 - p)

            sp.wait_ge(zeros3, 2)
            stack3(0, 0)
            stage3(0, 0)
            with sp.Fori(0, B // 2 - 1) as i:
                stage3(i * 2 + 1, 1)
                stage3(i * 2 + 2, 0)
            store(B - 2, 0)
            store(B - 1, 1)
            for p in range(2):
                sp.wait_ge(stored[p], 16 * (B // 2))
        W_FIRST, W_REST = 16 * 5, 16 * 21
        K_BANKS = (1, 1, 0, 1)
        QD, KD, QD3 = 3 * PAIRS // 2, 3 * PAIRS // 2, 3 * HH

        @block.tensor
        def _(pe):
            def unit_scores1(slot, c_par, u):
                w, r = divmod(u, 3)
                for i in range(2):
                    last = nc.tensor.matmul(
                        ps[:, SC + slot, i * 256:(i + 1) * 256],
                        qst[c_par][:, 2 * r + i, w * 2 * QW:(w + 1) * 2 * QW],
                        kst[:, 2 * r + i, w * KW:(w + 1) * KW], start=True, stop=True)
                last.then_inc(s_done, 1)

            def unit_scores3(slot, c_par, u):
                pair, e = divmod(u, 2)
                for i in range(2):
                    last = nc.tensor.matmul(
                        ps[:, SC + slot, i * 256:(i + 1) * 256],
                        qst3[c_par][:, pair, e, i * 128:(i + 1) * 128],
                        kst3[c_par][:, pair, :], start=True, stop=True)
                last.then_inc(s_done, 1)

            def unit_turn(u):
                for kc in range(2):
                    for i in range(2):
                        last = nc.tensor.transpose(
                            ps[:, TR + u % 2, kc * 256 + i * 128:kc * 256 + (i + 1) * 128],
                            prob[:, u % 3, i * 256 + kc * 128:i * 256 + (kc + 1) * 128], eye[:])
                last.then_inc(t_done, 1)

            def unit_pv1(p, u):
                w, r = divmod(u, 3)
                for kc in range(2):
                    for j in range(4):
                        last = nc.tensor.matmul(
                            psO[32 * j:32 * j + 32, r * L + w * QW:r * L + (w + 1) * QW],
                            va[p][:, 2 * w + kc, 4 * r + j, :],
                            probT[:, u % 3, kc * 256 + j * QW:kc * 256 + (j + 1) * QW],
                            start=(kc == 0), stop=(kc == 1), tile_position=(0, 32 * j))
                last.then_inc(pv_done, 1)

            def unit_pv3(p, u):
                g, j = divmod(u, 4)
                for kc in range(2):
                    last = nc.tensor.matmul(
                        psO[32 * j:32 * j + 32, g * L:(g + 1) * L], va3[p][:, kc, u, :],
                        probT[:, u % 3, kc * 256:(kc + 1) * 256],
                        start=(kc == 0), stop=(kc == 1), tile_position=(0, 32 * j))
                last.then_inc(pv_done, 1)

            def q_piece(p, k, bank):
                half, tb = divmod(k, 2)
                for a in range(2):
                    last = nc.tensor.matmul(ps[0:HC, bank, :], wqkv[0:HC + a, a, half * HC:(half + 1) * HC],
                                            xT[p][0:HC + a, a, tb * 512:(tb + 1) * 512],
                                            start=(a == 0), stop=(a == 1))
                last.then_inc(q_done, 1)

            def k_piece(p, k, bank):
                tb, half = divmod(k, 2)
                for a in range(2):
                    last = nc.tensor.matmul(ps[0:HC, bank, :], wqkv[0:HC + a, a, C + half * HC:C + (half + 1) * HC],
                                            xT[p][0:HC + a, a, tb * 512:(tb + 1) * 512],
                                            start=(a == 0), stop=(a == 1))
                last.then_inc(k_done, 1)

            def v_piece(p, k, bank):
                for i in range(2):
                    t = 2 * k + i
                    for a in range(2):
                        last = nc.tensor.matmul(ps[:, bank, i * C:(i + 1) * C],
                                                xT[p][0:HC + a, a, t * 128:(t + 1) * 128],
                                                wqkv[0:HC + a, a, 2 * C:3 * C],
                                                start=(a == 0), stop=(a == 1))
                last.then_inc(v_done, 1)
                return last

            def h_piece(t, bank):
                for g in range(G3):
                    last = nc.tensor.matmul(ps[:, bank, 0:C], oT[:, g, t * 128:(t + 1) * 128], wo[:, g, :],
                                            start=(g == 0), stop=(g == G3 - 1))
                last.then_inc(h_done, 1)

            def project(c, p, k, first, h_too):
                if k == 0:
                    pe.wait_ge(x_loaded[p], (c // 2 + 1) * 16 if isinstance(c, int) else (c - p) * 8 + 16)
                if k < 4:
                    if k < 2:
                        if not first:
                            pe.wait_ge(v_ready, c * 4 - 1 + k)
                    else:
                        pe.wait_ge(q_pooled, c * 4 + k - 1)
                    q_piece(p, k, k % 2)
                elif k == 4:
                    pe.wait_ge(q_pooled, c * 4 + 4)
                    k_piece(p, 0, 1)
                elif k == 5:
                    pe.wait_ge(k_split, c * 4 + 1)
                    k_piece(p, 1, 1)
                elif k == 6:
                    if h_too:
                        pe.wait_ge(h_ready, (c - 2) * 2 + 2)
                    k_piece(p, 2, 0)
                elif k == 7:
                    pe.wait_ge(k_split, c * 4 + 2)
                    k_piece(p, 3, 1)
                elif k == 8:
                    pe.wait_ge(k_split, c * 4 + 3)
                    v_piece(p, 0, 0)
                elif k == 9:
                    pe.wait_ge(k_split, c * 4 + 4)
                    v_piece(p, 1, 1)
                else:
                    pe.wait_ge(v_ready, c * 4 + k - 9)
                    last = v_piece(p, k - 8, k % 2)
                    if k == 11:
                        pe.wait_ge(v_done, c * 4 + 4)
                        pe.sem_inc(x_used, 1)

            def output1(b, t):
                if t == 0:
                    pe.wait_ge(q_pooled, (b + 2) * 4 + 3) if b_has_next(b) else None
                    pe.wait_ge(ot_ready, b + 1)
                else:
                    pe.wait_ge(h_ready, b * 2 + 1)
                h_piece(t, 0)

            def b_has_next(b):
                return not isinstance(b, int) or b + 2 < B

            def wait_q(c, p):
                pe.wait_ge(q_stacked[p], (c // 2 + 1) * 16 * QD if isinstance(c, int) else (c - p) * 8 * QD + 16 * QD)

            def stage1(b, p):
                last = isinstance(b, int) and b == B - 1
                first = isinstance(b, int) and b == 0
                for u in range(U):
                    n1 = b * U + u + 1
                    if u < U - 1:
                        if not (first and u == 0):
                            pe.wait_ge(exp_done, n1 - 1)
                        if u + 1 == U // 2:
                            pe.wait_ge(k_stacked[1], (b + 1) * 16 * KD)
                        unit_scores1((u + 1) % 2, p, u + 1)
                    elif not last:
                        pe.wait_ge(exp_done, n1 - 1)
                        wait_q(b + 1, 1 - p)
                        pe.wait_ge(k_stacked[0], (b + 2) * 16 * KD)
                        unit_scores1(0, 1 - p, 0)
                    if not last:
                        project(b + 1, 1 - p, u, False, not first)
                    pe.wait_ge(exp_done, b * U + u + 1)
                    if not (first and u < 2):
                        pe.wait_ge(pt_ready, b * U + u - 1)
                    unit_turn(u)
                    if u == 0:
                        if not first:
                            pe.wait_ge(pt_ready, b * U)
                            unit_pv1(1 - p, U - 1)
                    else:
                        if u == 1:
                            pe.wait_ge(v_ready, b * 4 + 4)
                            if not first:
                                pe.wait_ge(o_read, b)
                        pe.wait_ge(pt_ready, b * U + u)
                        unit_pv1(p, u - 1)
                    if u in (3, 4) and not first:
                        output1(b - 1, u - 3)

            pe.wait_ge(w_first, W_FIRST)
            pe.wait_ge(consts, 3)
            for k in range(U):
                project(0, 0, k, True, False)
            wait_q(0, 0)
            pe.wait_ge(k_stacked[0], 16 * KD)
            unit_scores1(0, 0, 0)
            over_batches(pe, stage1)
            pe.wait_ge(pt_ready, B * U)
            unit_pv1(1, U - 1)
            output1(B - 1, 0)
            output1(B - 1, 1)

            B2, B3 = TR, TR + 1

            def turn_x(b, p):
                pe.wait_ge(xh_ready, b + 1)
                if not (isinstance(b, int) and b < 3):
                    pe.wait_ge(yhT_ready, b - 2)
                for half in range(2):
                    for t in range(T2):
                        last = nc.tensor.transpose(ps[0:HC, B2, half * L + t * 128:half * L + (t + 1) * 128],
                                                   xh[:, p, t, half * HC:(half + 1) * HC], eye[:])
                last.then_inc(xt_done, 1)

            def project_zx(b):
                pe.wait_ge(xn_ready, b * 2 + 2)
                if not (isinstance(b, int) and b == 0):
                    pe.wait_ge(suf_ready, b)
                for t in range(T2):
                    for half in range(2):
                        last = nc.tensor.matmul(psDt[:, t * SH:(t + 1) * SH], xnT[:, half, t * 128:(t + 1) * 128],
                                                win[:, half, ZXD - SH:ZXD], start=(half == 0), stop=(half == 1))
                last.then_inc(dt_done, 1)
                for k in range(4):
                    if not (isinstance(b, int) and b == 0 and k < 2):
                        pe.wait_ge(zx_read, b * 4 + k - 1)
                    for i in range(2 if k < 3 else 1):
                        j = 2 * k + i
                        for half in range(2):
                            last = nc.tensor.matmul(ps[:, k % 2, i * L:(i + 1) * L],
                                                    win[:, half, j * 128:(j + 1) * 128], xnT[:, half, :],
                                                    start=(half == 0), stop=(half == 1))
                    last.then_inc(zx_done, 1)

            def turn_tok(b, p, t):
                for c in range(XC):
                    last = nc.tensor.transpose(ps[:, B3, c * 128:(c + 1) * 128],
                                               xc[:, p, c, t * 128:(t + 1) * 128], eye[:])
                last.then_inc(tok_done, 1)

            def decay(lhs, tile_):
                for i in range(2):
                    last = nc.tensor.matmul(ps[:, SC + i, 0:384], lhs,
                                            a1[:, tile_, 3 * i:3 * i + 3, :].rearrange("p h t -> p (h t)"),
                                            start=True, stop=True)
                last.then_inc(seg_done, 1)

            def mid(b, p):
                first = isinstance(b, int) and b == 0
                pe.wait_ge(xc_ready, b + 1)
                if not (isinstance(b, int) and b < 2):
                    pe.wait_ge(h2_ready, b - 1)
                turn_tok(b, p, 0)
                pe.wait_ge(a1_ready, b * 2 + 2)
                if not first:
                    pe.wait_ge(dec_ready, b * 3)
                decay(later[:], 0)
                if not first:
                    pe.wait_ge(y_ready, b)
                nc.tensor.matmul(psSuf, later[:], a2[:, p, 0, :], start=True, stop=True).then_inc(suf_done, 1)
                pe.wait_ge(xdt_ready, b * 3 + 1)
                turn_tok(b, p, 1)
                pe.wait_ge(dec_ready, b * 3 + 1)
                decay(later[:], 1)
                pe.wait_ge(xdt_ready, b * 3 + 3)
                nc.tensor.matmul(ps[:, B3, 0:256], bcT[:, 0, 0:128], bcT[:, 1, :], start=True, stop=True)
                nc.tensor.matmul(ps[:, B3, 256:384], bcT[:, 0, 128:256], bcT[:, 1, 128:256],
                                 start=True, stop=True).then_inc(g_done, 1)
                pe.wait_ge(dec_ready, b * 3 + 2)
                decay(ones[:], 1)

            def mix_y(b):
                pe.wait_ge(mix_ready, b * 3 + 3)
                if not (isinstance(b, int) and b == 0):
                    pe.wait_ge(y_ready, b)
                if not (isinstance(b, int) and b == B - 1):
                    pe.wait_ge(dt_step, b * 9 + 10)
                for hp in range(XC):
                    for i in range(2):
                        h = 2 * hp + i
                        o = psY[64 * i:64 * i + 64, hp * L:(hp + 1) * L]
                        nc.tensor.matmul(o[:, 0:128], xdt[:, 0, h, :], mix[:, 0, h, :], start=True, stop=True,
                                         tile_position=(0, 64 * i))
                        nc.tensor.matmul(o[:, 128:256], xdt[:, 1, h, :], mix[:, 2, h, :], start=True, stop=False,
                                         tile_position=(0, 64 * i))
                        last = nc.tensor.matmul(o[:, 128:256], xdt[:, 2, h, :], mix[:, 1, h, :], start=False,
                                                stop=True, tile_position=(0, 64 * i))
                last.then_inc(y_done, 1)

            def output2(b):
                pe.wait_ge(gsq_ready, b + 1)
                pe.wait_ge(gm_ready, B if isinstance(b, int) and b == B - 1 else b + 2)
                for t in range(T2):
                    for c in range(XC):
                        nc.tensor.matmul(ps[:, B3, t * C:(t + 1) * C], gt[:, c, t * 128:(t + 1) * 128],
                                         wout[:, c, :], start=(c == 0), stop=(c == XC - 1))
                    for c in range(XC):
                        last = nc.tensor.matmul(ps[:, B3, 2 * C + t:2 * C + t + 1], gsq[:, c, t * 128:(t + 1) * 128],
                                                ones[:, 0:1], start=(c == 0), stop=(c == XC - 1))
                last.then_inc(o2_done, 1)

            def turn_y(b):
                pe.wait_ge(yh_ready, b + 1)
                if not (isinstance(b, int) and b >= B - 2):
                    pe.wait_ge(xn_ready, (b + 2) * 2 + 2)
                for half in range(2):
                    for t in range(T2):
                        last = nc.tensor.transpose(ps[0:HC, B2, half * L + t * 128:half * L + (t + 1) * 128],
                                                   uu[:, t, half * HC:(half + 1) * HC], eye[:])
                last.then_inc(yt_done, 1)

            def route(b):
                pe.wait_ge(yhT_ready, b + 1)
                for t in range(T2):
                    for half in range(2):
                        last = nc.tensor.matmul(psLg[:, t * E:(t + 1) * E], yhT[:, half, t * 128:(t + 1) * 128],
                                                wr[:, half, :], start=(half == 0), stop=(half == 1))
                last.then_inc(lg_done, 1)

            def stage2(s, p):
                fixed = isinstance(s, int)
                if not fixed or 1 <= s <= B:
                    mid(s - 1, 1 - p)
                if not fixed or s < B:
                    turn_x(s, p)
                if not fixed or s >= 2:
                    output2(s - 2)
                if not fixed or s < B:
                    project_zx(s)
                if not fixed or s >= 2:
                    turn_y(s - 2)
                if not fixed or 1 <= s <= B:
                    mix_y(s - 1)
                if not fixed or s >= 2:
                    route(s - 2)

            pe.wait_ge(w_rest, W_REST)
            stage2(0, 0)
            stage2(1, 1)
            with pe.Fori(1, B // 2) as i:
                stage2(i * 2, 0)
                stage2(i * 2 + 1, 1)
            stage2(B, 0)
            stage2(B + 1, 1)

            pe.wait_ge(ch_step, 6)
            for t in range(T2):
                last = nc.tensor.transpose(ps[0:32, 0, t * 128:(t + 1) * 128],
                                           pe_[:, t * B:(t + 1) * B, :].rearrange("p b e -> p (b e)"), eye[:])
            last.then_inc(pr_done, 1)

            def project3(c, k, bank, p):
                first = isinstance(c, int) and c == 0
                if k == 0:
                    pe.wait_ge(selb_ready, c + 1)
                    if not first:
                        pe.wait_ge(m3_read, c * 3 - 1)
                    for half in range(2):
                        last = nc.tensor.matmul(ps[0:HC + 1, bank, half * L:(half + 1) * L],
                                                nest[:, half * (HC + 1):(half + 1) * (HC + 1)], selb[:],
                                                start=True, stop=True)
                    last.then_inc(m_done, 1)
                elif k in (1, 2):
                    pe.wait_ge(yhat_ready, c + 1)
                    if k == 1 and not first:
                        pe.wait_ge(m3_read, c * 3)
                    at = MLP + (k - 1) * C
                    for half in range(2):
                        for a in range(2):
                            last = nc.tensor.matmul(ps[0:HC, bank, half * L:(half + 1) * L],
                                                    w1[0:HC + a, a, at + half * HC:at + (half + 1) * HC],
                                                    yhat[0:HC + a, a, :], start=(a == 0), stop=(a == 1))
                    last.then_inc(q3_done if k == 1 else k3_done, 1)
                elif k in (3, 4):
                    t = k - 3
                    pe.wait_ge(q3_split, c + 1)
                    if k == 4:
                        pe.wait_ge(v3_ready, c * 2 + 1)
                    for a in range(2):
                        last = nc.tensor.matmul(ps[:, bank, 0:C], yhat[0:HC + a, a, t * 128:(t + 1) * 128],
                                                w1[0:HC + a, a, MLP + 2 * C:MLP + 3 * C],
                                                start=(a == 0), stop=(a == 1))
                    last.then_inc(v3_done, 1)
                else:
                    j = k - 5
                    if j == 0:
                        pe.wait_ge(v3_ready, c * 2 + 2)
                    if j == 1:
                        pe.wait_ge(k3_split, c + 1)
                        if not (isinstance(c, int) and c < 2):
                            pe.wait_ge(f_read, c * 2 - 2)
                    if j == 2:
                        pe.wait_ge(m3_read, c * 3 + 1)
                    for i in range(2):
                        m = 2 * j + i
                        for a in range(2):
                            last = nc.tensor.matmul(ps[:, bank, i * L:(i + 1) * L],
                                                    w1[0:HC + a, a, m * 128:(m + 1) * 128], yhat[0:HC + a, a, :],
                                                    start=(a == 0), stop=(a == 1))
                    last.then_inc(m3_done, 1)

            def output3(b, p, t):
                if t == 0:
                    if not (isinstance(b, int) and b + 2 >= B):
                        pe.wait_ge(k3_split, b + 3)
                    pe.wait_ge(ot_ready, B + b + 1)
                    pe.wait_ge(gelu_done, b + 1)
                    pe.wait_ge(gates_ready, b + 1)
                else:
                    pe.wait_ge(f_read, b * 2 + 1)
                for j in range(MJ):
                    nc.tensor.matmul(ps[:, 0, 0:C], y2T[p][:, j, t * 128:(t + 1) * 128], w2[:, j, :],
                                     start=(j == 0), stop=False)
                for g in range(G3):
                    nc.tensor.matmul(ps[:, 0, 0:C], oT[:, g, t * 128:(t + 1) * 128], w2[:, MJ + g, :],
                                     start=False, stop=(g == G3 - 1))
                nc.tensor.matmul(ps[:, 0, C:2 * C], gselb[:, p, t * 128:(t + 1) * 128],
                                 nestf[:, 2 * (HC + 1):2 * (HC + 1) + C], start=True, stop=True).then_inc(f_done, 1)

            PIECES = {0: (0, 0), 1: (1, 1), 2: (2, 0), 3: (3, 1), 5: (4, 1), 7: (5, 1), 8: (6, 0), 9: (7, 1)}

            def wait_qk3(c, p):
                each = 16 * (QD3 + KD)
                pe.wait_ge(qk3_stacked[p], (c // 2 + 1) * each if isinstance(c, int) else (c - p) * (each // 2) + each)

            def stage3(b, p):
                last = isinstance(b, int) and b == B - 1
                first = isinstance(b, int) and b == 0
                n0 = B * U + b * U
                for u in range(U):
                    if u < U - 1:
                        pe.wait_ge(exp_done, n0 + u)
                        unit_scores3((u + 1) % 2, p, u + 1)
                    elif not last:
                        pe.wait_ge(exp_done, n0 + u)
                        wait_qk3(b + 1, 1 - p)
                        unit_scores3(0, 1 - p, 0)
                    if not last and u in PIECES:
                        project3(b + 1, *PIECES[u], 1 - p)
                    pe.wait_ge(exp_done, n0 + u + 1)
                    pe.wait_ge(pt_ready, n0 + u - 1)
                    unit_turn(u)
                    if u == 0:
                        if not first:
                            pe.wait_ge(pt_ready, n0)
                            unit_pv3(1 - p, U - 1)
                    else:
                        if u == 1:
                            pe.wait_ge(v3_ready, b * 2 + 2)
                            pe.wait_ge(vones, 1)
                            pe.wait_ge(o_read, B + b)
                        pe.wait_ge(pt_ready, n0 + u)
                        unit_pv3(p, u - 1)
                    if u in (4, 6) and not first:
                        output3(b - 1, 1 - p, (u - 4) // 2)

            pe.wait_ge(w2_ready, 3)
            for k in range(8):
                project3(0, k, (0, 1, 0, 1, 1, 1, 0, 1)[k], 0)
            wait_qk3(0, 0)
            unit_scores3(0, 0, 0)
            over_batches(pe, stage3)
            pe.wait_ge(pt_ready, 2 * B * U)
            unit_pv3(1, U - 1)
            output3(B - 1, 1, 0)
            output3(B - 1, 1, 1)

        @block.vector
        def _(dve):
            def unit_max(n, slot):
                dve.wait_ge(s_done, n + 1)
                if not isinstance(n, int) or n >= 4:
                    dve.wait_ge(exp_done, n - 3)
                nc.vector.tensor_reduce(nmax[:, slot % 4, :],
                                        ps[:, SC + slot % 2, :].rearrange("p (a n) -> p a n", a=2),
                                        AX.X, ALU.max, negate=True).then_inc(max_done, 1)

            def unit_copy(n, u):
                dve.wait_ge(t_done, n + 1)
                if not isinstance(n, int) or n >= 3:
                    dve.wait_ge(pv_done, n - 2)
                nc.vector.tensor_copy(probT[:, u % 3, :], ps[:, TR + u % 2, :]).then_inc(pt_ready, 1)

            def normalise(b, tokens_inner):
                dve.wait_ge(pv_done, b * U + U)
                nc.vector.transpose(otA[:], psO).then_inc(o_read, 1)
                dve.wait_ge(o_read, b + 1)
                blocks = otA[:].rearrange("p (k e) -> p k e", e=32)
                nc.vector.reciprocal(rsum[:], blocks[:, :, D]).then_inc(ot_sum, 1)
                dve.wait_ge(ot_sum, b + 1)
                nc.vector.tensor_tensor(blocks[:, :, 0:D], blocks[:, :, 0:D],
                                        rsum[:].unsqueeze(2).broadcast_to([128, G3 * L // 32, D]),
                                        ALU.mult).then_inc(ot_norm, 1)
                dve.wait_ge(ot_norm, b + 1)
                if tokens_inner:
                    nc.vector.transpose(oT[:].rearrange("p g n -> p (g n)"), otA[:]).then_inc(ot_ready, 1)
                else:
                    for g in range(G3):
                        last = nc.vector.transpose(
                            oT[:, g, :].rearrange("p (q w) -> p w q", w=W),
                            otA[:, g * L:(g + 1) * L].rearrange("p (w q) -> p w q", w=W))
                    last.then_inc(ot_ready, 1)

            def pool_q(c, k, bank):
                half, tb = divmod(k, 2)
                dve.wait_ge(q_done, c * 4 + k + 1)
                if not (isinstance(c, int) and c == 0):
                    dve.wait_ge(q_split, c * 3)
                nc.vector.tensor_reduce(
                    qp[:, half, tb * 128:(tb + 1) * 128].rearrange("p (w j) -> p w j", w=2),
                    ps[0:HC, bank, :].rearrange("p (w s j) -> p w j s", w=2, s=STRIDE),
                    AX.X, ALU.max).then_inc(q_pooled, 1)

            def low_k(c, k, bank):
                tb, half = divmod(k, 2)
                dve.wait_ge(k_ready, c * 4 + k + 1)
                where = slice(tb * 512, (tb + 1) * 512)
                nc.vector.scalar_tensor_tensor(khl[:, 1, half, where], ps[0:HC, bank, :], SCALE,
                                               khl[:, 0, half, where].bitcast(F32), ALU.mult,
                                               ALU.subtract).then_inc(k_split, 1)

            def take_h(b, t):
                dve.wait_ge(h_done, b * 2 + t + 1)
                nc.vector.tensor_tensor(h_all[:, tile(b, t), :].rearrange("p a c -> p (a c)"), ps[:, 0, 0:C], bo[:],
                                        ALU.add).then_inc(h_ready, 1)

            def stats1(b):
                dve.wait_ge(consts, 1)
                dve.wait_ge(h_ready, b * 2 + 2)
                for t in range(T2):
                    last = nc.vector.bn_stats(st6[:, t, :], h_all[:, tile(b, t), :].rearrange("p a c -> p (a c)"))
                last.then_inc(bn_done, 1)
                dve.wait_ge(consts, 1)
                dve.wait_ge(bn_done, b + 1)
                if not (isinstance(b, int) and b == 0):
                    dve.wait_ge(stat_done, b)
                for t in range(T2):
                    last = nc.vector.bn_aggr(mv[:, t, :], st6[:, t, :])
                last.then_inc(mv_done, 1)
                dve.wait_ge(mv_done, b + 1)
                nc.vector.tensor_copy(mean_all[:, bass.ds(b * T2, T2)], mv[:, :, 0])
                nc.vector.tensor_scalar(ve[:], mv[:, :, 1], 1e-5, None, ALU.add).then_inc(ve_done, 1)

            def stage1(b, p):
                last = isinstance(b, int) and b == B - 1
                first = isinstance(b, int) and b == 0
                for u in range(U):
                    if u == 1 and not first:
                        normalise(b - 1, False)
                    if u < U - 1 or not last:
                        unit_max(b * U + u + 1, u + 1)
                    if u < 4 and not last:
                        pool_q(b + 1, u, u % 2)
                    unit_copy(b * U + u, u)
                    if 4 <= u < 8 and not last:
                        low_k(b + 1, u - 4, K_BANKS[u - 4])
                    if u in (3, 4) and not first:
                        take_h(b - 1, u - 3)
                    if u == 5 and not first:
                        stats1(b - 1)

            dve.wait_ge(w_first, W_FIRST)
            for k in range(4):
                pool_q(0, k, k % 2)
            for k in range(4):
                low_k(0, k, K_BANKS[k])
            unit_max(0, 0)
            over_batches(dve, stage1)
            normalise(B - 1, False)
            take_h(B - 1, 0)
            take_h(B - 1, 1)
            stats1(B - 1)

            def normal_x(b, p):
                for t in range(T2):
                    h = h_all[:, tile(b, t), :].rearrange("p a c -> p (a c)")
                    nc.vector.tensor_scalar(uu2[:, t, :], h, mean_all[:, tile(b, t)], r1_all[:, tile(b, t)],
                                            ALU.subtract, ALU.mult).then_inc(u_done, 1)
                    last = nc.vector.tensor_scalar(xh[:, p, t, :], h, mean_all[:, tile(b, t)], rr_all[:, tile(b, t)],
                                                   ALU.subtract, ALU.mult)
                last.then_inc(xh_ready, 1)
                dve.wait_ge(u_done, b * 2 + 2)
                dve.wait_ge(xh_ready, b + 1)
                hb = h_all[:, bass.ds(b * T2, T2), :]
                nc.vector.tensor_tensor(hb, hb, uu2[:], ALU.add).then_inc(hu_done, 1)
                dve.wait_ge(hu_done, b + 1)

            uu2 = res

            def step_sizes(b, p):
                k = [small[:, i, :] for i in range(9)]
                v3 = small[:, 0, :].rearrange("p (t h) -> p t h", t=T2)
                at = b * 9
                dve.wait_ge(dt_done, b + 1)
                nc.vector.tensor_tensor(v3, psDt.rearrange("p (t h) -> p t h", t=T2),
                                        dtb[:].unsqueeze(1).broadcast_to([128, T2, SH]), ALU.add).then_inc(dt_step, 1)
                dve.wait_ge(dt_step, at + 1)
                nc.vector.scalar_tensor_tensor(k[1], k[0], -1.0, k[0], ALU.mult, ALU.max).then_inc(dt_step, 1)
                dve.wait_ge(dt_exp, b + 1)
                nc.vector.tensor_scalar(k[3], k[2], 1.0, None, ALU.add).then_inc(dt_step, 1)
                dve.wait_ge(dt_step, at + 3)
                nc.vector.scalar_tensor_tensor(k[5], k[3], -1.0, k[2], ALU.add, ALU.subtract).then_inc(dt_step, 1)
                nc.vector.reciprocal(k[6], k[3]).then_inc(dt_step, 1)
                dve.wait_ge(dt_step, at + 5)
                nc.vector.tensor_tensor(k[7], k[5], k[6], ALU.mult).then_inc(dt_step, 1)
                dve.wait_ge(dt_step, at + 6)
                dve.wait_ge(dt_log, b + 1)
                nc.vector.tensor_tensor(k[8], k[4], k[7], ALU.subtract).then_inc(dt_step, 1)
                dve.wait_ge(dt_step, at + 7)
                dtf = dt2[:, p].rearrange("p t h -> p (t h)")
                nc.vector.scalar_tensor_tensor(dtf, k[0], 0.0, k[8], ALU.max, ALU.add).then_inc(dt_step, 1)
                dve.wait_ge(dt_step, at + 8)
                nc.vector.tensor_tensor(a2[:, p], dt2[:, p], aneg[:].unsqueeze(1).broadcast_to([128, T2, SH]),
                                        ALU.mult).then_inc(dt_step, 1)
                dve.wait_ge(dt_step, at + 9)

            def convolve(b, p):
                for c in range(TAPS):
                    dve.wait_ge(xp_ready, b * 4 + c + 1)
                    n = b * 16 + c * 4
                    if c == 0 and not (isinstance(b, int) and b == 0):
                        dve.wait_ge(xc_ready, b)
                    nc.vector.tensor_scalar(acc[:, c, :], xpad[:, c, 4:4 + L], cw[:, c, 3:4], cb[:, c:c + 1],
                                            ALU.mult, ALU.add).then_inc(conv_step, 1)
                    for k in range(3):
                        dve.wait_ge(conv_step, n + k + 1)
                        last = nc.vector.scalar_tensor_tensor(acc[:, c, :], xpad[:, c, 1 + k:1 + k + L],
                                                              cw[:, c, k:k + 1], acc[:, c, :], ALU.mult, ALU.add)
                        last.then_inc(conv_step, 1)

            def mix_tokens(b, p):
                for t in range(T2):
                    dve.wait_ge(tok_done, b * 2 + t + 1)
                    if t == 0 and not (isinstance(b, int) and b == 0):
                        dve.wait_ge(y_done, b)
                    nc.vector.tensor_tensor(xdt[:, 2 * t, :, :],
                                            ps[:, 3, 0:INNER].rearrange("p (h q) -> p h q", h=SH),
                                            dt2[:, p, t, :].unsqueeze(2).broadcast_to([128, SH, 64]),
                                            ALU.mult).then_inc(xdt_ready, 1)
                    if t == 0:
                        dve.wait_ge(suf_ready, b + 1)
                        dve.wait_ge(xdt_ready, b * 3 + 1)
                        nc.vector.tensor_tensor(xdt[:, 1, :, :], xdt[:, 0, :, :],
                                                esuf[:].unsqueeze(2).broadcast_to([128, SH, 64]),
                                                ALU.mult).then_inc(xdt_ready, 1)
                dve.wait_ge(g_done, b + 1)
                cut3 = ps[:, 3, 0:384].rearrange("p (a t) -> p a t", a=3)
                nc.vector.tensor_tensor(gmask[:, 0, :], cut3[:, 0, :], upto[:], ALU.mult)
                nc.vector.tensor_copy(gmask[:, 1, :], cut3[:, 1, :])
                nc.vector.tensor_tensor(gmask[:, 2, :], cut3[:, 2, :], upto[:], ALU.mult).then_inc(gm_ready, 1)
                dve.wait_ge(gm_ready, b + 1)
                for i, g in enumerate((0, 2, 1)):
                    dve.wait_ge(dec_ready, b * 3 + i + 1)
                    nc.vector.tensor_tensor(mix[:, i], dec[(i + p) % 2],
                                            gmask[:, g, :].unsqueeze(1).broadcast_to([128, SH, 128]),
                                            ALU.mult).then_inc(mix_ready, 1)

            def take_y(b, p):
                dve.wait_ge(y_done, b + 1)
                if not (isinstance(b, int) and b == 0):
                    dve.wait_ge(gt_ready, b)
                for c in range(XC):
                    last = nc.vector.scalar_tensor_tensor(y2[:, c, :], xc[:, p, c, :], dd[:, c:c + 1],
                                                          psY[:, c * L:(c + 1) * L], ALU.mult, ALU.add)
                last.then_inc(y_ready, 1)

            def take_h2(b):
                dve.wait_ge(o2_done, b + 1)
                nc.vector.tensor_scalar(ms[:], ps[:, 3, 2 * C:2 * C + 2], 1.0 / INNER, 1e-5,
                                        ALU.mult, ALU.add).then_inc(ms_done, 1)
                dve.wait_ge(rt_done, b + 1)
                if not (isinstance(b, int) and b == 0):
                    dve.wait_ge(h2_used, b)
                for t in range(T2):
                    last = nc.vector.scalar_tensor_tensor(h2[:, t, :], ps[:, 3, t * C:(t + 1) * C], rt[:, t:t + 1],
                                                          h_all[:, tile(b, t), :].rearrange("p a c -> p (a c)"),
                                                          ALU.mult, ALU.add)
                last.then_inc(h2_ready, 1)
                dve.wait_ge(h2_ready, b + 1)
                for t in range(T2):
                    last = nc.vector.bn_stats(st6[:, t, :], h2[:, t, :])
                last.then_inc(bn2_done, 1)
                dve.wait_ge(consts, 1)
                dve.wait_ge(bn2_done, b + 1)
                for t in range(T2):
                    last = nc.vector.bn_aggr(mv[:, t, :], st6[:, t, :])
                last.then_inc(mv2_done, 1)
                dve.wait_ge(mv2_done, b + 1)
                nc.vector.tensor_scalar(ve[:], mv[:, :, 1], 1e-5, None, ALU.add).then_inc(ve3_done, 1)

            def take_u3(b):
                dve.wait_ge(r3_done, b + 1)
                if not (isinstance(b, int) and b == 0):
                    dve.wait_ge(yt_done, b)
                for t in range(T2):
                    nc.vector.tensor_scalar(u3_all[:, tile(b, t), :].rearrange("p a c -> p (a c)"), h2[:, t, :],
                                            mv[:, t, 0:1], r1[:, t:t + 1], ALU.subtract, ALU.mult)
                    last = nc.vector.tensor_scalar(uu[:, t, :], h2[:, t, :], mv[:, t, 0:1], rr[:, t:t + 1],
                                                   ALU.subtract, ALU.mult)
                last.then_inc(yh_ready, 1)

            def take_yT(b):
                dve.wait_ge(yt_done, b + 1)
                if not (isinstance(b, int) and b == 0):
                    dve.wait_ge(lg_done, b)
                    dve.wait_ge(yT_ready, b)
                nc.vector.tensor_copy(yhT[:].rearrange("p a n -> p (a n)"), ps[0:HC, TR, :]).then_inc(yhT_ready, 1)

            def take_logits(b):
                dve.wait_ge(lg_done, b + 1)
                for t in range(T2):
                    last = nc.vector.tensor_scalar(lg[:, t, bass.ds(b, 1), :].rearrange("p b e -> p (b e)"),
                                                   psLg[:, t * E:(t + 1) * E], s2[:, t:t + 1], None, ALU.mult)
                last.then_inc(lg_ready, 1)

            def stage2(s, p):
                fixed = isinstance(s, int)
                if not fixed or s >= 2:
                    take_y(s - 2, p)
                if not fixed or s < B:
                    normal_x(s, p)
                if not fixed or 1 <= s <= B:
                    mix_tokens(s - 1, 1 - p)
                if not fixed or s >= 2:
                    take_h2(s - 2)
                if not fixed or s < B:
                    step_sizes(s, p)
                if not fixed or s >= 2:
                    take_u3(s - 2)
                if not fixed or s < B:
                    convolve(s, p)
                if not fixed or s >= 2:
                    take_yT(s - 2)
                    take_logits(s - 2)

            dve.wait_ge(w_rest, W_REST)
            for c in range(XC):
                last = nc.vector.tensor_scalar(wout[:, c, :], wout[:, c, :], rms[:, c:c + 1], None, ALU.mult)
            last.then_inc(setup, 1)
            nc.vector.tensor_copy(nest[:], nestf[:, 0:2 * (HC + 1)]).then_inc(w2_ready, 1)
            dve.wait_ge(alog_exp, 1)
            nc.vector.tensor_scalar(aneg[:], small[:, 11, 0:SH], -1.0, None, ALU.mult).then_inc(setup, 1)
            nc.vector.tensor_tensor(b2[:], b2[:], b2x[:], ALU.add).then_inc(w2_ready, 1)
            dve.wait_ge(w2x_loaded, 16)
            nc.vector.tensor_tensor(w2[:], w2[:], w2x, ALU.add).then_inc(w2_ready, 1)
            dve.wait_ge(setup, 2)
            dve.wait_ge(w2_ready, 3)
            dve.wait_ge(stat_done, B)
            dve.wait_ge(fills, 1)
            stage2(0, 0)
            stage2(1, 1)
            with dve.Fori(1, B // 2) as i:
                stage2(i * 2, 0)
                stage2(i * 2 + 1, 1)
            stage2(B, 0)
            stage2(B + 1, 1)

            lgf = lg[:].rearrange("p t b e -> p (t b) e")
            tb = [128, T2 * B, E]
            dve.wait_ge(lg_ready, B)
            nc.vector.tensor_reduce(lsm[:, 0, :], lgf, AX.X, ALU.max).then_inc(ch_step, 1)
            dve.wait_ge(ch_step, 1)
            nc.vector.tensor_tensor(lgf, lgf, lsm[:, 0, :].unsqueeze(2).broadcast_to(tb), ALU.subtract).then_inc(ch_step, 1)
            dve.wait_ge(ch_exp, 1)
            nc.vector.tensor_reduce(lsm[:, 1, :], pe_[:], AX.X, ALU.add).then_inc(ch_step, 1)
            dve.wait_ge(ch_step, 3)
            nc.vector.reciprocal(lsm[:, 2, :], lsm[:, 1, :]).then_inc(ch_step, 1)
            dve.wait_ge(ch_step, 4)
            nc.vector.tensor_tensor(pe_[:], pe_[:], lsm[:, 2, :].unsqueeze(2).broadcast_to(tb), ALU.mult).then_inc(ch_step, 2)
            dve.wait_ge(pr_done, 1)
            nc.vector.tensor_copy(pr[:], ps[0:32, 0, 0:L]).then_inc(ch_step, 1)
            src, n = pr[:], 7
            for i in range(CAP // 8):
                dve.wait_ge(ch_step, n)
                nc.vector.max(top8[:], src).then_inc(ch_step, 1)
                dve.wait_ge(ch_step, n + 1)
                nc.vector.match_replace(pick[:, i % 2, :], top8[:], src, -1.0).then_inc(ch_step, 1)
                src, n = pick[:, i % 2, :], n + 2
            dve.wait_ge(ch_step, n)
            nc.vector.tensor_scalar(sel[:], src, 0.0, None, ALU.is_lt).then_inc(ch_step, 1)
            dve.wait_ge(ch_step, n + 1)
            nc.vector.tensor_tensor(gsel[:], pr[:], sel[:], ALU.mult).then_inc(ch_step, 1)
            dve.wait_ge(ch_step, n + 2)

            def take_sel(c, p):
                if not (isinstance(c, int) and c == 0):
                    dve.wait_ge(m_done, c)
                nc.vector.tensor_scalar(selb[:], sel[:], rowm[:, bass.ds(c, 1)], None, ALU.mult).then_inc(selb_ready, 1)

            def take_gates(c, p):
                if not (isinstance(c, int) and c < 2):
                    dve.wait_ge(f_done, c * 2 - 2)
                nc.vector.tensor_scalar(gselb[:, p, :], gsel[:], rowm[:, bass.ds(c, 1)], None, ALU.mult).then_inc(gates_ready, 1)

            def take_yhat(c):
                dve.wait_ge(m_done, c + 1)
                if not (isinstance(c, int) and c == 0):
                    dve.wait_ge(m3_done, c * 3)
                nc.vector.tensor_tensor(yhat[:], yT_all[:, :, bass.ds(c * L, L)],
                                        ps[0:HC + 1, 0, :].rearrange("p (a n) -> p a n", a=2),
                                        ALU.mult).then_inc(yhat_ready, 1)

            def low_q3(c):
                dve.wait_ge(q3_ready, c + 1)
                nc.vector.tensor_tensor(qhl[:, 1].rearrange("p a n -> p (a n)"), ps[0:HC, 1, :],
                                        qhl[:, 0].rearrange("p a n -> p (a n)").bitcast(F32),
                                        ALU.subtract).then_inc(q3_split, 1)

            def low_k3(c):
                dve.wait_ge(k3_ready, c + 1)
                nc.vector.scalar_tensor_tensor(khl3[:, 1].rearrange("p a n -> p (a n)"), ps[0:HC, 0, :], SCALE,
                                               khl3[:, 0].rearrange("p a n -> p (a n)").bitcast(F32),
                                               ALU.mult, ALU.subtract).then_inc(k3_split, 1)

            def take_mlp(c, p, j, bank):
                dve.wait_ge(m3_done, c * 3 + j + 1)
                if j == 0 and not (isinstance(c, int) and c < 2):
                    dve.wait_ge(f_done, c * 2 - 2)
                nc.vector.tensor_copy(y2T[p][:, 2 * j:2 * j + 2, :].rearrange("p j n -> p (j n)"),
                                      ps[:, bank, :]).then_inc(m3_read, 1)

            def take_out(b, t):
                dve.wait_ge(f_done, b * 2 + t + 1)
                if t == 0 and not (isinstance(b, int) and b == 0):
                    dve.wait_ge(res_ready, b)
                nc.vector.tensor_tensor(res[:, t, :], ps[:, 0, 0:C], b2[:], ALU.add).then_inc(res_step, 1)
                dve.wait_ge(res_step, b * 2 + t + 1)
                nc.vector.tensor_tensor(res[:, t, :], res[:, t, :], ps[:, 0, C:2 * C], ALU.mult).then_inc(f_read, 1)

            def stage3(b, p):
                last = isinstance(b, int) and b == B - 1
                first = isinstance(b, int) and b == 0
                n0 = B * U + b * U
                if not last:
                    take_sel(b + 1, 1 - p)
                for u in range(U):
                    if u == 1 and not first:
                        normalise(B + b - 1, True)
                    if u < U - 1 or not last:
                        unit_max(n0 + u + 1, u + 1)
                    if not last:
                        if u == 0:
                            take_yhat(b + 1)
                        if u == 7:
                            take_mlp(b + 1, 1 - p, 0, 1)
                        if u == 8:
                            take_mlp(b + 1, 1 - p, 1, 0)
                        if u == 9:
                            take_mlp(b + 1, 1 - p, 2, 1)
                        if u == 10:
                            take_gates(b + 1, 1 - p)
                    unit_copy(n0 + u, u)
                    if u == 1 and not last:
                        low_q3(b + 1)
                    if u == 2 and not last:
                        low_k3(b + 1)
                    if u in (4, 6) and not first:
                        take_out(b - 1, (u - 4) // 2)

            take_sel(0, 0)
            take_yhat(0)
            low_q3(0)
            low_k3(0)
            for j in range(3):
                take_mlp(0, 0, j, (1, 0, 1)[j])
            take_gates(0, 0)
            unit_max(B * U, 0)
            over_batches(dve, stage3)
            normalise(2 * B - 1, True)
            take_out(B - 1, 0)
            take_out(B - 1, 1)

        @block.scalar
        def _(act):
            def unit_exp(n, u):
                act.wait_ge(max_done, n + 1)
                if not isinstance(n, int) or n >= 3:
                    act.wait_ge(t_done, n - 2)
                for i in range(2):
                    last = nc.scalar.activation(prob[:, u % 3, i * 256:(i + 1) * 256],
                                                ps[:, SC + u % 2, i * 256:(i + 1) * 256], ACT.Exp,
                                                bias=nmax[:, u % 4, i:i + 1])
                last.then_inc(exp_done, 1)

            def take_k(c, p, k, bank):
                tb, half = divmod(k, 2)
                act.wait_ge(k_done, c * 4 + k + 1)
                if not (isinstance(c, int) and c == 0):
                    wait_k_stacked(c, tb)
                nc.scalar.activation(khl[:, 0, half, tb * 512:(tb + 1) * 512], ps[0:HC, bank, :],
                                     ACT.Copy, scale=SCALE).then_inc(k_ready, 1)

            def wait_k_stacked(c, tb):
                act.wait_ge(k_stacked[tb], c * 16 * KD)

            def take_v(c, p, k, bank):
                act.wait_ge(v_done, c * 4 + k + 1)
                if not (isinstance(c, int) and c < 2):
                    act.wait_ge(pv_done, (c - 1) * U)
                nc.scalar.activation(va[p][:, 2 * k:2 * k + 2, :, 0:D],
                                     ps[:, bank, 0:2 * C].rearrange("p (t h e) -> p t h e", t=2, e=D),
                                     ACT.Copy).then_inc(v_ready, 1)

            def take_kv(c, p, u):
                if 4 <= u < 8:
                    take_k(c, p, u - 4, K_BANKS[u - 4])
                elif u >= 8:
                    take_v(c, p, u - 8, u % 2)

            def stage1(b, p):
                last = isinstance(b, int) and b == B - 1
                for u in range(U):
                    unit_exp(b * U + u, u)
                    if not last:
                        take_kv(b + 1, 1 - p, u)

            for u in range(U):
                take_kv(0, 0, u)
            over_batches(act, stage1)

            def square(b):
                act.wait_ge(gt_ready, b + 1)
                if not (isinstance(b, int) and b == 0):
                    act.wait_ge(o2_done, b)
                nc.scalar.activation(gsq_, g_,
                                     ACT.Square).then_inc(gsq_ready, 1)

            def decays(b, p):
                act.wait_ge(suf_done, b + 1)
                if not (isinstance(b, int) and b == 0):
                    act.wait_ge(mix_ready, b * 3)
                for i in range(3):
                    act.wait_ge(seg_done, b * 3 + i + 1)
                    if i == 2:
                        act.wait_ge(mix_ready, b * 3 + 1)
                    nc.scalar.activation(dec[(i + p) % 2][:].rearrange("p (a h) t -> p a (h t)", a=2),
                                         ps[:, SC:SC + 2, 0:384], ACT.Exp).then_inc(dec_ready, 1)
                    if i == 0:
                        nc.scalar.activation(esuf[:], psSuf, ACT.Exp).then_inc(suf_ready, 1)

            def take_xn(b):
                act.wait_ge(xt_done, b + 1)
                if not (isinstance(b, int) and b == 0):
                    act.wait_ge(zx_done, b * 4)
                for half in range(2):
                    nc.scalar.activation(xnT[:, half, :], ps[0:HC, TR, half * L:(half + 1) * L], ACT.Identity,
                                         bias=lnb[:, half:half + 1], scale=lnw[:, half:half + 1]).then_inc(xn_ready, 1)

            def dt_functions(b):
                act.wait_ge(dt_step, b * 9 + 2)
                nc.scalar.activation(small[:, 2, :], small[:, 1, :], ACT.Exp, scale=-1.0).then_inc(dt_exp, 1)
                act.wait_ge(dt_step, b * 9 + 3)
                nc.scalar.activation(small[:, 4, :], small[:, 3, :], ACT.Ln).then_inc(dt_log, 1)

            def take_zx(b, p):
                first = isinstance(b, int) and b == 0
                act.wait_ge(zx_done, b * 4 + 1)
                if not (isinstance(b, int) and b < 2):
                    act.wait_ge(gt_ready, b - 1)
                nc.scalar.activation(sz[:, p, 0:2, :].rearrange("p c t -> p (c t)"), ps[:, 0, :], ACT.Silu).then_inc(zx_read, 1)
                act.wait_ge(zx_done, b * 4 + 2)
                if not first:
                    act.wait_ge(conv_step, b * 16)
                nc.scalar.activation(sz[:, p, 2, :], ps[:, 1, 0:L], ACT.Silu)
                nc.scalar.activation(xpad[:, 0, 4:4 + L], ps[:, 1, L:2 * L], ACT.Copy).then_inc(xp_ready, 1)
                act.wait_ge(xp_ready, b * 4 + 1)
                act.sem_inc(zx_read, 1)
                act.wait_ge(zx_done, b * 4 + 3)
                nc.scalar.activation(xpad[:, 1:3, 4:4 + L], ps[:, 0, :].rearrange("p (c t) -> p c t", c=2),
                                     ACT.Copy).then_inc(xp_ready, 2)
                act.wait_ge(xp_ready, b * 4 + 3)
                act.sem_inc(zx_read, 1)
                act.wait_ge(zx_done, b * 4 + 4)
                nc.scalar.activation(xpad[:, 3, 4:4 + L], ps[:, 1, 0:L], ACT.Copy).then_inc(xp_ready, 1)
                act.wait_ge(xp_ready, b * 4 + 4)
                act.sem_inc(zx_read, 1)
                for c in range(XC):
                    act.wait_ge(conv_step, b * 16 + 4 * c + 4)
                    if c == 0 and not (isinstance(b, int) and b < 2):
                        act.wait_ge(y_ready, b - 1)
                    nc.scalar.activation(xc[:, p, c, :], acc[:, c, :], ACT.Silu)
                act.wait_ge(conv_step, b * 16 + 16)
                if not first:
                    act.wait_ge(g_done, b)
                for i in range(2):
                    last = nc.scalar.activation(bcT[:, i, :], acc[64 * i:64 * i + 64, 3, :], ACT.Silu)
                last.then_inc(xc_ready, 1)

            def take_y(b):
                act.wait_ge(yhT_ready, b + 1)
                for half in range(2):
                    last = nc.scalar.activation(yT_all[0:HC, half, bass.ds(b * L, L)],
                                                yhT[:, half, :], ACT.Identity,
                                                bias=bet[:, half:half + 1], scale=gam[:, half:half + 1])
                last.then_inc(yT_ready, 1)

            def stage2(s, p):
                fixed = isinstance(s, int)
                if not fixed or s >= 2:
                    square(s - 2)
                if not fixed or 1 <= s <= B:
                    decays(s - 1, 1 - p)
                if not fixed or s < B:
                    take_xn(s)
                    dt_functions(s)
                    take_zx(s, p)
                if not fixed or s >= 2:
                    take_y(s - 2)

            act.wait_ge(w_rest, W_REST)
            nc.scalar.activation(small[:, 11, 0:SH], aneg[:], ACT.Exp).then_inc(alog_exp, 1)
            act.wait_ge(fills, 1)
            stage2(0, 0)
            stage2(1, 1)
            with act.Fori(1, B // 2) as i:
                stage2(i * 2, 0)
                stage2(i * 2 + 1, 1)
            stage2(B, 0)
            stage2(B + 1, 1)

            act.wait_ge(ch_step, 2)
            nc.scalar.activation(pe_[:].rearrange("p a e -> p (a e)"), lg[:].rearrange("p t b e -> p (t b e)"),
                                 ACT.Exp).then_inc(ch_exp, 1)

            def take_q3(c):
                act.wait_ge(q3_done, c + 1)
                nc.scalar.activation(qhl[:, 0].rearrange("p a n -> p (a n)"), ps[0:HC, 1, :],
                                     ACT.Copy).then_inc(q3_ready, 1)

            def take_k3(c, p):
                act.wait_ge(k3_done, c + 1)
                nc.scalar.activation(khl3[:, 0].rearrange("p a n -> p (a n)"), ps[0:HC, 0, :],
                                     ACT.Copy, scale=SCALE).then_inc(k3_ready, 1)

            def take_v3(c, p, t):
                act.wait_ge(v3_done, c * 2 + t + 1)
                if not (isinstance(c, int) and c < 2):
                    act.wait_ge(pv_done, B * U + (c - 1) * U)
                nc.scalar.activation(va3[p][:, t, :, 0:D], ps[:, 1, 0:C].rearrange("p (h e) -> p h e", e=D),
                                     ACT.Copy).then_inc(v3_ready, 1)

            def gelu(c, p):
                act.wait_ge(m3_read, c * 3 + 3)
                y = y2T[p].rearrange("p j n -> p (j n)")
                nc.scalar.activation(y, y, ACT.Gelu).then_inc(gelu_done, 1)

            def stage3(b, p):
                last = isinstance(b, int) and b == B - 1
                for u in range(U):
                    unit_exp(B * U + b * U + u, u)
                    if last:
                        continue
                    if u == 1:
                        take_q3(b + 1)
                    if u == 2:
                        take_k3(b + 1, 1 - p)
                    if u in (3, 5):
                        take_v3(b + 1, 1 - p, (u - 3) // 2)
                    if u == 10:
                        gelu(b + 1, 1 - p)

            take_q3(0)
            take_k3(0, 0)
            take_v3(0, 0, 0)
            take_v3(0, 0, 1)
            gelu(0, 0)
            over_batches(act, stage3)

        @block.gpsimd
        def _(pool):
            filled = [(xT[0][HC:HC + 1, 1, :], 1.0), (xT[1][HC:HC + 1, 1, :], 1.0), (va_ones(areaV1, N // 128), 1.0),
                      (ones[:], 1.0), (mhalf[:], -0.5), (eps5[:], 1e-5), (eps6[:], 1e-6)]
            for i, (where, value) in enumerate(filled):
                if i:
                    pool.wait_ge(consts, i)
                nc.gpsimd.memset(where, value).then_inc(consts, 1)

            def split_q(c):
                qm_, high, low = (a.rearrange("p a n -> p (a n)") for a in (
                    qm[:].rearrange("p a w e q -> p a (w e q)"), qmhl[:, 0], qmhl[:, 1]))
                for half in range(2):
                    pool.wait_ge(q_pooled, c * 4 + 2 * half + 2)
                    if not (isinstance(c, int) and c == 0):
                        pool.wait_ge(q_split, c * 3)
                        pool.wait_ge(s_done, (c - 1) * U + 1)
                    for to in (qm[:, half], qmhl[:, 0, half, :].rearrange("p (w e q) -> p w e q", w=W, e=2)):
                        last = nc.gpsimd.tensor_tensor(
                            to, qp[:, half, :].rearrange("p (w q) -> p w q", w=W).unsqueeze(2)
                            .broadcast_to([HC, W, 2, QW]),
                            hm[:].unsqueeze(1).unsqueeze(3).broadcast_to([HC, W, 2, QW]), ALU.mult)
                    last.then_inc(q_split, 1)
                pool.wait_ge(q_split, c * 3 + 2)
                nc.gpsimd.tensor_tensor(low, qm_, high.bitcast(F32), ALU.subtract).then_inc(q_split, 1)

            def factors(b):
                pool.wait_ge(consts, 7)
                pool.wait_ge(ve_done, b + 1)
                at = b * 4
                r = r1[:]
                nc.gpsimd.tensor_tensor(r1_all[:, bass.ds(b * T2, T2)], ve[:], mhalf[:], ALU.pow)
                nc.gpsimd.tensor_tensor(r, ve[:], mhalf[:], ALU.pow).then_inc(pow_step, 1)
                pool.wait_ge(pow_step, at + 1)
                nc.gpsimd.tensor_tensor(vu[:], mv[:, :, 1], r, ALU.mult).then_inc(pow_step, 1)
                pool.wait_ge(pow_step, at + 2)
                nc.gpsimd.tensor_tensor(vu[:], vu[:], r, ALU.mult).then_inc(pow_step, 1)
                pool.wait_ge(pow_step, at + 3)
                nc.gpsimd.tensor_tensor(ve2[:], vu[:], eps5[:], ALU.add).then_inc(pow_step, 1)
                pool.wait_ge(pow_step, at + 4)
                nc.gpsimd.tensor_tensor(vu[:], ve2[:], mhalf[:], ALU.pow).then_inc(r1_done, 1)
                pool.wait_ge(consts, 7)
                pool.wait_ge(r1_done, b + 1)
                nc.gpsimd.tensor_tensor(rr_all[:, bass.ds(b * T2, T2)], vu[:], r, ALU.mult).then_inc(stat_done, 1)

            def stage1(b, p):
                last = isinstance(b, int) and b == B - 1
                first = isinstance(b, int) and b == 0
                if not last:
                    split_q(b + 1)
                if not first:
                    factors(b - 1)

            pool.wait_ge(w_first, W_FIRST)
            split_q(0)
            over_batches(pool, stage1)
            factors(B - 1)

            pool.wait_ge(stat_done, B)
            pool.wait_ge(pv_done, B * U)
            nc.gpsimd.memset(yT_all[HC:HC + 1, :, :], 1.0).then_inc(consts, 1)
            pool.wait_ge(consts, 8)
            nc.gpsimd.memset(xpad[:, :, 0:4], 0.0).then_inc(fills, 1)
            pool.wait_ge(w_rest, W_REST)

            def gate(b, p):
                pool.wait_ge(y_ready, b + 1)
                if not (isinstance(b, int) and b == 0):
                    pool.wait_ge(o2_done, b)
                    pool.wait_ge(gsq_ready, b)
                nc.gpsimd.tensor_tensor(g_, y_, sz[:, p].rearrange("p c t -> p (c t)"), ALU.mult).then_inc(gt_ready, 1)

            def factors2(b):
                pool.wait_ge(ms_done, b + 1)
                nc.gpsimd.tensor_tensor(rt[:], ms[:], mhalf[:], ALU.pow).then_inc(rt_done, 1)
                pool.wait_ge(ve3_done, b + 1)
                at = b * 6
                if not (isinstance(b, int) and b == 0):
                    pool.wait_ge(yh_ready, b)
                nc.gpsimd.tensor_tensor(r1[:], ve[:], mhalf[:], ALU.pow).then_inc(pow2_step, 1)
                pool.wait_ge(pow2_step, at + 1)
                nc.gpsimd.tensor_tensor(vu[:], mv[:, :, 1], r1[:], ALU.mult).then_inc(pow2_step, 1)
                pool.wait_ge(pow2_step, at + 2)
                nc.gpsimd.tensor_tensor(vu[:], vu[:], r1[:], ALU.mult).then_inc(pow2_step, 1)
                pool.wait_ge(pow2_step, at + 3)
                nc.gpsimd.tensor_tensor(ve2[:], vu[:], eps6[:], ALU.add).then_inc(pow2_step, 1)
                pool.wait_ge(pow2_step, at + 4)
                nc.gpsimd.tensor_tensor(r2[:], ve2[:], mhalf[:], ALU.pow).then_inc(pow2_step, 1)
                pool.wait_ge(pow2_step, at + 5)
                nc.gpsimd.tensor_tensor(rr[:], r1[:], r2[:], ALU.mult).then_inc(pow2_step, 1)
                if not (isinstance(b, int) and b == 0):
                    pool.wait_ge(lg_ready, b)
                nc.gpsimd.tensor_tensor(s2[:], ve2[:], r2[:], ALU.mult).then_inc(r3_done, 1)

            def residual3(b):
                pool.wait_ge(consts, 8)
                pool.wait_ge(yh_ready, b + 1)
                where = u3_all[:, bass.ds(b * T2, T2), :]
                nc.gpsimd.tensor_tensor(where, where, h2[:], ALU.add).then_inc(h2_used, 1)

            def spread_a(b, p):
                pool.wait_ge(dt_step, b * 9 + 9)
                for t in range(T2):
                    if not (isinstance(b, int) and b == 0):
                        pool.wait_ge(seg_done, b * 3)
                    nc.gpsimd.tensor_tensor(a1[:, t], a2[:, p, t, :].unsqueeze(2).broadcast_to([128, SH, 128]),
                                            upto[:].unsqueeze(1).broadcast_to([128, SH, 128]),
                                            ALU.mult).then_inc(a1_ready, 1)

            def stage2(s, p):
                fixed = isinstance(s, int)
                if not fixed or s >= 2:
                    gate(s - 2, p)
                    factors2(s - 2)
                    residual3(s - 2)
                if not fixed or s < B:
                    spread_a(s, p)

            stage2(0, 0)
            stage2(1, 1)
            with pool.Fori(1, B // 2) as i:
                stage2(i * 2, 0)
                stage2(i * 2 + 1, 1)
            stage2(B, 0)
            stage2(B + 1, 1)
            pool.wait_ge(lg_ready, B)
            nc.gpsimd.memset(va_ones(areaV3, T2), 1.0).then_inc(vones, 1)
            pool.wait_ge(vones, 1)
            nc.gpsimd.memset(qst3[0][:].bitcast(F32), 0.0).then_inc(zeros3, 1)
            pool.wait_ge(zeros3, 1)
            nc.gpsimd.memset(qst3[1][:].bitcast(F32), 0.0).then_inc(zeros3, 1)

            def add_u3(b):
                pool.wait_ge(f_read, b * 2 + 2)
                nc.gpsimd.tensor_tensor(res2[:], res[:], u3_all[:, bass.ds(b * T2, T2), :], ALU.add).then_inc(res_ready, 1)

            def stage3(b, p):
                last = isinstance(b, int) and b == B - 1
                first = isinstance(b, int) and b == 0
                if not first:
                    pool.wait_ge(consts, 8)
                    wait_stored(b - 1, 1 - p)
                    add_u3(b - 1)

            def wait_stored(b, p):
                if isinstance(b, int) and b == 0:
                    return
                q = 1 - p
                pool.wait_ge(stored[q], (b - 1 - q) * 8 + 16)

            over_batches(pool, stage3)
            wait_stored(B - 1, 1)
            add_u3(B - 1)


def va_ones(areaV, tiles):
    return (areaV[:, :, 0:tiles * H * 32].rearrange("p a (t e) -> p a t e", e=32))[:, :, :, D:32]


def _layouts(v):
    f = np.float32

    def halves(a):
        got = np.zeros((HC + 1, 2, a.shape[1]), f)
        got[:HC, 0], got[:HC, 1] = a[:HC], a[HC:C]
        if a.shape[0] > C:
            got[HC, 1] = a[C]
        return got if a.shape[0] > C else np.ascontiguousarray(got[:HC])

    def heads(a):
        got = np.zeros((128, G3, a.shape[1]), f)
        for h in range(H):
            got[32 * (h % 4):32 * (h % 4) + D, h // 4] = a[h * D:(h + 1) * D]
        return got

    def chunks(a):
        return np.ascontiguousarray(a.reshape((-1, 128) + a.shape[1:]).swapaxes(0, 1))

    x = v["x"].reshape(B, STRIDE, QW, W, C)
    x = x.transpose(0, 4, 3, 1, 2).reshape(B, 2, HC, N).transpose(0, 2, 1, 3)
    w2 = v["L0_ffn_w2"].reshape(2, C, MLP + C).transpose(0, 2, 1)
    r, c = np.arange(128)[:, None], np.arange(128)[None, :]
    keeps = [C >> (E - 1 - e) for e in range(E)]
    inside = np.array([[ch < keeps[e % E] for ch in range(C)] for e in range(B * E)], f)
    nest = np.ones((B * E, 2 * (HC + 1) + C), f)
    nest[:, 0:HC], nest[:, HC + 1:2 * HC + 1], nest[:, 2 * HC + 2:] = inside[:, :HC], inside[:, HC:], inside
    return {
        "x": x,
        "wqkv": halves(np.concatenate([v["L0_tok_qkv_w"].T, v["L0_tok_qkv_b"][None]])),
        "wo": heads(v["L0_tok_proj_w"].T), "bo": v["L0_tok_proj_b"],
        "win": halves(v["L0_attn_W_in"]),
        "lnw": v["L0_attn_ln_w"].reshape(2, HC).T, "lnb": v["L0_attn_ln_b"].reshape(2, HC).T,
        "cw": chunks(v["L0_attn_conv_w"]), "cb": chunks(v["L0_attn_conv_b"]),
        "dtb": v["L0_attn_dt_bias"], "alog": v["L0_attn_A_log"],
        "dd": chunks(np.repeat(v["L0_attn_D"], 64)), "rms": chunks(v["L0_attn_rms_w"]),
        "wout": chunks(v["L0_attn_W_out"]), "wr": halves(v["L0_ffn_w_router"].T),
        "gam": v["L0_ffn_gamma1"].reshape(2, HC).T, "bet": v["L0_ffn_beta1"].reshape(2, HC).T,
        "w1": halves(np.concatenate([v["L0_ffn_w1"].T, v["L0_ffn_b1"][None]])),
        "w2": np.stack([np.concatenate([chunks(w[:MLP]), heads(w[MLP:])], 1) for w in w2]),
        "b2": v["L0_ffn_b2"].reshape(2, C),
        "hm": np.arange(HC)[:, None] // D % 2 == np.arange(2)[None, :],
        "later": r > c, "upto": r <= c, "eye": r == c,
        "nest": nest, "row": np.arange(B * E)[:, None] // E == np.arange(B)[None, :],
    }


def kernel(**inputs):
    import concourse.bacc as _bacc
    from concourse import mybir as _mybir
    from concourse.bass_utils import run_bass_kernel_spmd as _run

    nc = _bacc.Bacc("TRN2", target_bir_lowering=False, num_devices=1)
    laid = _layouts({k: np.asarray(a) for k, a in inputs.items()})
    arrays, args = {}, []
    for name, a in laid.items():
        a = np.ascontiguousarray(a, dtype=np.float32)
        arrays[f"in_{name}_dram"] = a
        args.append(nc.dram_tensor(f"in_{name}_dram", a.shape, _mybir.dt.float32, kind="ExternalInput").ap())
    out = nc.dram_tensor("out_dram", (B, L, C), _mybir.dt.float32, kind="ExternalOutput").ap()
    audio_tower(nc, *args, out)
    r = _run(nc, [arrays], core_ids=[0])
    return r.results[0]["out_dram"]
```

```python
from contextlib import ExitStack

import numpy as np

import concourse.bass as bass
from concourse import mybir
from concourse.alu_op_type import AluOpType as ALU

F32 = mybir.dt.float32
F32R = mybir.dt.float32r
BF16 = mybir.dt.bfloat16
ACT = mybir.ActivationFunctionType
AX = mybir.AxisListType

B = 8
N = 1024
L = 256
C = 192
HC = C // 2
H = 12
D = C // H
HH = H // 2
PAIRS = H // 2
SR = 6 * D
STRIDE = 4
W = 4
QW = 64
KW = 256
E = 4
CAP = L // 2
MLP = 4 * C
F1 = MLP + 3 * C
MJ = MLP // 128
G3 = H // 4
INNER = 2 * C
STATE = 64
SH = INNER // 64
XC = INNER // 128
ZXD = 2 * INNER + 2 * STATE + SH
U = 12
TAPS = 4
T2 = 2
SCALE = float(D) ** -0.5


def audio_tower(nc, x, wqkv_d, wo_d, bo_d, win_d, lnw_d, lnb_d, cw_d, cb_d, dtb_d, alog_d, dd_d, rms_d,
                wout_d, wr_d, gam_d, bet_d, w1_d, w2_d, b2_d, hm_d, later_d, upto_d, eye_d, nest_d,
                row_d, out):
    with ExitStack() as ctx:
        def sb(name, shape, dt=F32):
            return ctx.enter_context(nc.sbuf_tensor(name, shape, dt))

        def sb_phase(*tensors):
            with ExitStack() as phase:
                return [phase.enter_context(nc.sbuf_tensor(*t)) for t in tensors]

        def sem(name):
            return ctx.enter_context(nc.semaphore(name))

        ps = ctx.enter_context(nc.psum_tensor("ps", [128, 8, 512], F32))
        TR, SC, OB = 2, 3, 6
        TR2, SC2 = 2, 4
        psO = ps[:, OB:OB + 2, :].rearrange("p a n -> p (a n)")[:, 0:G3 * L]
        psH = ps[:, 7, 256:256 + C]
        psY = psO
        psDt = ps[:, 7, 256:256 + T2 * SH]
        psSuf = ps[:, 7, 272:272 + SH]
        psLg = ps[:, 7, 288:288 + T2 * E]

        areaX = sb("areaX", [128, 2, 2048])
        xT = [areaX[:, p, :].rearrange("p (a n) -> p a n", a=2) for p in range(2)]

        prob = sb("prob", [128, 3, 512])
        probT = sb("probT", [128, 3, 512])
        nmax = sb("nmax", [128, 4, 2])
        qp = sb("qp", [HC, 2, L])
        qhl = sb("qhl", [HC, 2, 2, L], F32R)
        otA = sb("otA", [128, G3 * L])
        rsum = sb("rsum", [128, G3 * L // 32])
        oT = sb("oT", [128, G3, L])
        h_all = sb("h_all", [128, B * T2, C])
        st6 = sb("st6", [128, T2, 6])
        mv = sb("mv", [128, T2, 2])
        mean_all = sb("mean_all", [128, B * T2])
        ve = sb("ve", [128, T2])
        vu = sb("vu", [128, T2])
        ve2 = sb("ve2", [128, T2])
        r1_all = sb("r1_all", [128, B * T2])
        rr_all = sb("rr_all", [128, B * T2])
        mhalf = sb("mhalf", [128, T2])
        eps5 = sb("eps5", [128, T2])
        eps6 = sb("eps6", [128, T2])

        wqkv = sb("wqkv", [HC + 1, 2, 3 * C])
        wo = sb("wo", [128, G3, C])
        bo = sb("bo", [128, C])
        hm = sb("hm", [HC, 2])
        eye = sb("eye", [128, 128])
        later = sb("later", [128, 128])
        upto = sb("upto", [128, 128])
        ones = sb("ones", [128, 128])
        win = sb("win", [HC, 2, ZXD])
        lnw = sb("lnw", [HC, 2])
        lnb = sb("lnb", [HC, 2])
        cw = sb("cw", [128, TAPS, TAPS])
        cb = sb("cb", [128, TAPS])
        dtb = sb("dtb", [128, SH])
        aneg = sb("aneg", [128, SH])
        dd = sb("dd", [128, XC])
        rms = sb("rms", [128, XC])
        wout = sb("wout", [128, XC, C])
        wr = sb("wr", [HC, 2, E])
        gam = sb("gam", [HC, 2])
        bet = sb("bet", [HC, 2])
        w1 = sb("w1", [HC + 1, 2, F1])
        w2 = sb("w2", [128, MJ + G3, C])
        w2x = areaX[:, 1, 0:(MJ + G3) * C].rearrange("p (j c) -> p j c", c=C)
        b2 = sb("b2", [128, C])
        b2x = sb("b2x", [128, C])
        nestf = sb("nestf", [32, 2 * (HC + 1) + C])
        nest = sb("nest", [32, 2 * (HC + 1)], BF16)
        rowm = sb("rowm", [32, B])

        small = sb("small", [128, 12, T2 * SH])
        dt2 = sb("dt2", [128, 2, T2, SH])
        a2 = sb("a2", [128, 2, T2, SH])
        esuf = sb("esuf", [128, SH])
        ms = sb("ms", [128, T2])
        rt = sb("rt", [128, T2])
        r1 = sb("r1", [128, T2])
        r2 = sb("r2", [128, T2])
        rr = sb("rr", [128, T2])
        s2 = sb("s2", [128, T2])
        lg = sb("lg", [128, T2, B, E])
        lsm = sb("lsm", [128, 4, T2 * B])
        pe_ = sb("pe_", [128, T2 * B, E])
        pr = sb("pr", [32, L])
        pick = sb("pick", [32, 2, L])
        top8 = sb("top8", [32, 8])
        sel = sb("sel", [32, L])
        gsel = sb("gsel", [32, L])
        selb = sb("selb", [32, L], BF16)
        gselb = sb("gselb", [32, 2, L])
        yhat = sb("yhat", [HC + 1, 2, L])
        y2T = [areaX[:, p, 0:MJ * L].rearrange("p (j n) -> p j n", j=MJ) for p in range(2)]
        res = sb("res", [128, T2, C])
        res2 = sb("res2", [128, T2, C])
        uu2 = res

        kst, qst0, qst1, qm, qmhl, khl, areaV1 = sb_phase(
            ("kst", [SR, PAIRS, N], F32R), ("qst0", [SR, PAIRS, 2 * L], F32R), ("qst1", [SR, PAIRS, 2 * L], F32R),
            ("qm", [HC, 2, W, 2, QW], F32), ("qmhl", [HC, 2, 2, 2 * L], F32R), ("khl", [HC, 2, 2, N], F32R), ("areaV1", [128, 2, 3072], F32))
        qst = [qst0, qst1]
        va = [areaV1[:, p, :].rearrange("p (t h e) -> p t h e", t=N // 128, e=32) for p in range(2)]
        u3_all = sb("u3_all", [128, B * T2, C])
        yT_all = sb("yT_all", [HC + 1, 2, B * L])
        areaQ, areaK, areaV, uu, xnT, bcT, h2, yhT = sb_phase(
            ("areaQ", [128, 6144], F32), ("areaK", [128, 4096], F32), ("areaV", [128, 6144], F32),
            ("uu", [128, T2, C], F32), ("xnT", [HC, 2, L], F32), ("bcT", [STATE, 2, L], F32),
            ("h2", [128, T2, C], F32), ("yhT", [HC, 2, L], F32))
        qst30, qst31, kst30, kst31, khl3, areaV3 = sb_phase(
            ("qst30", [SR, PAIRS, 2, L], F32R), ("qst31", [SR, PAIRS, 2, L], F32R),
            ("kst30", [SR, PAIRS, L], F32R), ("kst31", [SR, PAIRS, L], F32R), ("khl3", [HC, 2, 2, L], F32R),
            ("areaV3", [128, 2, T2 * H * 32], F32))
        qst3, kst3 = [qst30, qst31], [kst30, kst31]
        va3 = [areaV3[:, p, :].rearrange("p (t h e) -> p t h e", t=T2, e=32) for p in range(2)]

        def cut(area, sizes):
            got, at = [], 0
            for n in sizes:
                got.append(area[:, at:at + n])
                at += n
            return got

        qflat, kflat, vflat = areaQ[:, :], areaK[:, :], areaV[:, :]
        m_, a1_, ex0, ex1 = cut(qflat, [3 * 768, 2 * 768, 768, 768])
        mix = m_.rearrange("p (a h t) -> p a h t", a=3, h=SH)
        a1 = a1_.rearrange("p (a h t) -> p a h t", a=2, h=SH)
        dec = [ex0.rearrange("p (h t) -> p h t", h=SH), ex1.rearrange("p (h t) -> p h t", h=SH)]
        xdt_, y_, g_, gsq_, gm_ = cut(kflat, [3 * INNER, XC * L, XC * L, XC * L, 3 * 128])
        xdt = xdt_.rearrange("p (a h q) -> p a h q", a=3, h=SH)
        y2 = y_.rearrange("p (c t) -> p c t", c=XC)
        gt = g_.rearrange("p (c t) -> p c t", c=XC)
        gsq = gsq_.rearrange("p (c t) -> p c t", c=XC)
        gmask = gm_.rearrange("p (a t) -> p a t", a=3)
        xc_, sz_, xpad_, acc_, xh_ = cut(vflat, [2 * XC * L, 2 * XC * L, TAPS * (L + 4), TAPS * L, 2 * T2 * C])
        xh = xh_.rearrange("p (b t c) -> p b t c", b=2, t=T2)
        xc = xc_.rearrange("p (b c t) -> p b c t", b=2, c=XC)
        sz = sz_.rearrange("p (b c t) -> p b c t", b=2, c=XC)
        xpad = xpad_.rearrange("p (c t) -> p c t", c=TAPS)
        acc = acc_.rearrange("p (c t) -> p c t", c=TAPS)
        x_first, w_first, w_rest, w2x_loaded = sem("x_first"), sem("w_first"), sem("w_rest"), sem("w2x_loaded")
        x_loaded = [sem("x_loaded0"), sem("x_loaded1")]
        x_used = sem("x_used")
        consts = sem("consts")
        fills = sem("fills")
        vones = sem("vones")
        s_done, max_done, exp_done = sem("s_done"), sem("max_done"), sem("exp_done")
        t_done, pt_ready, pv_done = sem("t_done"), sem("pt_ready"), sem("pv_done")
        o_read, ot_sum, ot_norm, ot_ready = sem("o_read"), sem("ot_sum"), sem("ot_norm"), sem("ot_ready")
        q_done, k_done, v_done, h_done = sem("q_done"), sem("k_done"), sem("v_done"), sem("h_done")
        q_pooled, k_ready, v_ready, h_ready = sem("q_pooled"), sem("k_ready"), sem("v_ready"), sem("h_ready")
        q_split, q_low, k_split = sem("q_split"), sem("q_low"), sem("k_split")
        q_stacked = [sem("q_stacked0"), sem("q_stacked1")]
        k_stacked = [sem("k_stacked0"), sem("k_stacked1")]
        bn_done, mv_done, ve_done, r1_done = sem("bn_done"), sem("mv_done"), sem("ve_done"), sem("r1_done")
        pow_step = sem("pow_step")
        stat_done = sem("stat_done")
        alog_exp = sem("alog_exp")
        setup, w2_ready = sem("setup"), sem("w2_ready")
        xh_ready, u_done, hu_done = sem("xh_ready"), sem("u_done"), sem("hu_done")
        xt_done, xn_ready = sem("xt_done"), sem("xn_ready")
        dt_done, zx_done, zx_read = sem("dt_done"), sem("zx_done"), sem("zx_read")
        dt_step, dt_exp, dt_log, dt_ready = sem("dt_step"), sem("dt_exp"), sem("dt_log"), sem("dt_ready")
        xp_ready, conv_step, conv_done = sem("xp_ready"), sem("conv_step"), sem("conv_done")
        z_ready, xc_ready = sem("z_ready"), sem("xc_ready")
        a1_ready, tok_done, g_done, suf_done = sem("a1_ready"), sem("tok_done"), sem("g_done"), sem("suf_done")
        seg_done, dec_ready, suf_ready = sem("seg_done"), sem("dec_ready"), sem("suf_ready")
        xdt_ready, gm_ready, mix_ready = sem("xdt_ready"), sem("gm_ready"), sem("mix_ready")
        y_done, y_ready, gt_ready, gsq_ready = sem("y_done"), sem("y_ready"), sem("gt_ready"), sem("gsq_ready")
        o2_done, ms_done, rt_done, h2_ready = sem("o2_done"), sem("ms_done"), sem("rt_done"), sem("h2_ready")
        bn2_done, mv2_done, ve3_done, r3_done = sem("bn2_done"), sem("mv2_done"), sem("ve3_done"), sem("r3_done")
        h2_used = sem("h2_used")
        pow2_step, yh_ready, u3_ready = sem("pow2_step"), sem("yh_ready"), sem("u3_ready")
        yt_done, yhT_ready, yT_ready = sem("yt_done"), sem("yhT_ready"), sem("yT_ready")
        lg_done, lg_ready = sem("lg_done"), sem("lg_ready")
        ch_step, ch_exp, pr_done = sem("ch_step"), sem("ch_exp"), sem("pr_done")
        gates_ready, sel_ready = sem("gates_ready"), sem("sel_ready")
        selb_ready, m_done, yhat_ready = sem("selb_ready"), sem("m_done"), sem("yhat_ready")
        q3_done, k3_done, v3_done, m3_done = sem("q3_done"), sem("k3_done"), sem("v3_done"), sem("m3_done")
        q3_ready, k3_ready, v3_ready, m3_read = sem("q3_ready"), sem("k3_ready"), sem("v3_ready"), sem("m3_read")
        gelu_done, q3_split, k3_split = sem("gelu_done"), sem("q3_split"), sem("k3_split")
        zeros3 = sem("zeros3")
        qk3_stacked = [sem("qk3_stacked0"), sem("qk3_stacked1")]
        first3 = [sem(f"first3_{j}") for j in range(PAIRS // 2)]
        f_done, f_read, res_step, res_ready = sem("f_done"), sem("f_read"), sem("res_step"), sem("res_ready")
        stored = [sem("stored0"), sem("stored1")]

        block = ctx.enter_context(nc.Block())

        def over_batches(eng, stage):
            stage(0, 0)
            with eng.Fori(0, B // 2 - 1) as i:
                stage(i * 2 + 1, 1)
                stage(i * 2 + 2, 0)
            stage(B - 1, 1)

        def over_stages2(eng, stage):
            for s in range(3):
                stage(s, s % 2)
            with eng.Fori(0, (B - 4) // 2) as i:
                stage(i * 2 + 3, 1)
                stage(i * 2 + 4, 0)
            for s in range(B - 1, B + 3):
                stage(s, s % 2)

        def parts2(s):
            if not isinstance(s, int):
                return (True,) * 5
            return s < B, s + 1 < B, 0 <= s - 1 < B, 0 <= s - 2 < B, 0 <= s - 3 < B

        def tile(b, t):
            return bass.ds(b * T2 + t, 1)

        @block.sync
        def _(sp):
            sp.dma_start(xT[0][0:HC, :, 0:N // 2], x[0][:, :, 0:N // 2]).then_inc(x_first, 16)
            sp.dma_start(wqkv[:, :, 0:C], wqkv_d[:, :, 0:C]).then_inc(x_first, 16)
            sp.dma_start(xT[0][0:HC, :, N // 2:N], x[0][:, :, N // 2:N]).then_inc(x_loaded[0], 16)
            sp.dma_start(wqkv[:, :, C:2 * C], wqkv_d[:, :, C:2 * C]).then_inc(w_first, 16)
            sp.dma_start(wqkv[:, :, 2 * C:3 * C], wqkv_d[:, :, 2 * C:3 * C]).then_inc(w_first, 16)
            sp.dma_start(hm[:], hm_d).then_inc(w_first, 16)
            sp.dma_start(eye[:], eye_d).then_inc(w_first, 16)
            sp.dma_start(wo[:], wo_d).then_inc(w_first, 16)
            sp.dma_start(bo[:], bo_d.rearrange("(a n) -> a n", a=1).broadcast_to([128, C])).then_inc(w_first, 16)
            sp.dma_start(xT[1][0:HC], x[1]).then_inc(x_loaded[1], 16)
            for dst, src in ((win, win_d), (lnw, lnw_d), (lnb, lnb_d), (cw, cw_d), (cb, cb_d), (dd, dd_d),
                             (rms, rms_d), (wout, wout_d), (wr, wr_d), (gam, gam_d), (bet, bet_d),
                             (w1, w1_d), (w2, w2_d[0]), (nestf, nest_d), (rowm, row_d), (later, later_d),
                             (upto, upto_d)):
                sp.dma_start(dst[:], src).then_inc(w_rest, 16)
            for dst, src in ((dtb, dtb_d), (aneg, alog_d), (b2, b2_d[0]), (b2x, b2_d[1])):
                n = dst.shape[1]
                sp.dma_start(dst[:], src.rearrange("(a n) -> a n", a=1).broadcast_to([128, n])).then_inc(w_rest, 16)

            def stack_q(c, p):
                sp.wait_ge(q_split, c * 3 + 3)
                for r, part in enumerate((0, 1, 0)):
                    for pair in range(PAIRS // 2):
                        sp.dma_start(qst[p][32 * r:32 * r + 32, pair:PAIRS:PAIRS // 2, :].bitcast(F32),
                                     qmhl[32 * pair:32 * pair + 32, part].bitcast(F32)).then_inc(q_stacked[p], 16)

            def stack_k(c, tb):
                if tb == 0 or isinstance(c, int) and c == 0:
                    sp.wait_ge(k_split, c * 4 + 2 * tb + 2)
                else:
                    sp.wait_ge(s_done, c * U + 1)
                for r, part in enumerate((0, 0, 1)):
                    for pair in range(PAIRS // 2):
                        sp.dma_start(kst[32 * r:32 * r + 32, pair:PAIRS:PAIRS // 2, tb * 512:(tb + 1) * 512].bitcast(F32),
                                     khl[32 * pair:32 * pair + 32, part, :, tb * 512:(tb + 1) * 512].bitcast(F32)
                                     ).then_inc(k_stacked[tb], 16)

            def load_x(c, p):
                sp.wait_ge(x_used, c - 1)
                sp.dma_start(xT[p][0:HC], x[bass.ds(c, 1)].rearrange("b p a n -> p (b a) n")).then_inc(x_loaded[p], 16)

            def stage1(b, p):
                stack_q(b + 1, 1 - p)
                stack_k(b + 1, 0)
                if not isinstance(b, int) or b + 3 < B:
                    load_x(b + 3, 1 - p)
                stack_k(b + 1, 1)

            sp.wait_ge(consts, 7)
            stack_q(0, 0)
            stack_k(0, 0)
            load_x(2, 0)
            stack_k(0, 1)
            stage1(0, 0)
            with sp.Fori(0, B // 2 - 2) as i:
                stage1(i * 2 + 1, 1)
                stage1(i * 2 + 2, 0)
            stage1(B - 3, 1)
            stage1(B - 2, 0)
            sp.wait_ge(x_used, B)
            sp.dma_start(w2x, w2_d[1]).then_inc(w2x_loaded, 16)

            def store(b, p):
                sp.wait_ge(res_ready, b + 1)
                sp.dma_start(out[bass.ds(b, 1)].rearrange("b (t p) c -> p (b t) c", p=128), res2[:]).then_inc(stored[p], 16)

            def stack3_q(c, p, pair, signal):
                for r, part in enumerate((0, 1, 0)):
                    for e in range(2):
                        h = 2 * pair + e
                        sp.dma_start(qst3[p][32 * r + D * e:32 * r + D * (e + 1), pair:PAIRS:PAIRS // 2, e, :].bitcast(F32),
                                     qhl[D * h:D * (h + 1), part].bitcast(F32)).then_inc(signal, 16)

            def stack3_k(c, p, pair, signal):
                for r, part in enumerate((0, 0, 1)):
                    sp.dma_start(kst3[p][32 * r:32 * r + 32, pair:PAIRS:PAIRS // 2, :].bitcast(F32),
                                 khl3[32 * pair:32 * pair + 32, part].bitcast(F32)).then_inc(signal, 16)

            def stack3(c, p):
                sp.wait_ge(q3_split, c + 1)
                for pair in range(PAIRS // 2):
                    stack3_q(c, p, pair, qk3_stacked[p])
                sp.wait_ge(k3_split, c + 1)
                for pair in range(PAIRS // 2):
                    stack3_k(c, p, pair, qk3_stacked[p])

            def stage3(b, p):
                stack3(b + 1, 1 - p)
                if not (isinstance(b, int) and b == 0):
                    store(b - 1, 1 - p)

            sp.wait_ge(zeros3, 2)
            sp.wait_ge(q3_split, 1)
            for pair in range(PAIRS // 2):
                stack3_q(0, 0, pair, first3[pair])
                if pair == 0:
                    sp.wait_ge(k3_split, 1)
                stack3_k(0, 0, pair, first3[pair])
            stage3(0, 0)
            with sp.Fori(0, B // 2 - 1) as i:
                stage3(i * 2 + 1, 1)
                stage3(i * 2 + 2, 0)
            store(B - 2, 0)
            store(B - 1, 1)
            for p in range(2):
                sp.wait_ge(stored[p], 16 * (B // 2))
        W_FIRST, W_REST = 16 * 6, 16 * 21
        K_BANKS = (0, 1, 0, 1)
        QD, KD, QD3 = 3 * PAIRS // 2, 3 * PAIRS // 2, 3 * HH

        @block.tensor
        def _(pe):
            def unit_scores1(c_par, u):
                w, r = divmod(u, 3)
                for i in range(2):
                    last = nc.tensor.matmul(
                        ps[:, SC + u % 3, i * 256:(i + 1) * 256],
                        qst[c_par][:, 2 * r + i, w * 2 * QW:(w + 1) * 2 * QW],
                        kst[:, 2 * r + i, w * KW:(w + 1) * KW], start=True, stop=True)
                last.then_inc(s_done, 1)

            def unit_scores3(c_par, u):
                pair, e = divmod(u, 2)
                for i in range(2):
                    last = nc.tensor.matmul(
                        ps[:, SC + u % 3, i * 256:(i + 1) * 256],
                        qst3[c_par][:, pair, e, i * 128:(i + 1) * 128],
                        kst3[c_par][:, pair, :], start=True, stop=True)
                last.then_inc(s_done, 1)

            def unit_turn(u):
                for kc in range(2):
                    for i in range(2):
                        last = nc.tensor.transpose(
                            ps[:, TR, kc * 256 + i * 128:kc * 256 + (i + 1) * 128],
                            prob[:, u % 3, i * 256 + kc * 128:i * 256 + (kc + 1) * 128], eye[:])
                last.then_inc(t_done, 1)

            def unit_pv1(p, u):
                w, r = divmod(u, 3)
                for kc in range(2):
                    for j in range(4):
                        last = nc.tensor.matmul(
                            psO[32 * j:32 * j + 32, r * L + w * QW:r * L + (w + 1) * QW],
                            va[p][:, 2 * w + kc, 4 * r + j, :],
                            probT[:, u % 3, kc * 256 + j * QW:kc * 256 + (j + 1) * QW],
                            start=(kc == 0), stop=(kc == 1), tile_position=(0, 32 * j))
                last.then_inc(pv_done, 1)

            def unit_pv3(p, u):
                g, j = divmod(u, 4)
                for kc in range(2):
                    last = nc.tensor.matmul(
                        psO[32 * j:32 * j + 32, g * L:(g + 1) * L], va3[p][:, kc, u, :],
                        probT[:, u % 3, kc * 256:(kc + 1) * 256],
                        start=(kc == 0), stop=(kc == 1), tile_position=(0, 32 * j))
                last.then_inc(pv_done, 1)

            def q_piece(p, k, bank):
                half, tb = divmod(k, 2)
                for a in range(2):
                    last = nc.tensor.matmul(ps[0:HC, bank, :], wqkv[0:HC + a, a, half * HC:(half + 1) * HC],
                                            xT[p][0:HC + a, a, tb * 512:(tb + 1) * 512],
                                            start=(a == 0), stop=(a == 1))
                last.then_inc(q_done, 1)

            def k_piece(p, k, bank):
                tb, half = divmod(k, 2)
                for a in range(2):
                    last = nc.tensor.matmul(ps[0:HC, bank, :], wqkv[0:HC + a, a, C + half * HC:C + (half + 1) * HC],
                                            xT[p][0:HC + a, a, tb * 512:(tb + 1) * 512],
                                            start=(a == 0), stop=(a == 1))
                last.then_inc(k_done, 1)

            def v_piece(p, k, bank):
                for i in range(2):
                    t = 2 * k + i
                    for a in range(2):
                        last = nc.tensor.matmul(ps[:, bank, i * C:(i + 1) * C],
                                                xT[p][0:HC + a, a, t * 128:(t + 1) * 128],
                                                wqkv[0:HC + a, a, 2 * C:3 * C],
                                                start=(a == 0), stop=(a == 1))
                last.then_inc(v_done, 1)
                return last

            def h_piece(t):
                for g in range(G3):
                    last = nc.tensor.matmul(psH, oT[:, g, t * 128:(t + 1) * 128], wo[:, g, :],
                                            start=(g == 0), stop=(g == G3 - 1))
                last.then_inc(h_done, 1)

            def project(c, p, k, first):
                if k == (1 if first else 0):
                    pe.wait_ge(x_loaded[p], (c // 2 + 1) * 16 if isinstance(c, int) else (c - p) * 8 + 16)
                if k < 2:
                    if not first:
                        pe.wait_ge(v_ready, c * 4 - 1 + k)
                elif k < 6:
                    pe.wait_ge(q_pooled, c * 4 + k - 1)
                elif k < 10:
                    pe.wait_ge(k_split, c * 4 + k - 5)
                else:
                    pe.wait_ge(v_ready, c * 4 + k - 9)
                if k < 4:
                    q_piece(p, k, k % 2)
                elif k < 8:
                    k_piece(p, k - 4, k % 2)
                else:
                    v_piece(p, k - 8, k % 2)
                if k == 11:
                    pe.wait_ge(v_done, c * 4 + 4)
                    pe.sem_inc(x_used, 1)

            def output1(b, t):
                if t == 0:
                    pe.wait_ge(ot_ready, b + 1)
                else:
                    pe.wait_ge(h_ready, b * 2 + 1)
                h_piece(t)

            def wait_q(c, p):
                pe.wait_ge(q_stacked[p], (c // 2 + 1) * 16 * QD if isinstance(c, int) else (c - p) * 8 * QD + 16 * QD)

            def stage1(b, p):
                last = isinstance(b, int) and b == B - 1
                first = isinstance(b, int) and b == 0
                for u in range(U):
                    if u < U - 2:
                        if not (first and u == 0):
                            pe.wait_ge(exp_done, b * U + u)
                        if u + 2 == U // 2:
                            pe.wait_ge(k_stacked[1], (b + 1) * 16 * KD)
                        unit_scores1(p, u + 2)
                    elif not last:
                        pe.wait_ge(exp_done, b * U + u)
                        if u == U - 2:
                            wait_q(b + 1, 1 - p)
                            pe.wait_ge(k_stacked[0], (b + 2) * 16 * KD)
                        unit_scores1(1 - p, u + 2 - U)
                    if not last:
                        project(b + 1, 1 - p, u, False)
                    pe.wait_ge(exp_done, b * U + u + 1)
                    if not (first and u == 0):
                        pe.wait_ge(pt_ready, b * U + u)
                    unit_turn(u)
                    if u == 0:
                        if not first:
                            unit_pv1(1 - p, U - 1)
                    else:
                        if u == 1:
                            pe.wait_ge(v_ready, b * 4 + 4)
                            if not first:
                                pe.wait_ge(o_read, b)
                        if u in (6, 9) and not first:
                            pe.wait_ge(h_ready, (b - 1) * 2 + u // 3 - 1)
                        unit_pv1(p, u - 1)
                    if u in (4, 7) and not first:
                        output1(b - 1, u // 7)

            pe.wait_ge(x_first, 32)
            pe.wait_ge(consts, 3)
            for k in range(U):
                if k == 4:
                    pe.wait_ge(w_first, W_FIRST)
                project(0, 0, k, True)
            wait_q(0, 0)
            pe.wait_ge(k_stacked[0], 16 * KD)
            unit_scores1(0, 0)
            unit_scores1(0, 1)
            over_batches(pe, stage1)
            pe.wait_ge(pt_ready, B * U)
            unit_pv1(1, U - 1)

            B2, B3 = TR2, TR2 + 1

            def turn_x(b, p):
                pe.wait_ge(xh_ready, b + 1)
                if not (isinstance(b, int) and b < 4):
                    pe.wait_ge(yhT_ready, b - 3)
                for half in range(2):
                    for t in range(T2):
                        last = nc.tensor.transpose(ps[0:HC, B2, half * L + t * 128:half * L + (t + 1) * 128],
                                                   xh[:, p, t, half * HC:(half + 1) * HC], eye[:])
                last.then_inc(xt_done, 1)

            def project_dt(b):
                if isinstance(b, int) and b == 0:
                    pe.wait_ge(h_ready, 2 * B)
                if not (isinstance(b, int) and b < 2):
                    pe.wait_ge(y_ready, b - 1)
                for t in range(T2):
                    for half in range(2):
                        last = nc.tensor.matmul(psDt[:, t * SH:(t + 1) * SH], xnT[:, half, t * 128:(t + 1) * 128],
                                                win[:, half, ZXD - SH:ZXD], start=(half == 0), stop=(half == 1))
                last.then_inc(dt_done, 1)

            def project_zx(b, k):
                if k == 0:
                    pe.wait_ge(xn_ready, b * 2 + 2)
                if not (isinstance(b, int) and b == 0 and k < 2):
                    pe.wait_ge(zx_read, b * 4 + k - 1)
                for i in range(2 if k < 3 else 1):
                    j = (XC + 2 * k + i) % (XC + TAPS)
                    for half in range(2):
                        last = nc.tensor.matmul(ps[:, k % 2, i * L:(i + 1) * L],
                                                win[:, half, j * 128:(j + 1) * 128], xnT[:, half, :],
                                                start=(half == 0), stop=(half == 1))
                last.then_inc(zx_done, 1)

            def turn_tok(b, p, t):
                for c in range(XC):
                    last = nc.tensor.transpose(ps[:, B3, c * 128:(c + 1) * 128],
                                               xc[:, p, c, t * 128:(t + 1) * 128], eye[:])
                last.then_inc(tok_done, 1)

            def decay(lhs, tile_):
                for i in range(2):
                    last = nc.tensor.matmul(ps[:, SC2 + i, 0:384], lhs,
                                            a1[:, tile_, 3 * i:3 * i + 3, :].rearrange("p h t -> p (h t)"),
                                            start=True, stop=True)
                last.then_inc(seg_done, 1)

            def mid_first(b, p):
                pe.wait_ge(xc_ready, b + 1)
                if not (isinstance(b, int) and b < 2):
                    pe.wait_ge(h2_ready, b - 1)
                turn_tok(b, p, 0)
                pe.wait_ge(a1_ready, b * 2 + 2)
                if not (isinstance(b, int) and b == 0):
                    pe.wait_ge(dec_ready, b * 3)
                decay(later[:], 0)
                if not (isinstance(b, int) and b == B - 1):
                    pe.wait_ge(dt_step, b * 9 + 10)
                elif b:
                    pe.wait_ge(y_ready, b)
                nc.tensor.matmul(psSuf, later[:], a2[:, p, 0, :], start=True, stop=True).then_inc(suf_done, 1)
                pe.wait_ge(xdt_ready, b * 3 + 1)
                turn_tok(b, p, 1)

            def mid_last(b):
                pe.wait_ge(dec_ready, b * 3 + 1)
                decay(later[:], 1)
                pe.wait_ge(xdt_ready, b * 3 + 2)
                nc.tensor.matmul(ps[:, B3, 0:256], bcT[:, 0, 0:128], bcT[:, 1, :], start=True, stop=True)
                nc.tensor.matmul(ps[:, B3, 256:384], bcT[:, 0, 128:256], bcT[:, 1, 128:256],
                                 start=True, stop=True).then_inc(g_done, 1)
                pe.wait_ge(dec_ready, b * 3 + 2)
                decay(ones[:], 1)

            def mix_y(b):
                pe.wait_ge(mix_ready, b * 3 + 3)
                if not (isinstance(b, int) and b == 0):
                    pe.wait_ge(y_ready, b)
                if not (isinstance(b, int) and b < 2):
                    pe.wait_ge(lg_ready, b - 1)
                for hp in range(XC):
                    for i in range(2):
                        h = 2 * hp + i
                        o = psY[64 * i:64 * i + 64, hp * L:(hp + 1) * L]
                        nc.tensor.matmul(o[:, 0:128], xdt[:, 0, h, :], mix[:, 0, h, :], start=True, stop=True,
                                         tile_position=(0, 64 * i))
                        nc.tensor.matmul(o[:, 128:256], xdt[:, 1, h, :], mix[:, 2, h, :], start=True, stop=False,
                                         tile_position=(0, 64 * i))
                        last = nc.tensor.matmul(o[:, 128:256], xdt[:, 2, h, :], mix[:, 1, h, :], start=False,
                                                stop=True, tile_position=(0, 64 * i))
                last.then_inc(y_done, 1)

            def output2(b):
                pe.wait_ge(gsq_ready, b + 1)
                pe.wait_ge(gm_ready, B if isinstance(b, int) and b == B - 1 else b + 2)
                for t in range(T2):
                    for c in range(XC):
                        nc.tensor.matmul(ps[:, B3, t * C:(t + 1) * C], gt[:, c, t * 128:(t + 1) * 128],
                                         wout[:, c, :], start=(c == 0), stop=(c == XC - 1))
                    for c in range(XC):
                        last = nc.tensor.matmul(ps[:, B3, 2 * C + t:2 * C + t + 1], gsq[:, c, t * 128:(t + 1) * 128],
                                                ones[:, 0:1], start=(c == 0), stop=(c == XC - 1))
                last.then_inc(o2_done, 1)

            def turn_y(b):
                pe.wait_ge(yh_ready, b + 1)
                for half in range(2):
                    for t in range(T2):
                        last = nc.tensor.transpose(ps[0:HC, B2, half * L + t * 128:half * L + (t + 1) * 128],
                                                   uu[:, t, half * HC:(half + 1) * HC], eye[:])
                last.then_inc(yt_done, 1)

            def route(b):
                pe.wait_ge(suf_ready, b + 3 if not isinstance(b, int) or b + 3 < B else B)
                pe.wait_ge(yhT_ready, b + 1)
                for t in range(T2):
                    for half in range(2):
                        last = nc.tensor.matmul(psLg[:, t * E:(t + 1) * E], yhT[:, half, t * 128:(t + 1) * 128],
                                                wr[:, half, :], start=(half == 0), stop=(half == 1))
                last.then_inc(lg_done, 1)

            def stage2(s, p):
                project, next_x, mixing, output, routing = parts2(s)
                if project:
                    project_zx(s, 0)
                    project_zx(s, 1)
                    project_dt(s)
                    project_zx(s, 2)
                if mixing:
                    mid_first(s - 1, 1 - p)
                if routing:
                    turn_y(s - 3)
                if project:
                    project_zx(s, 3)
                if mixing:
                    mid_last(s - 1)
                if routing:
                    route(s - 3)
                if next_x:
                    turn_x(s + 1, 1 - p)
                if output:
                    output2(s - 2)
                if mixing:
                    mix_y(s - 1)

            pe.wait_ge(w_rest, W_REST)
            turn_x(0, 0)
            output1(B - 1, 0)
            output1(B - 1, 1)
            over_stages2(pe, stage2)

            pe.wait_ge(ch_step, 6)
            for t in range(T2):
                last = nc.tensor.transpose(ps[0:32, 0, t * 128:(t + 1) * 128],
                                           pe_[:, t * B:(t + 1) * B, :].rearrange("p b e -> p (b e)"), eye[:])
            last.then_inc(pr_done, 1)

            def project3(c, k, bank, p):
                first = isinstance(c, int) and c == 0
                if k == 0:
                    pe.wait_ge(selb_ready, c + 1)
                    if not first:
                        pe.wait_ge(m3_read, c * 3 - 1)
                    for half in range(2):
                        last = nc.tensor.matmul(ps[0:HC + 1, bank, half * L:(half + 1) * L],
                                                nest[:, half * (HC + 1):(half + 1) * (HC + 1)], selb[:],
                                                start=True, stop=True)
                    last.then_inc(m_done, 1)
                elif k in (1, 2):
                    pe.wait_ge(yhat_ready, c + 1)
                    if k == 1 and not first:
                        pe.wait_ge(m3_read, c * 3)
                    at = MLP + (k - 1) * C
                    for half in range(2):
                        for a in range(2):
                            last = nc.tensor.matmul(ps[0:HC, bank, half * L:(half + 1) * L],
                                                    w1[0:HC + a, a, at + half * HC:at + (half + 1) * HC],
                                                    yhat[0:HC + a, a, :], start=(a == 0), stop=(a == 1))
                    last.then_inc(q3_done if k == 1 else k3_done, 1)
                elif k == 3:
                    pe.wait_ge(q3_split, c + 1)
                    for t in range(T2):
                        for a in range(2):
                            last = nc.tensor.matmul(ps[:, bank, t * C:(t + 1) * C],
                                                    yhat[0:HC + a, a, t * 128:(t + 1) * 128],
                                                    w1[0:HC + a, a, MLP + 2 * C:MLP + 3 * C],
                                                    start=(a == 0), stop=(a == 1))
                    last.then_inc(v3_done, 1)
                else:
                    j = k - 4
                    if j == 0:
                        pe.wait_ge(v3_ready, c + 1)
                    if j == 1:
                        pe.wait_ge(k3_split, c + 1)
                        if not (isinstance(c, int) and c < 2):
                            pe.wait_ge(f_read, c * 2 - 2)
                    if j == 2:
                        pe.wait_ge(m3_read, c * 3 + 1)
                    for i in range(2):
                        m = 2 * j + i
                        for a in range(2):
                            last = nc.tensor.matmul(ps[:, bank, i * L:(i + 1) * L],
                                                    w1[0:HC + a, a, m * 128:(m + 1) * 128], yhat[0:HC + a, a, :],
                                                    start=(a == 0), stop=(a == 1))
                    last.then_inc(m3_done, 1)

            def output3(b, p, t, part):
                if part == 1:
                    for j in range(MJ - 2, MJ):
                        nc.tensor.matmul(ps[:, 0, 0:C], y2T[p][:, j, t * 128:(t + 1) * 128], w2[:, j, :],
                                         start=False, stop=False)
                    for g in range(G3):
                        nc.tensor.matmul(ps[:, 0, 0:C], oT[:, g, t * 128:(t + 1) * 128], w2[:, MJ + g, :],
                                         start=False, stop=(g == G3 - 1))
                    nc.tensor.matmul(ps[:, 0, C:2 * C], gselb[:, p, t * 128:(t + 1) * 128],
                                     nestf[:, 2 * (HC + 1):2 * (HC + 1) + C], start=True,
                                     stop=True).then_inc(f_done, 1)
                    return
                if t == 0:
                    if not (isinstance(b, int) and b + 2 >= B):
                        pe.wait_ge(k3_split, b + 3)
                    pe.wait_ge(ot_ready, B + b + 1)
                    pe.wait_ge(gelu_done, b + 1)
                    pe.wait_ge(gates_ready, b + 1)
                else:
                    pe.wait_ge(f_read, b * 2 + 1)
                for j in range(MJ - 2):
                    nc.tensor.matmul(ps[:, 0, 0:C], y2T[p][:, j, t * 128:(t + 1) * 128], w2[:, j, :],
                                     start=(j == 0), stop=False)

            PIECES = {0: (0, 0), 1: (1, 1), 2: (2, 0), 3: (3, 1), 8: (4, 1), 9: (5, 0), 10: (6, 1)}

            def wait_qk3(c, p):
                each = 16 * (QD3 + KD)
                pe.wait_ge(qk3_stacked[p], (c + p) * (each // 2))

            def stage3(b, p):
                last = isinstance(b, int) and b == B - 1
                first = isinstance(b, int) and b == 0
                n0 = B * U + b * U
                for u in range(U):
                    pe.wait_ge(exp_done, n0 + u)
                    if u < U - 2:
                        if first and u in (0, 2):
                            pe.wait_ge(first3[(u + 2) // 2], 16 * 9)
                        unit_scores3(p, u + 2)
                    elif not last:
                        if u == U - 2:
                            wait_qk3(b + 1, 1 - p)
                        unit_scores3(1 - p, u + 2 - U)
                    if not last and u in PIECES:
                        project3(b + 1, *PIECES[u], 1 - p)
                    pe.wait_ge(exp_done, n0 + u + 1)
                    pe.wait_ge(pt_ready, n0 + u)
                    unit_turn(u)
                    if u == 0:
                        if not first:
                            unit_pv3(1 - p, U - 1)
                    else:
                        if u == 1:
                            pe.wait_ge(v3_ready, b + 1)
                            pe.wait_ge(vones, 1)
                            pe.wait_ge(o_read, B + b)
                        unit_pv3(p, u - 1)
                    if u in (4, 5, 6, 7) and not first:
                        output3(b - 1, 1 - p, *divmod(u - 4, 2))

            pe.wait_ge(w2_ready, 3)
            for k, bank in PIECES.values():
                project3(0, k, bank, 0)
            pe.wait_ge(first3[0], 16 * 9)
            unit_scores3(0, 0)
            unit_scores3(0, 1)
            over_batches(pe, stage3)
            pe.wait_ge(pt_ready, 2 * B * U)
            unit_pv3(1, U - 1)
            for t in range(T2):
                for part in range(2):
                    output3(B - 1, 1, t, part)

        @block.vector
        def _(dve):
            def unit_max(n, slot):
                dve.wait_ge(s_done, n + 1)
                if not isinstance(n, int) or n >= 4:
                    dve.wait_ge(exp_done, n - 3)
                nc.vector.tensor_reduce(nmax[:, slot % 4, :],
                                        ps[:, SC + slot % 3, :].rearrange("p (a n) -> p a n", a=2),
                                        AX.X, ALU.max, negate=True).then_inc(max_done, 1)

            def unit_copy(n, u):
                dve.wait_ge(t_done, n + 1)
                if not isinstance(n, int) or n >= 3:
                    dve.wait_ge(pv_done, n - 2)
                nc.vector.tensor_copy(probT[:, u % 3, :], ps[:, TR, :]).then_inc(pt_ready, 1)

            def normalise(b, tokens_inner):
                dve.wait_ge(pv_done, b * U + U)
                nc.vector.transpose(otA[:], psO).then_inc(o_read, 1)
                dve.wait_ge(o_read, b + 1)
                blocks = otA[:].rearrange("p (k e) -> p k e", e=32)
                nc.vector.reciprocal(rsum[:], blocks[:, :, D]).then_inc(ot_sum, 1)
                dve.wait_ge(ot_sum, b + 1)
                nc.vector.tensor_tensor(blocks[:, :, 0:D], blocks[:, :, 0:D],
                                        rsum[:].unsqueeze(2).broadcast_to([128, G3 * L // 32, D]),
                                        ALU.mult).then_inc(ot_norm, 1)
                dve.wait_ge(ot_norm, b + 1)
                if tokens_inner:
                    nc.vector.transpose(oT[:].rearrange("p g n -> p (g n)"), otA[:]).then_inc(ot_ready, 1)
                else:
                    for g in range(G3):
                        last = nc.vector.transpose(
                            oT[:, g, :].rearrange("p (q w) -> p w q", w=W),
                            otA[:, g * L:(g + 1) * L].rearrange("p (w q) -> p w q", w=W))
                    last.then_inc(ot_ready, 1)

            def pool_q(c, k, bank):
                half, tb = divmod(k, 2)
                dve.wait_ge(q_done, c * 4 + k + 1)
                if not (isinstance(c, int) and c == 0):
                    dve.wait_ge(q_split, c * 3)
                nc.vector.tensor_reduce(
                    qp[:, half, tb * 128:(tb + 1) * 128].rearrange("p (w j) -> p w j", w=2),
                    ps[0:HC, bank, :].rearrange("p (w s j) -> p w j s", w=2, s=STRIDE),
                    AX.X, ALU.max).then_inc(q_pooled, 1)

            def low_k(c, k, bank):
                tb, half = divmod(k, 2)
                dve.wait_ge(k_ready, c * 4 + k + 1)
                where = slice(tb * 512, (tb + 1) * 512)
                nc.vector.scalar_tensor_tensor(khl[:, 1, half, where], ps[0:HC, bank, :], SCALE,
                                               khl[:, 0, half, where].bitcast(F32), ALU.mult,
                                               ALU.subtract).then_inc(k_split, 1)

            def take_h(b, t):
                dve.wait_ge(h_done, b * 2 + t + 1)
                nc.vector.tensor_tensor(h_all[:, tile(b, t), :].rearrange("p a c -> p (a c)"), psH, bo[:],
                                        ALU.add).then_inc(h_ready, 1)

            def stats1(b):
                dve.wait_ge(consts, 1)
                dve.wait_ge(h_ready, b * 2 + 2)
                for t in range(T2):
                    last = nc.vector.bn_stats(st6[:, t, :], h_all[:, tile(b, t), :].rearrange("p a c -> p (a c)"))
                last.then_inc(bn_done, 1)
                dve.wait_ge(consts, 1)
                dve.wait_ge(bn_done, b + 1)
                if not (isinstance(b, int) and b == 0):
                    dve.wait_ge(stat_done, b)
                for t in range(T2):
                    last = nc.vector.bn_aggr(mv[:, t, :], st6[:, t, :])
                last.then_inc(mv_done, 1)
                dve.wait_ge(mv_done, b + 1)
                nc.vector.tensor_copy(mean_all[:, bass.ds(b * T2, T2)], mv[:, :, 0])
                nc.vector.tensor_scalar(ve[:], mv[:, :, 1], 1e-5, None, ALU.add).then_inc(ve_done, 1)

            def stage1(b, p):
                last = isinstance(b, int) and b == B - 1
                first = isinstance(b, int) and b == 0
                for u in range(U):
                    if u == 1 and not first:
                        normalise(b - 1, False)
                    if u < U - 2 or not last:
                        unit_max(b * U + u + 2, u + 2)
                    if u < 4 and not last:
                        pool_q(b + 1, u, u % 2)
                    unit_copy(b * U + u, u)
                    if 4 <= u < 8 and not last:
                        low_k(b + 1, u - 4, K_BANKS[u - 4])
                    if u in (4, 7) and not first:
                        take_h(b - 1, u // 7)
                    if u == 8 and not first:
                        stats1(b - 1)
                    if u == U - 1 and last:
                        dve.wait_ge(w2x_loaded, 16)
                        nc.vector.tensor_tensor(w2[:], w2[:], w2x, ALU.add).then_inc(w2_ready, 1)

            for k in range(4):
                pool_q(0, k, k % 2)
            for k in range(4):
                low_k(0, k, K_BANKS[k])
            unit_max(0, 0)
            unit_max(1, 1)
            over_batches(dve, stage1)
            def normal_x(b, p):
                dve.wait_ge(stat_done, b + 1)
                if not (isinstance(b, int) and b == 0):
                    dve.wait_ge(hu_done, b)
                for t in range(T2):
                    h = h_all[:, tile(b, t), :].rearrange("p a c -> p (a c)")
                    nc.vector.tensor_scalar(uu2[:, t, :], h, mean_all[:, tile(b, t)], r1_all[:, tile(b, t)],
                                            ALU.subtract, ALU.mult).then_inc(u_done, 1)
                    last = nc.vector.tensor_scalar(xh[:, p, t, :], h, mean_all[:, tile(b, t)], rr_all[:, tile(b, t)],
                                                   ALU.subtract, ALU.mult)
                last.then_inc(xh_ready, 1)

            k = [small[:, i, :] for i in range(9)]

            def step_sizes_v(b):
                v3 = small[:, 0, :].rearrange("p (t h) -> p t h", t=T2)
                dve.wait_ge(dt_done, b + 1)
                nc.vector.tensor_tensor(v3, psDt.rearrange("p (t h) -> p t h", t=T2),
                                        dtb[:].unsqueeze(1).broadcast_to([128, T2, SH]), ALU.add).then_inc(dt_step, 1)
                dve.wait_ge(dt_step, b * 9 + 1)
                nc.vector.scalar_tensor_tensor(k[1], k[0], -1.0, k[0], ALU.mult, ALU.max).then_inc(dt_step, 1)

            def step_sizes_e(b):
                at = b * 9
                dve.wait_ge(dt_exp, b + 1)
                nc.vector.tensor_scalar(k[3], k[2], 1.0, None, ALU.add).then_inc(dt_step, 1)
                dve.wait_ge(dt_step, at + 3)
                nc.vector.scalar_tensor_tensor(k[5], k[3], -1.0, k[2], ALU.add, ALU.subtract).then_inc(dt_step, 1)
                nc.vector.reciprocal(k[6], k[3]).then_inc(dt_step, 1)
                dve.wait_ge(dt_step, at + 5)
                nc.vector.tensor_tensor(k[7], k[5], k[6], ALU.mult).then_inc(dt_step, 1)

            def step_sizes_a(b, p):
                at = b * 9
                dve.wait_ge(dt_step, at + 6)
                dve.wait_ge(dt_log, b + 1)
                nc.vector.tensor_tensor(k[8], k[4], k[7], ALU.subtract).then_inc(dt_step, 1)
                dve.wait_ge(dt_step, at + 7)
                dtf = dt2[:, p].rearrange("p t h -> p (t h)")
                nc.vector.scalar_tensor_tensor(dtf, k[0], 0.0, k[8], ALU.max, ALU.add).then_inc(dt_step, 1)
                dve.wait_ge(dt_step, at + 8)
                nc.vector.tensor_tensor(a2[:, p], dt2[:, p], aneg[:].unsqueeze(1).broadcast_to([128, T2, SH]),
                                        ALU.mult).then_inc(dt_step, 1)

            def convolve(b, j):
                at = b * 16 + j * 8
                for k in range(TAPS):
                    for i in range(2):
                        c = 2 * j + i
                        if k == 0:
                            dve.wait_ge(xp_ready, b * 4 + 2 * j + 2)
                            if c == 0 and not (isinstance(b, int) and b == 0):
                                dve.wait_ge(xc_ready, b)
                            nc.vector.tensor_scalar(acc[:, c, :], xpad[:, c, 4:4 + L], cw[:, c, 3:4],
                                                    cb[:, c:c + 1], ALU.mult, ALU.add).then_inc(conv_step, 1)
                        else:
                            dve.wait_ge(conv_step, at + 2 * k + i - 1)
                            nc.vector.scalar_tensor_tensor(acc[:, c, :], xpad[:, c, k:k + L], cw[:, c, k - 1:k],
                                                           acc[:, c, :], ALU.mult, ALU.add).then_inc(conv_step, 1)

            def weigh_x(b, p, t):
                dve.wait_ge(tok_done, b * 2 + t + 1)
                if t == 0 and not (isinstance(b, int) and b == 0):
                    dve.wait_ge(y_done, b)
                nc.vector.tensor_tensor(xdt[:, 2 * t, :, :],
                                        ps[:, 3, 0:INNER].rearrange("p (h q) -> p h q", h=SH),
                                        dt2[:, p, t, :].unsqueeze(2).broadcast_to([128, SH, 64]),
                                        ALU.mult).then_inc(xdt_ready, 1)

            def decay_x(b):
                dve.wait_ge(suf_ready, b + 1)
                dve.wait_ge(xdt_ready, b * 3 + 1)
                nc.vector.tensor_tensor(xdt[:, 1, :, :], xdt[:, 0, :, :],
                                        esuf[:].unsqueeze(2).broadcast_to([128, SH, 64]),
                                        ALU.mult).then_inc(xdt_ready, 1)

            def mask_g(b):
                dve.wait_ge(g_done, b + 1)
                cut3 = ps[:, 3, 0:384].rearrange("p (a t) -> p a t", a=3)
                nc.vector.tensor_tensor(gmask[:, 0, :], cut3[:, 0, :], upto[:], ALU.mult)
                nc.vector.tensor_copy(gmask[:, 1, :], cut3[:, 1, :])
                nc.vector.tensor_tensor(gmask[:, 2, :], cut3[:, 2, :], upto[:], ALU.mult).then_inc(gm_ready, 1)
                dve.wait_ge(gm_ready, b + 1)

            def mix_decays(b, p):
                for i, g in enumerate((0, 2, 1)):
                    dve.wait_ge(dec_ready, b * 3 + i + 1)
                    nc.vector.tensor_tensor(mix[:, i], dec[(i + p) % 2],
                                            gmask[:, g, :].unsqueeze(1).broadcast_to([128, SH, 128]),
                                            ALU.mult).then_inc(mix_ready, 1)

            def take_y(b, p):
                dve.wait_ge(y_done, b + 1)
                if not (isinstance(b, int) and b == 0):
                    dve.wait_ge(gt_ready, b)
                for c in range(XC):
                    last = nc.vector.scalar_tensor_tensor(y2[:, c, :], xc[:, p, c, :], dd[:, c:c + 1],
                                                          psY[:, c * L:(c + 1) * L], ALU.mult, ALU.add)
                last.then_inc(y_ready, 1)

            def mean_square(b):
                dve.wait_ge(o2_done, b + 1)
                nc.vector.tensor_scalar(ms[:], ps[:, 3, 2 * C:2 * C + 2], 1.0 / INNER, 1e-5,
                                        ALU.mult, ALU.add).then_inc(ms_done, 1)

            def take_h2(b):
                dve.wait_ge(rt_done, b + 1)
                dve.wait_ge(hu_done, b + 1)
                if not (isinstance(b, int) and b == 0):
                    dve.wait_ge(h2_used, b)
                for t in range(T2):
                    last = nc.vector.scalar_tensor_tensor(h2[:, t, :], ps[:, 3, t * C:(t + 1) * C], rt[:, t:t + 1],
                                                          h_all[:, tile(b, t), :].rearrange("p a c -> p (a c)"),
                                                          ALU.mult, ALU.add)
                last.then_inc(h2_ready, 1)
                dve.wait_ge(h2_ready, b + 1)
                for t in range(T2):
                    last = nc.vector.bn_stats(st6[:, t, :], h2[:, t, :])
                last.then_inc(bn2_done, 1)
                dve.wait_ge(consts, 1)
                dve.wait_ge(bn2_done, b + 1)
                for t in range(T2):
                    last = nc.vector.bn_aggr(mv[:, t, :], st6[:, t, :])
                last.then_inc(mv2_done, 1)
                dve.wait_ge(mv2_done, b + 1)
                nc.vector.tensor_scalar(ve[:], mv[:, :, 1], 1e-5, None, ALU.add).then_inc(ve3_done, 1)

            def take_u3(b):
                dve.wait_ge(r3_done, b + 1)
                if not (isinstance(b, int) and b == 0):
                    dve.wait_ge(yt_done, b)
                for t in range(T2):
                    nc.vector.tensor_scalar(u3_all[:, tile(b, t), :].rearrange("p a c -> p (a c)"), h2[:, t, :],
                                            mv[:, t, 0:1], r1[:, t:t + 1], ALU.subtract, ALU.mult)
                    last = nc.vector.tensor_scalar(uu[:, t, :], h2[:, t, :], mv[:, t, 0:1], rr[:, t:t + 1],
                                                   ALU.subtract, ALU.mult)
                last.then_inc(yh_ready, 1)

            def take_yT(b):
                dve.wait_ge(yt_done, b + 1)
                if isinstance(b, int) and b:
                    dve.wait_ge(yT_ready, b)
                nc.vector.tensor_copy(yhT[:].rearrange("p a n -> p (a n)"), ps[0:HC, TR2, :]).then_inc(yhT_ready, 1)

            def take_logits(b):
                dve.wait_ge(lg_done, b + 1)
                for t in range(T2):
                    last = nc.vector.tensor_scalar(lg[:, t, bass.ds(b, 1), :].rearrange("p b e -> p (b e)"),
                                                   psLg[:, t * E:(t + 1) * E], s2[:, t:t + 1], None, ALU.mult)
                last.then_inc(lg_ready, 1)

            def stage2(s, p):
                project, next_x, mixing, output, routing = parts2(s)
                if output:
                    take_y(s - 2, p)
                if next_x:
                    normal_x(s + 1, 1 - p)
                if project:
                    convolve(s, 0)
                if routing:
                    take_u3(s - 3)
                if project:
                    step_sizes_v(s)
                if mixing:
                    weigh_x(s - 1, 1 - p, 0)
                if project:
                    convolve(s, 1)
                if mixing:
                    weigh_x(s - 1, 1 - p, 1)
                    decay_x(s - 1)
                if project:
                    step_sizes_e(s)
                if routing:
                    take_yT(s - 3)
                if mixing:
                    mask_g(s - 1)
                    mix_decays(s - 1, 1 - p)
                if routing:
                    take_logits(s - 3)
                if output:
                    mean_square(s - 2)
                if project:
                    step_sizes_a(s, p)
                if output:
                    take_h2(s - 2)

            normalise(B - 1, False)
            dve.wait_ge(w_rest, W_REST)
            normal_x(0, 0)
            take_h(B - 1, 0)
            for c in range(XC):
                last = nc.vector.tensor_scalar(wout[:, c, :], wout[:, c, :], rms[:, c:c + 1], None, ALU.mult)
            last.then_inc(setup, 1)
            take_h(B - 1, 1)
            stats1(B - 1)
            dve.wait_ge(alog_exp, 1)
            nc.vector.tensor_scalar(aneg[:], small[:, 11, 0:SH], -1.0, None, ALU.mult).then_inc(setup, 1)
            dve.wait_ge(setup, 2)
            dve.wait_ge(fills, 1)
            over_stages2(dve, stage2)

            nc.vector.tensor_copy(nest[:], nestf[:, 0:2 * (HC + 1)]).then_inc(w2_ready, 1)
            nc.vector.tensor_tensor(b2[:], b2[:], b2x[:], ALU.add).then_inc(w2_ready, 1)
            lgf = lg[:].rearrange("p t b e -> p (t b) e")
            tb = [128, T2 * B, E]
            dve.wait_ge(lg_ready, B)
            nc.vector.tensor_reduce(lsm[:, 0, :], lgf, AX.X, ALU.max).then_inc(ch_step, 1)
            dve.wait_ge(ch_step, 1)
            nc.vector.tensor_tensor(lgf, lgf, lsm[:, 0, :].unsqueeze(2).broadcast_to(tb), ALU.subtract).then_inc(ch_step, 1)
            dve.wait_ge(ch_exp, 1)
            nc.vector.tensor_reduce(lsm[:, 1, :], pe_[:], AX.X, ALU.add).then_inc(ch_step, 1)
            dve.wait_ge(ch_step, 3)
            nc.vector.reciprocal(lsm[:, 2, :], lsm[:, 1, :]).then_inc(ch_step, 1)
            dve.wait_ge(ch_step, 4)
            nc.vector.tensor_tensor(pe_[:], pe_[:], lsm[:, 2, :].unsqueeze(2).broadcast_to(tb), ALU.mult).then_inc(ch_step, 2)
            dve.wait_ge(pr_done, 1)
            nc.vector.tensor_copy(pr[:], ps[0:32, 0, 0:L]).then_inc(ch_step, 1)
            src, n = pr[:], 7
            for i in range(CAP // 8):
                dve.wait_ge(ch_step, n)
                nc.vector.max(top8[:], src).then_inc(ch_step, 1)
                dve.wait_ge(ch_step, n + 1)
                nc.vector.match_replace(pick[:, i % 2, :], top8[:], src, -1.0).then_inc(ch_step, 1)
                src, n = pick[:, i % 2, :], n + 2
            dve.wait_ge(ch_step, n)
            nc.vector.tensor_scalar(sel[:], src, 0.0, None, ALU.is_lt).then_inc(sel_ready, 1)
            dve.wait_ge(sel_ready, 1)
            nc.vector.tensor_tensor(gsel[:], pr[:], sel[:], ALU.mult).then_inc(sel_ready, 1)

            def take_yhat(c):
                dve.wait_ge(m_done, c + 1)
                if not (isinstance(c, int) and c == 0):
                    dve.wait_ge(m3_done, c * 3)
                nc.vector.tensor_tensor(yhat[:], yT_all[:, :, bass.ds(c * L, L)],
                                        ps[0:HC + 1, 0, :].rearrange("p (a n) -> p a n", a=2),
                                        ALU.mult).then_inc(yhat_ready, 1)

            def low_q3(c):
                dve.wait_ge(q3_ready, c + 1)
                nc.vector.tensor_tensor(qhl[:, 1].rearrange("p a n -> p (a n)"), ps[0:HC, 1, :],
                                        qhl[:, 0].rearrange("p a n -> p (a n)").bitcast(F32),
                                        ALU.subtract).then_inc(q3_split, 1)

            def low_k3(c):
                dve.wait_ge(k3_ready, c + 1)
                nc.vector.scalar_tensor_tensor(khl3[:, 1].rearrange("p a n -> p (a n)"), ps[0:HC, 0, :], SCALE,
                                               khl3[:, 0].rearrange("p a n -> p (a n)").bitcast(F32),
                                               ALU.mult, ALU.subtract).then_inc(k3_split, 1)

            def take_mlp(c, p, j, bank):
                dve.wait_ge(m3_done, c * 3 + j + 1)
                if j == 0 and not (isinstance(c, int) and c < 2):
                    dve.wait_ge(f_done, c * 2 - 2)
                nc.vector.tensor_copy(y2T[p][:, 2 * j:2 * j + 2, :].rearrange("p j n -> p (j n)"),
                                      ps[:, bank, :]).then_inc(m3_read, 1)

            def take_out(b, t):
                dve.wait_ge(f_done, b * 2 + t + 1)
                if t == 0 and not (isinstance(b, int) and b == 0):
                    dve.wait_ge(res_ready, b)
                nc.vector.tensor_tensor(res[:, t, :], ps[:, 0, 0:C], b2[:], ALU.add).then_inc(res_step, 1)
                dve.wait_ge(res_step, b * 2 + t + 1)
                nc.vector.tensor_tensor(res[:, t, :], res[:, t, :], ps[:, 0, C:2 * C], ALU.mult).then_inc(f_read, 1)

            def stage3(b, p):
                last = isinstance(b, int) and b == B - 1
                first = isinstance(b, int) and b == 0
                n0 = B * U + b * U
                for u in range(U):
                    if u == 1 and not first:
                        normalise(B + b - 1, True)
                    if u < U - 2 or not last:
                        unit_max(n0 + u + 2, u + 2)
                    if not last:
                        if u == 0:
                            take_yhat(b + 1)
                    unit_copy(n0 + u, u)
                    if 8 <= u < 11 and not last:
                        take_mlp(b + 1, 1 - p, u - 8, (1, 0, 1)[u - 8])
                    if u == 1 and not last:
                        low_q3(b + 1)
                    if u == 2 and not last:
                        low_k3(b + 1)
                    if u in (5, 7) and not first:
                        take_out(b - 1, (u - 5) // 2)

            take_yhat(0)
            low_q3(0)
            low_k3(0)
            for j in range(3):
                take_mlp(0, 0, j, (1, 0, 1)[j])
            unit_max(B * U, 0)
            unit_max(B * U + 1, 1)
            over_batches(dve, stage3)
            normalise(2 * B - 1, True)
            take_out(B - 1, 0)
            take_out(B - 1, 1)

        @block.scalar
        def _(act):
            def unit_exp(n, u):
                act.wait_ge(max_done, n + 1)
                if not isinstance(n, int) or n >= 3:
                    act.wait_ge(t_done, n - 2)
                for i in range(2):
                    last = nc.scalar.activation(prob[:, u % 3, i * 256:(i + 1) * 256],
                                                ps[:, SC + u % 3, i * 256:(i + 1) * 256], ACT.Exp,
                                                bias=nmax[:, u % 4, i:i + 1])
                last.then_inc(exp_done, 1)

            def take_k(c, p, k, bank):
                tb, half = divmod(k, 2)
                act.wait_ge(k_done, c * 4 + k + 1)
                if not (isinstance(c, int) and c == 0):
                    wait_k_stacked(c, tb)
                nc.scalar.activation(khl[:, 0, half, tb * 512:(tb + 1) * 512], ps[0:HC, bank, :],
                                     ACT.Copy, scale=SCALE).then_inc(k_ready, 1)

            def wait_k_stacked(c, tb):
                act.wait_ge(k_stacked[tb], c * 16 * KD)

            def take_v(c, p, k, bank):
                act.wait_ge(v_done, c * 4 + k + 1)
                if not (isinstance(c, int) and c < 2):
                    act.wait_ge(pv_done, (c - 1) * U)
                nc.scalar.activation(va[p][:, 2 * k:2 * k + 2, :, 0:D],
                                     ps[:, bank, 0:2 * C].rearrange("p (t h e) -> p t h e", t=2, e=D),
                                     ACT.Copy).then_inc(v_ready, 1)

            def take_kv(c, p, u):
                if 4 <= u < 8:
                    take_k(c, p, u - 4, K_BANKS[u - 4])
                elif u >= 8:
                    take_v(c, p, u - 8, u % 2)

            def stage1(b, p):
                last = isinstance(b, int) and b == B - 1
                for u in range(U):
                    if u < U - 1 or not last:
                        unit_exp(b * U + u + 1, (u + 1) % U)
                    if not last:
                        take_kv(b + 1, 1 - p, u)

            for u in range(U):
                take_kv(0, 0, u)
            unit_exp(0, 0)
            over_batches(act, stage1)

            def square(b):
                act.wait_ge(gt_ready, b + 1)
                if not (isinstance(b, int) and b == 0):
                    act.wait_ge(o2_done, b)
                nc.scalar.activation(gsq_, g_,
                                     ACT.Square).then_inc(gsq_ready, 1)

            def decays(b, p, i):
                if i == 0:
                    act.wait_ge(suf_done, b + 1)
                    if not (isinstance(b, int) and b == 0):
                        act.wait_ge(mix_ready, b * 3)
                act.wait_ge(seg_done, b * 3 + i + 1)
                if i == 2:
                    act.wait_ge(mix_ready, b * 3 + 1)
                nc.scalar.activation(dec[(i + p) % 2][:].rearrange("p (a h) t -> p a (h t)", a=2),
                                     ps[:, SC2:SC2 + 2, 0:384], ACT.Exp).then_inc(dec_ready, 1)
                if i == 0:
                    nc.scalar.activation(esuf[:], psSuf, ACT.Exp).then_inc(suf_ready, 1)

            def take_xn(b):
                act.wait_ge(xt_done, b + 1)
                if not (isinstance(b, int) and b == 0):
                    act.wait_ge(zx_done, b * 4)
                for half in range(2):
                    nc.scalar.activation(xnT[:, half, :], ps[0:HC, TR2, half * L:(half + 1) * L], ACT.Identity,
                                         bias=lnb[:, half:half + 1], scale=lnw[:, half:half + 1]).then_inc(xn_ready, 1)

            def dt_e(b):
                act.wait_ge(dt_step, b * 9 + 2)
                nc.scalar.activation(small[:, 2, :], small[:, 1, :], ACT.Exp, scale=-1.0).then_inc(dt_exp, 1)

            def dt_ln(b):
                act.wait_ge(dt_step, b * 9 + 3)
                nc.scalar.activation(small[:, 4, :], small[:, 3, :], ACT.Ln).then_inc(dt_log, 1)

            def take_x(b):
                for k in range(2):
                    act.wait_ge(zx_done, b * 4 + k + 1)
                    if k == 0 and not (isinstance(b, int) and b == 0):
                        act.wait_ge(conv_step, b * 16)
                    nc.scalar.activation(xpad[:, 2 * k:2 * k + 2, 4:4 + L],
                                         ps[:, k, :].rearrange("p (c t) -> p c t", c=2), ACT.Copy).then_inc(xp_ready, 2)
                    act.wait_ge(xp_ready, b * 4 + 2 * k + 2)
                    act.sem_inc(zx_read, 1)

            def take_z(b, p):
                act.wait_ge(zx_done, b * 4 + 3)
                if not (isinstance(b, int) and b < 2):
                    act.wait_ge(gt_ready, b - 1)
                nc.scalar.activation(sz[:, p, 0:2, :].rearrange("p c t -> p (c t)"), ps[:, 0, :], ACT.Silu).then_inc(zx_read, 1)
                act.wait_ge(zx_done, b * 4 + 4)
                nc.scalar.activation(sz[:, p, 2, :], ps[:, 1, 0:L], ACT.Silu).then_inc(zx_read, 1)

            def convolved(b, p):
                for c in range(XC):
                    act.wait_ge(conv_step, b * 16 + (7, 8, 15)[c])
                    if c == 0 and not (isinstance(b, int) and b < 2):
                        act.wait_ge(y_ready, b - 1)
                    nc.scalar.activation(xc[:, p, c, :], acc[:, c, :], ACT.Silu)
                act.wait_ge(conv_step, b * 16 + 16)
                if not (isinstance(b, int) and b == 0):
                    act.wait_ge(g_done, b)
                for i in range(2):
                    last = nc.scalar.activation(bcT[:, i, :], acc[64 * i:64 * i + 64, 3, :], ACT.Silu)
                last.then_inc(xc_ready, 1)

            def take_y(b):
                act.wait_ge(yhT_ready, b + 1)
                for half in range(2):
                    last = nc.scalar.activation(yT_all[0:HC, half, bass.ds(b * L, L)],
                                                yhT[:, half, :], ACT.Identity,
                                                bias=bet[:, half:half + 1], scale=gam[:, half:half + 1])
                last.then_inc(yT_ready, 1)

            def stage2(s, p):
                project, next_x, mixing, output, routing = parts2(s)
                if project:
                    take_x(s)
                if project:
                    dt_e(s)
                if mixing:
                    decays(s - 1, 1 - p, 0)
                if output:
                    square(s - 2)
                if mixing:
                    decays(s - 1, 1 - p, 1)
                    decays(s - 1, 1 - p, 2)
                if next_x:
                    take_xn(s + 1)
                if project:
                    dt_ln(s)
                    take_z(s, p)
                    convolved(s, p)
                if routing:
                    take_y(s - 3)

            act.wait_ge(w_rest, W_REST)
            nc.scalar.activation(small[:, 11, 0:SH], aneg[:], ACT.Exp).then_inc(alog_exp, 1)
            take_xn(0)
            over_stages2(act, stage2)

            act.wait_ge(ch_step, 2)
            nc.scalar.activation(pe_[:].rearrange("p a e -> p (a e)"), lg[:].rearrange("p t b e -> p (t b e)"),
                                 ACT.Exp).then_inc(ch_exp, 1)

            def take_q3(c):
                act.wait_ge(q3_done, c + 1)
                if isinstance(c, int) and c == 1:
                    for group in first3:
                        act.wait_ge(group, 16 * 9)
                nc.scalar.activation(qhl[:, 0].rearrange("p a n -> p (a n)"), ps[0:HC, 1, :],
                                     ACT.Copy).then_inc(q3_ready, 1)

            def take_k3(c, p):
                act.wait_ge(k3_done, c + 1)
                nc.scalar.activation(khl3[:, 0].rearrange("p a n -> p (a n)"), ps[0:HC, 0, :],
                                     ACT.Copy, scale=SCALE).then_inc(k3_ready, 1)

            def take_v3(c, p):
                act.wait_ge(v3_done, c + 1)
                if not (isinstance(c, int) and c < 2):
                    act.wait_ge(pv_done, B * U + (c - 1) * U)
                nc.scalar.activation(va3[p][:, :, :, 0:D], ps[:, 1, 0:T2 * C].rearrange("p (t h e) -> p t h e", t=T2, e=D),
                                     ACT.Copy).then_inc(v3_ready, 1)

            def gelu(c, p):
                act.wait_ge(m3_read, c * 3 + 3)
                y = y2T[p].rearrange("p j n -> p (j n)")
                nc.scalar.activation(y, y, ACT.Gelu).then_inc(gelu_done, 1)

            def stage3(b, p):
                last = isinstance(b, int) and b == B - 1
                for u in range(U):
                    if u < U - 1 or not last:
                        unit_exp(B * U + b * U + u + 1, (u + 1) % U)
                    if last:
                        continue
                    if u == 1:
                        take_q3(b + 1)
                    if u == 2:
                        take_k3(b + 1, 1 - p)
                    if u == 3:
                        take_v3(b + 1, 1 - p)
                    if u == 11:
                        gelu(b + 1, 1 - p)

            take_q3(0)
            take_k3(0, 0)
            take_v3(0, 0)
            gelu(0, 0)
            unit_exp(B * U, 0)
            over_batches(act, stage3)

        @block.gpsimd
        def _(pool):
            filled = [(xT[0][HC:HC + 1, 1, :], 1.0), (xT[1][HC:HC + 1, 1, :], 1.0), (va_ones(areaV1, N // 128), 1.0),
                      (ones[:], 1.0), (mhalf[:], -0.5), (eps5[:], 1e-5), (eps6[:], 1e-6)]
            for i, (where, value) in enumerate(filled):
                if i:
                    pool.wait_ge(consts, i)
                nc.gpsimd.memset(where, value).then_inc(consts, 1)

            def split_q(c):
                qm_, high, low = (a.rearrange("p a n -> p (a n)") for a in (
                    qm[:].rearrange("p a w e q -> p a (w e q)"), qmhl[:, 0], qmhl[:, 1]))
                for half in range(2):
                    pool.wait_ge(q_pooled, c * 4 + 2 * half + 2)
                    if not (isinstance(c, int) and c == 0):
                        pool.wait_ge(q_split, c * 3)
                        pool.wait_ge(s_done, (c - 1) * U + 1)
                    for to in (qm[:, half], qmhl[:, 0, half, :].rearrange("p (w e q) -> p w e q", w=W, e=2)):
                        last = nc.gpsimd.tensor_tensor(
                            to, qp[:, half, :].rearrange("p (w q) -> p w q", w=W).unsqueeze(2)
                            .broadcast_to([HC, W, 2, QW]),
                            hm[:].unsqueeze(1).unsqueeze(3).broadcast_to([HC, W, 2, QW]), ALU.mult)
                    last.then_inc(q_split, 1)
                pool.wait_ge(q_split, c * 3 + 2)
                nc.gpsimd.tensor_tensor(low, qm_, high.bitcast(F32), ALU.subtract).then_inc(q_split, 1)

            def factors(b):
                pool.wait_ge(consts, 7)
                pool.wait_ge(ve_done, b + 1)
                at = b * 4
                r = r1[:]
                nc.gpsimd.tensor_tensor(r1_all[:, bass.ds(b * T2, T2)], ve[:], mhalf[:], ALU.pow)
                nc.gpsimd.tensor_tensor(r, ve[:], mhalf[:], ALU.pow).then_inc(pow_step, 1)
                pool.wait_ge(pow_step, at + 1)
                nc.gpsimd.tensor_tensor(vu[:], mv[:, :, 1], r, ALU.mult).then_inc(pow_step, 1)
                pool.wait_ge(pow_step, at + 2)
                nc.gpsimd.tensor_tensor(vu[:], vu[:], r, ALU.mult).then_inc(pow_step, 1)
                pool.wait_ge(pow_step, at + 3)
                nc.gpsimd.tensor_tensor(ve2[:], vu[:], eps5[:], ALU.add).then_inc(pow_step, 1)
                pool.wait_ge(pow_step, at + 4)
                nc.gpsimd.tensor_tensor(vu[:], ve2[:], mhalf[:], ALU.pow).then_inc(r1_done, 1)
                pool.wait_ge(consts, 7)
                pool.wait_ge(r1_done, b + 1)
                nc.gpsimd.tensor_tensor(rr_all[:, bass.ds(b * T2, T2)], vu[:], r, ALU.mult).then_inc(stat_done, 1)

            def stage1(b, p):
                last = isinstance(b, int) and b == B - 1
                first = isinstance(b, int) and b == 0
                if not last:
                    split_q(b + 1)
                if not first:
                    factors(b - 1)

            pool.wait_ge(w_first, W_FIRST)
            split_q(0)
            over_batches(pool, stage1)

            pool.wait_ge(stat_done, B - 1)
            pool.wait_ge(pv_done, B * U)
            nc.gpsimd.memset(xpad[:, :, 0:4], 0.0).then_inc(fills, 1)
            pool.wait_ge(fills, 1)
            factors(B - 1)
            pool.wait_ge(w_rest, W_REST)
            pool.wait_ge(stat_done, B)

            def add_u(b):
                pool.wait_ge(consts, 7)
                pool.wait_ge(xh_ready, b + 1)
                hb = h_all[:, bass.ds(b * T2, T2), :]
                nc.gpsimd.tensor_tensor(hb, hb, uu2[:], ALU.add).then_inc(hu_done, 1)

            def gate(b, p):
                pool.wait_ge(y_ready, b + 1)
                if not (isinstance(b, int) and b == 0):
                    pool.wait_ge(o2_done, b)
                    pool.wait_ge(gsq_ready, b)
                nc.gpsimd.tensor_tensor(g_, y_, sz[:, p].rearrange("p c t -> p (c t)"), ALU.mult).then_inc(gt_ready, 1)

            def factors2(b):
                pool.wait_ge(ms_done, b + 1)
                nc.gpsimd.tensor_tensor(rt[:], ms[:], mhalf[:], ALU.pow).then_inc(rt_done, 1)
                pool.wait_ge(ve3_done, b + 1)
                at = b * 6
                if not (isinstance(b, int) and b == 0):
                    pool.wait_ge(yh_ready, b)
                nc.gpsimd.tensor_tensor(r1[:], ve[:], mhalf[:], ALU.pow).then_inc(pow2_step, 1)
                pool.wait_ge(pow2_step, at + 1)
                nc.gpsimd.tensor_tensor(vu[:], mv[:, :, 1], r1[:], ALU.mult).then_inc(pow2_step, 1)
                pool.wait_ge(pow2_step, at + 2)
                nc.gpsimd.tensor_tensor(vu[:], vu[:], r1[:], ALU.mult).then_inc(pow2_step, 1)
                pool.wait_ge(pow2_step, at + 3)
                nc.gpsimd.tensor_tensor(ve2[:], vu[:], eps6[:], ALU.add).then_inc(pow2_step, 1)
                pool.wait_ge(pow2_step, at + 4)
                nc.gpsimd.tensor_tensor(r2[:], ve2[:], mhalf[:], ALU.pow).then_inc(pow2_step, 1)
                pool.wait_ge(pow2_step, at + 5)
                nc.gpsimd.tensor_tensor(rr[:], r1[:], r2[:], ALU.mult).then_inc(pow2_step, 1)
                if not (isinstance(b, int) and b == 0):
                    pool.wait_ge(lg_ready, b)
                nc.gpsimd.tensor_tensor(s2[:], ve2[:], r2[:], ALU.mult).then_inc(r3_done, 1)

            def residual3(b):
                pool.wait_ge(consts, 7)
                pool.wait_ge(yh_ready, b + 1)
                where = u3_all[:, bass.ds(b * T2, T2), :]
                nc.gpsimd.tensor_tensor(where, where, h2[:], ALU.add).then_inc(h2_used, 1)

            def spread_a(b, p):
                pool.wait_ge(dt_step, b * 9 + 9)
                for t in range(T2):
                    if not (isinstance(b, int) and b == 0):
                        pool.wait_ge(seg_done, b * 3)
                    nc.gpsimd.tensor_tensor(a1[:, t], a2[:, p, t, :].unsqueeze(2).broadcast_to([128, SH, 128]),
                                            upto[:].unsqueeze(1).broadcast_to([128, SH, 128]),
                                            ALU.mult).then_inc(a1_ready, 1)

            def stage2(s, p):
                project, next_x, mixing, output, routing = parts2(s)
                if output:
                    gate(s - 2, p)
                if next_x:
                    add_u(s + 1)
                if routing:
                    residual3(s - 3)
                if output:
                    factors2(s - 2)
                if project:
                    spread_a(s, p)

            add_u(0)
            over_stages2(pool, stage2)
            pool.wait_ge(lg_ready, B)
            pool.wait_ge(h2_used, B)
            nc.gpsimd.memset(yT_all[HC:HC + 1, :, :], 1.0).then_inc(consts, 1)
            pool.wait_ge(consts, 8)
            nc.gpsimd.memset(va_ones(areaV3, T2), 1.0).then_inc(vones, 1)
            pool.wait_ge(vones, 1)
            nc.gpsimd.memset(qst3[0][:].bitcast(F32), 0.0).then_inc(zeros3, 1)
            pool.wait_ge(zeros3, 1)
            nc.gpsimd.memset(qst3[1][:].bitcast(F32), 0.0).then_inc(zeros3, 1)

            def take_sel(c):
                pool.wait_ge(consts, 8)
                if isinstance(c, int) and c == 0:
                    pool.wait_ge(sel_ready, 1)
                else:
                    pool.wait_ge(m_done, c)
                nc.gpsimd.tensor_tensor(selb[:], sel[:], rowm[:, bass.ds(c, 1)].broadcast_to([32, L]),
                                        ALU.mult).then_inc(selb_ready, 1)

            def take_gates(c, p):
                pool.wait_ge(consts, 8)
                if isinstance(c, int) and c == 0:
                    pool.wait_ge(sel_ready, 2)
                nc.gpsimd.tensor_tensor(gselb[:, p, :], gsel[:], rowm[:, bass.ds(c, 1)].broadcast_to([32, L]),
                                        ALU.mult).then_inc(gates_ready, 1)

            def add_u3(b):
                pool.wait_ge(f_read, b * 2 + 2)
                nc.gpsimd.tensor_tensor(res2[:], res[:], u3_all[:, bass.ds(b * T2, T2), :], ALU.add).then_inc(res_ready, 1)

            def stage3(b, p):
                last = isinstance(b, int) and b == B - 1
                first = isinstance(b, int) and b == 0
                if not last:
                    take_sel(b + 1)
                if not first:
                    pool.wait_ge(consts, 8)
                    wait_stored(b - 1, 1 - p)
                    add_u3(b - 1)
                if not last:
                    take_gates(b + 1, 1 - p)

            def wait_stored(b, p):
                if isinstance(b, int) and b == 0:
                    return
                q = 1 - p
                pool.wait_ge(stored[q], (b - 1 - q) * 8 + 16)

            take_sel(0)
            take_gates(0, 0)
            over_batches(pool, stage3)
            wait_stored(B - 1, 1)
            add_u3(B - 1)


def va_ones(areaV, tiles):
    return (areaV[:, :, 0:tiles * H * 32].rearrange("p a (t e) -> p a t e", e=32))[:, :, :, D:32]


def _layouts(v):
    f = np.float32

    def halves(a):
        got = np.zeros((HC + 1, 2, a.shape[1]), f)
        got[:HC, 0], got[:HC, 1] = a[:HC], a[HC:C]
        if a.shape[0] > C:
            got[HC, 1] = a[C]
        return got if a.shape[0] > C else np.ascontiguousarray(got[:HC])

    def heads(a):
        got = np.zeros((128, G3, a.shape[1]), f)
        for h in range(H):
            got[32 * (h % 4):32 * (h % 4) + D, h // 4] = a[h * D:(h + 1) * D]
        return got

    def chunks(a):
        return np.ascontiguousarray(a.reshape((-1, 128) + a.shape[1:]).swapaxes(0, 1))

    x = v["x"].reshape(B, STRIDE, QW, W, C)
    x = x.transpose(0, 4, 3, 1, 2).reshape(B, 2, HC, N).transpose(0, 2, 1, 3)
    w2 = v["L0_ffn_w2"].reshape(2, C, MLP + C).transpose(0, 2, 1)
    r, c = np.arange(128)[:, None], np.arange(128)[None, :]
    keeps = [C >> (E - 1 - e) for e in range(E)]
    inside = np.array([[ch < keeps[e % E] for ch in range(C)] for e in range(B * E)], f)
    nest = np.ones((B * E, 2 * (HC + 1) + C), f)
    nest[:, 0:HC], nest[:, HC + 1:2 * HC + 1], nest[:, 2 * HC + 2:] = inside[:, :HC], inside[:, HC:], inside
    return {
        "x": x,
        "wqkv": halves(np.concatenate([v["L0_tok_qkv_w"].T, v["L0_tok_qkv_b"][None]])),
        "wo": heads(v["L0_tok_proj_w"].T), "bo": v["L0_tok_proj_b"],
        "win": halves(v["L0_attn_W_in"]),
        "lnw": v["L0_attn_ln_w"].reshape(2, HC).T, "lnb": v["L0_attn_ln_b"].reshape(2, HC).T,
        "cw": chunks(v["L0_attn_conv_w"]), "cb": chunks(v["L0_attn_conv_b"]),
        "dtb": v["L0_attn_dt_bias"], "alog": v["L0_attn_A_log"],
        "dd": chunks(np.repeat(v["L0_attn_D"], 64)), "rms": chunks(v["L0_attn_rms_w"]),
        "wout": chunks(v["L0_attn_W_out"]), "wr": halves(v["L0_ffn_w_router"].T),
        "gam": v["L0_ffn_gamma1"].reshape(2, HC).T, "bet": v["L0_ffn_beta1"].reshape(2, HC).T,
        "w1": halves(np.concatenate([v["L0_ffn_w1"].T, v["L0_ffn_b1"][None]])),
        "w2": np.stack([np.concatenate([chunks(w[:MLP]), heads(w[MLP:])], 1) for w in w2]),
        "b2": v["L0_ffn_b2"].reshape(2, C),
        "hm": np.arange(HC)[:, None] // D % 2 == np.arange(2)[None, :],
        "later": r > c, "upto": r <= c, "eye": r == c,
        "nest": nest, "row": np.arange(B * E)[:, None] // E == np.arange(B)[None, :],
    }


def kernel(**inputs):
    import concourse.bacc as _bacc
    from concourse import mybir as _mybir
    from concourse.bass_utils import run_bass_kernel_spmd as _run

    nc = _bacc.Bacc("TRN2", target_bir_lowering=False, num_devices=1)
    laid = _layouts({k: np.asarray(a) for k, a in inputs.items()})
    arrays, args = {}, []
    for name, a in laid.items():
        a = np.ascontiguousarray(a, dtype=np.float32)
        arrays[f"in_{name}_dram"] = a
        args.append(nc.dram_tensor(f"in_{name}_dram", a.shape, _mybir.dt.float32, kind="ExternalInput").ap())
    out = nc.dram_tensor("out_dram", (B, L, C), _mybir.dt.float32, kind="ExternalOutput").ap()
    audio_tower(nc, *args, out)
    r = _run(nc, [arrays], core_ids=[0])
    return r.results[0]["out_dram"]
```

```python
from contextlib import ExitStack

import numpy as np

import concourse.bass as bass
from concourse import mybir
from concourse.alu_op_type import AluOpType as ALU

F32 = mybir.dt.float32
F32R = mybir.dt.float32r
BF16 = mybir.dt.bfloat16
ACT = mybir.ActivationFunctionType
AX = mybir.AxisListType

B = 8
N = 1024
L = 256
C = 192
HC = C // 2
H = 12
D = C // H
HH = H // 2
PAIRS = H // 2
SR = 6 * D
STRIDE = 4
W = 4
QW = 64
KW = 256
E = 4
CAP = L // 2
MLP = 4 * C
F1 = MLP + 3 * C
MJ = MLP // 128
G3 = H // 4
INNER = 2 * C
STATE = 64
SH = INNER // 64
XC = INNER // 128
ZXD = 2 * INNER + 2 * STATE + SH
U = 12
TAPS = 4
T2 = 2
SCALE = float(D) ** -0.5


def audio_tower(nc, x, wqkv_d, wo_d, bo_d, win_d, lnw_d, lnb_d, cw_d, cb_d, dtb_d, alog_d, dd_d, rms_d,
                wout_d, wr_d, gam_d, bet_d, w1_d, w2_d, b2_d, hm_d, later_d, upto_d, eye_d, nest_d,
                row_d, out):
    with ExitStack() as ctx:
        def sb(name, shape, dt=F32):
            return ctx.enter_context(nc.sbuf_tensor(name, shape, dt))

        def sb_phase(*tensors):
            with ExitStack() as phase:
                return [phase.enter_context(nc.sbuf_tensor(*t)) for t in tensors]

        def sem(name):
            return ctx.enter_context(nc.semaphore(name))

        ps = ctx.enter_context(nc.psum_tensor("ps", [128, 8, 512], F32))
        TR, SC, OB = 2, 3, 6
        TR2, SC2 = 2, 4
        psO = ps[:, OB:OB + 2, :].rearrange("p a n -> p (a n)")[:, 0:G3 * L]
        psH = ps[:, 7, 256:256 + C]
        psY = psO
        psDt = ps[:, 7, 256:256 + T2 * SH]
        psSuf = ps[:, 7, 272:272 + SH]
        psLg = ps[:, 7, 288:288 + T2 * E]

        areaX = sb("areaX", [128, 2, 2048])
        xT = [areaX[:, p, :].rearrange("p (a n) -> p a n", a=2) for p in range(2)]

        prob = sb("prob", [128, 3, 512])
        probT = sb("probT", [128, 3, 512])
        nmax = sb("nmax", [128, 4, 2])
        qp = sb("qp", [HC, 2, L])
        qhl = sb("qhl", [HC, 2, 2, L], F32R)
        otA = sb("otA", [128, G3 * L])
        rsum = sb("rsum", [128, G3 * L // 32])
        oT = sb("oT", [128, G3, L])
        h_all = sb("h_all", [128, B * T2, C])
        st6 = sb("st6", [128, T2, 6])
        mv = sb("mv", [128, T2, 2])
        mean_all = sb("mean_all", [128, B * T2])
        ve = sb("ve", [128, T2])
        vu = sb("vu", [128, T2])
        ve2 = sb("ve2", [128, T2])
        r1_all = sb("r1_all", [128, B * T2])
        rr_all = sb("rr_all", [128, B * T2])
        mhalf = sb("mhalf", [128, T2])
        eps5 = sb("eps5", [128, T2])
        eps6 = sb("eps6", [128, T2])

        wqkv = sb("wqkv", [HC + 1, 2, 3 * C])
        wo = sb("wo", [128, G3, C])
        bo = sb("bo", [128, C])
        hm = sb("hm", [HC, 2])
        eye = sb("eye", [128, 128])
        later = sb("later", [128, 128])
        upto = sb("upto", [128, 128])
        ones = sb("ones", [128, 128])
        win = sb("win", [HC, 2, ZXD])
        lnw = sb("lnw", [HC, 2])
        lnb = sb("lnb", [HC, 2])
        cw = sb("cw", [128, TAPS, TAPS])
        cb = sb("cb", [128, TAPS])
        dtb = sb("dtb", [128, SH])
        aneg = sb("aneg", [128, SH])
        dd = sb("dd", [128, XC])
        rms = sb("rms", [128, XC])
        wout = sb("wout", [128, XC, C])
        wr = sb("wr", [HC, 2, E])
        gam = sb("gam", [HC, 2])
        bet = sb("bet", [HC, 2])
        w1 = sb("w1", [HC + 1, 2, F1])
        w2 = sb("w2", [128, MJ + G3, C])
        w2x = areaX[:, 1, 0:(MJ + G3) * C].rearrange("p (j c) -> p j c", c=C)
        b2 = sb("b2", [128, C])
        b2x = sb("b2x", [128, C])
        nestf = sb("nestf", [32, 2 * (HC + 1) + C])
        nest = sb("nest", [32, 2 * (HC + 1)], BF16)
        rowm = sb("rowm", [32, B])

        small = sb("small", [128, 12, T2 * SH])
        dt2 = sb("dt2", [128, 2, T2, SH])
        a2 = sb("a2", [128, 2, T2, SH])
        esuf = sb("esuf", [128, SH])
        ms = sb("ms", [128, T2])
        rt = sb("rt", [128, T2])
        r1 = sb("r1", [128, T2])
        r2 = sb("r2", [128, T2])
        rr = sb("rr", [128, T2])
        s2 = sb("s2", [128, T2])
        lg = sb("lg", [128, T2, B, E])
        lsm = sb("lsm", [128, 4, T2 * B])
        pe_ = sb("pe_", [128, T2 * B, E])
        top8 = sb("top8", [32, 8])
        y2T = [areaX[:, p, 0:MJ * L].rearrange("p (j n) -> p j n", j=MJ) for p in range(2)]

        kst, qst0, qst1, qmhl, khl, xhl, whl, areaV1 = sb_phase(
            ("kst", [SR, PAIRS, N], F32R), ("qst0", [SR, PAIRS, 2 * L], F32R), ("qst1", [SR, PAIRS, 2 * L], F32R),
            ("qmhl", [HC, 2, 2, 2 * L], F32R), ("khl", [HC, 2, 2, N], F32R),
            ("xhl", [HC + 1, 2, 2, N], F32R), ("whl", [HC + 1, 2, 2, 2 * C], F32R), ("areaV1", [128, 3072], F32))
        qst = [qst0, qst1]
        va = areaV1[:, :].rearrange("p (t h e) -> p t h e", t=N // 128, e=32)
        u3_all = sb("u3_all", [128, B * T2, C])
        yT_all = sb("yT_all", [HC + 1, 2, B * L])
        res = sb("res", [128, T2, C])
        res2 = sb("res2", [128, T2, C])
        uu2 = res
        areaQ, areaK, areaV, uu, xnT, bcT, h2, yhT = sb_phase(
            ("areaQ", [128, 5376], F32), ("areaK", [128, 3840], F32), ("areaV", [128, 5904], F32),
            ("uu", [128, T2, C], F32), ("xnT", [HC, 2, L], F32), ("bcT", [STATE, 2, L], F32),
            ("h2", [128, T2, C], F32), ("yhT", [HC, 2, L], F32))
        qst30, qst31, kst30, kst31, khl3, pr, pick, sel, gsel, selb, gselb, yhat, areaV3, w1hl, yhl0, yhl1 = sb_phase(
            ("qst30", [SR, PAIRS, 2, L], F32R), ("qst31", [SR, PAIRS, 2, L], F32R),
            ("kst30", [SR, PAIRS, L], F32R), ("kst31", [SR, PAIRS, L], F32R), ("khl3", [HC, 2, 2, L], F32R),
            ("pr", [32, L], F32), ("pick", [32, 2, L], F32), ("sel", [32, L], F32), ("gsel", [32, L], F32),
            ("selb", [32, L], BF16), ("gselb", [32, 2, L], F32), ("yhat", [HC + 1, 2, L], F32),
            ("areaV3", [128, 2, T2 * H * 32], F32),
            ("w1hl", [HC + 1, 2, 2, MLP + 2 * C], F32R), ("yhl0", [HC + 1, 2, 2, L], F32R),
            ("yhl1", [HC + 1, 2, 2, L], F32R))
        qst3, kst3, yhl = [qst30, qst31], [kst30, kst31], [yhl0, yhl1]
        va3 = [areaV3[:, p, :].rearrange("p (t h e) -> p t h e", t=T2, e=32) for p in range(2)]

        def cut(area, sizes):
            got, at = [], 0
            for n in sizes:
                got.append(area[:, at:at + n])
                at += n
            return got

        qflat, kflat, vflat = areaQ[:, :], areaK[:, :], areaV[:, :]
        m_, a1_, ex0, ex1 = cut(qflat, [3 * 768, 2 * 768, 768, 768])
        mix = m_.rearrange("p (a h t) -> p a h t", a=3, h=SH)
        a1 = a1_.rearrange("p (a h t) -> p a h t", a=2, h=SH)
        dec = [ex0.rearrange("p (h t) -> p h t", h=SH), ex1.rearrange("p (h t) -> p h t", h=SH)]
        xdt_, y_, g_, gsq_, gm_ = cut(kflat, [3 * INNER, XC * L, XC * L, XC * L, 3 * 128])
        xdt = xdt_.rearrange("p (a h q) -> p a h q", a=3, h=SH)
        y2 = y_.rearrange("p (c t) -> p c t", c=XC)
        gt = g_.rearrange("p (c t) -> p c t", c=XC)
        gsq = gsq_.rearrange("p (c t) -> p c t", c=XC)
        gmask = gm_.rearrange("p (a t) -> p a t", a=3)
        xc_, sz_, xpad_, acc_, xh_ = cut(vflat, [2 * XC * L, 2 * XC * L, TAPS * (L + 4), TAPS * L, 2 * T2 * C])
        xh = xh_.rearrange("p (b t c) -> p b t c", b=2, t=T2)
        xc = xc_.rearrange("p (b c t) -> p b c t", b=2, c=XC)
        sz = sz_.rearrange("p (b c t) -> p b c t", b=2, c=XC)
        xpad = xpad_.rearrange("p (c t) -> p c t", c=TAPS)
        acc = acc_.rearrange("p (c t) -> p c t", c=TAPS)
        x_first, w_first, w_rest, w2x_loaded = sem("x_first"), sem("w_first"), sem("w_rest"), sem("w2x_loaded")
        x_loaded = [sem("x_loaded0"), sem("x_loaded1")]
        x_used = sem("x_used")
        consts = sem("consts")
        fills = sem("fills")
        vones = sem("vones")
        s_done, max_done, exp_done = sem("s_done"), sem("max_done"), sem("exp_done")
        t_done, pt_ready, pv_done = sem("t_done"), sem("pt_ready"), sem("pv_done")
        o_read, ot_sum, ot_norm, ot_ready = sem("o_read"), sem("ot_sum"), sem("ot_norm"), sem("ot_ready")
        q_done, k_done, v_done, h_done = sem("q_done"), sem("k_done"), sem("v_done"), sem("h_done")
        q_pooled, k_ready, v_ready, h_ready = sem("q_pooled"), sem("k_ready"), sem("v_ready"), sem("h_ready")
        q_high, q_split, q_low, k_split = sem("q_high"), sem("q_split"), sem("q_low"), sem("k_split")
        x_high, x_low, w_high, w_low = sem("x_high"), sem("x_low"), sem("w_high"), sem("w_low")
        q_stacked = [sem("q_stacked0"), sem("q_stacked1")]
        k_stacked = [sem("k_stacked0"), sem("k_stacked1")]
        bn_done, mv_done, ve_done, r1_done = sem("bn_done"), sem("mv_done"), sem("ve_done"), sem("r1_done")
        pow_step = sem("pow_step")
        stat_done = sem("stat_done")
        alog_exp = sem("alog_exp")
        setup, w2_ready = sem("setup"), sem("w2_ready")
        xh_ready, hu_done = sem("xh_ready"), sem("hu_done")
        xt_done, xn_ready = sem("xt_done"), sem("xn_ready")
        dt_done, zx_done, zx_read = sem("dt_done"), sem("zx_done"), sem("zx_read")
        dt_step, dt_exp, dt_log = sem("dt_step"), sem("dt_exp"), sem("dt_log")
        xp_ready, conv_step = sem("xp_ready"), sem("conv_step")
        xc_ready = sem("xc_ready")
        a1_ready, tok_done, g_done, suf_done = sem("a1_ready"), sem("tok_done"), sem("g_done"), sem("suf_done")
        seg_done, dec_ready, suf_ready = sem("seg_done"), sem("dec_ready"), sem("suf_ready")
        xdt_ready, gm_ready, mix_ready = sem("xdt_ready"), sem("gm_ready"), sem("mix_ready")
        y_done, y_ready, gt_ready, gsq_ready = sem("y_done"), sem("y_ready"), sem("gt_ready"), sem("gsq_ready")
        o2_done, ms_done, rt_done, h2_ready = sem("o2_done"), sem("ms_done"), sem("rt_done"), sem("h2_ready")
        bn2_done, mv2_done, ve3_done, r3_done = sem("bn2_done"), sem("mv2_done"), sem("ve3_done"), sem("r3_done")
        h2_used = sem("h2_used")
        pow2_step, yh_ready = sem("pow2_step"), sem("yh_ready")
        yt_done, yhT_ready, yT_ready = sem("yt_done"), sem("yhT_ready"), sem("yT_ready")
        lg_done, lg_ready = sem("lg_done"), sem("lg_ready")
        ch_step, ch_exp, pr_done = sem("ch_step"), sem("ch_exp"), sem("pr_done")
        w1_high, w1_low = sem("w1_high"), sem("w1_low")
        yhat_high, yhat_split = sem("yhat_high"), sem("yhat_split")
        gates_ready, sel_ready = sem("gates_ready"), sem("sel_ready")
        selb_ready, m_done, yhat_ready = sem("selb_ready"), sem("m_done"), sem("yhat_ready")
        q3_done, k3_done, v3_done, m3_done = sem("q3_done"), sem("k3_done"), sem("v3_done"), sem("m3_done")
        q3_ready, k3_ready, v3_ready, m3_read = sem("q3_ready"), sem("k3_ready"), sem("v3_ready"), sem("m3_read")
        gelu_done, q3_split, k3_split = sem("gelu_done"), sem("q3_split"), sem("k3_split")
        zeros3 = sem("zeros3")
        qk3_stacked = [sem("qk3_stacked0"), sem("qk3_stacked1")]
        first3 = [sem(f"first3_{j}") for j in range(PAIRS // 2)]
        f_done, f_read, res_step, res_ready = sem("f_done"), sem("f_read"), sem("res_step"), sem("res_ready")
        stored = [sem("stored0"), sem("stored1")]

        block = ctx.enter_context(nc.Block())

        def over_batches(eng, stage):
            stage(0, 0)
            with eng.Fori(0, B // 2 - 1) as i:
                stage(i * 2 + 1, 1)
                stage(i * 2 + 2, 0)
            stage(B - 1, 1)

        def over_split_batches(eng, stage):
            stage(0, 0)
            with eng.Fori(0, B // 2 - 2) as i:
                stage(i * 2 + 1, 1)
                stage(i * 2 + 2, 0)
            for b in range(B - 3, B):
                stage(b, b % 2)

        def over_stages2(eng, stage):
            for s in range(3):
                stage(s, s % 2)
            with eng.Fori(0, (B - 4) // 2) as i:
                stage(i * 2 + 3, 1)
                stage(i * 2 + 4, 0)
            for s in range(B - 1, B + 3):
                stage(s, s % 2)

        def parts2(s):
            if not isinstance(s, int):
                return (True,) * 5
            return s < B, s + 1 < B, 0 <= s - 1 < B, 0 <= s - 2 < B, 0 <= s - 3 < B

        def tile(b, t):
            return bass.ds(b * T2 + t, 1)

        @block.sync
        def _(sp):
            sp.dma_start(xT[0][0:HC, :, 0:N // 2], x[0][:, :, 0:N // 2]).then_inc(x_first, 16)
            sp.dma_start(wqkv[:, :, 0:C], wqkv_d[:, :, 0:C]).then_inc(x_first, 16)
            sp.dma_start(xT[0][0:HC, :, N // 2:N], x[0][:, :, N // 2:N]).then_inc(x_loaded[0], 16)
            sp.dma_start(wqkv[:, :, C:2 * C], wqkv_d[:, :, C:2 * C]).then_inc(w_first, 16)
            sp.dma_start(wqkv[:, :, 2 * C:3 * C], wqkv_d[:, :, 2 * C:3 * C]).then_inc(w_first, 16)
            sp.dma_start(hm[:], hm_d).then_inc(w_first, 16)
            sp.dma_start(eye[:], eye_d).then_inc(w_first, 16)
            sp.dma_start(wo[:], wo_d).then_inc(w_first, 16)
            sp.dma_start(bo[:], bo_d.rearrange("(a n) -> a n", a=1).broadcast_to([128, C])).then_inc(w_first, 16)
            sp.dma_start(xT[1][0:HC], x[1]).then_inc(x_loaded[1], 16)
            for dst, src in ((win, win_d), (lnw, lnw_d), (lnb, lnb_d), (cw, cw_d), (cb, cb_d), (dd, dd_d),
                             (rms, rms_d), (wout, wout_d), (wr, wr_d), (gam, gam_d), (bet, bet_d),
                             (w1, w1_d), (w2, w2_d[0]), (nestf, nest_d), (rowm, row_d), (later, later_d),
                             (upto, upto_d)):
                sp.dma_start(dst[:], src).then_inc(w_rest, 16)
            for dst, src in ((dtb, dtb_d), (aneg, alog_d), (b2, b2_d[0]), (b2x, b2_d[1])):
                n = dst.shape[1]
                sp.dma_start(dst[:], src.rearrange("(a n) -> a n", a=1).broadcast_to([128, n])).then_inc(w_rest, 16)

            def stack_q(c, p):
                for r, part in ((0, 0), (2, 0), (1, 1)):
                    if r == 0:
                        sp.wait_ge(q_split, c + 1)
                    if r == 1:
                        sp.wait_ge(q_low, c * 2 + 2)
                    for pair in range(PAIRS // 2):
                        sp.dma_start(qst[p][32 * r:32 * r + 32, pair:PAIRS:PAIRS // 2, :].bitcast(F32),
                                     qmhl[32 * pair:32 * pair + 32, part].bitcast(F32)).then_inc(q_stacked[p], 16)

            def stack_k(c, tb):
                if tb == 0 or isinstance(c, int) and c == 0:
                    sp.wait_ge(k_split, c * 4 + 2 * tb + 2)
                else:
                    sp.wait_ge(s_done, c * U + 1)
                for r, part in enumerate((0, 0, 1)):
                    for pair in range(PAIRS // 2):
                        sp.dma_start(kst[32 * r:32 * r + 32, pair:PAIRS:PAIRS // 2, tb * 512:(tb + 1) * 512].bitcast(F32),
                                     khl[32 * pair:32 * pair + 32, part, :, tb * 512:(tb + 1) * 512].bitcast(F32)
                                     ).then_inc(k_stacked[tb], 16)

            def load_x(c, p):
                sp.wait_ge(x_used, c - 1)
                sp.dma_start(xT[p][0:HC], x[bass.ds(c, 1)].rearrange("b p a n -> p (b a) n")).then_inc(x_loaded[p], 16)

            def stage1(b, p):
                stack_q(b + 1, 1 - p)
                stack_k(b + 1, 0)
                if not isinstance(b, int) or b + 3 < B:
                    load_x(b + 3, 1 - p)
                stack_k(b + 1, 1)

            sp.wait_ge(consts, 7)
            stack_q(0, 0)
            stack_k(0, 0)
            load_x(2, 0)
            stack_k(0, 1)
            stage1(0, 0)
            with sp.Fori(0, B // 2 - 2) as i:
                stage1(i * 2 + 1, 1)
                stage1(i * 2 + 2, 0)
            stage1(B - 3, 1)
            stage1(B - 2, 0)
            sp.wait_ge(x_used, B)
            sp.dma_start(w2x, w2_d[1]).then_inc(w2x_loaded, 16)

            def store(b, p):
                sp.wait_ge(res_ready, b + 1)
                sp.dma_start(out[bass.ds(b, 1)].rearrange("b (t p) c -> p (b t) c", p=128), res2[:]).then_inc(stored[p], 16)

            def stack3_q(c, p, pair, signal):
                for r, part in enumerate((0, 1, 0)):
                    for e in range(2):
                        h = 2 * pair + e
                        sp.dma_start(qst3[p][32 * r + D * e:32 * r + D * (e + 1), pair:PAIRS:PAIRS // 2, e, :].bitcast(F32),
                                     qhl[D * h:D * (h + 1), part].bitcast(F32)).then_inc(signal, 16)

            def stack3_k(c, p, pair, signal):
                for r, part in enumerate((0, 0, 1)):
                    sp.dma_start(kst3[p][32 * r:32 * r + 32, pair:PAIRS:PAIRS // 2, :].bitcast(F32),
                                 khl3[32 * pair:32 * pair + 32, part].bitcast(F32)).then_inc(signal, 16)

            def stack3(c, p):
                sp.wait_ge(q3_split, c + 1)
                for pair in range(PAIRS // 2):
                    stack3_q(c, p, pair, qk3_stacked[p])
                sp.wait_ge(k3_split, c + 1)
                for pair in range(PAIRS // 2):
                    stack3_k(c, p, pair, qk3_stacked[p])

            def stage3(b, p):
                stack3(b + 1, 1 - p)
                if not (isinstance(b, int) and b == 0):
                    store(b - 1, 1 - p)

            sp.wait_ge(zeros3, 2)
            sp.wait_ge(q3_split, 1)
            for pair in range(PAIRS // 2):
                stack3_q(0, 0, pair, first3[pair])
                if pair == 0:
                    sp.wait_ge(k3_split, 1)
                stack3_k(0, 0, pair, first3[pair])
            stage3(0, 0)
            with sp.Fori(0, B // 2 - 1) as i:
                stage3(i * 2 + 1, 1)
                stage3(i * 2 + 2, 0)
            store(B - 2, 0)
            store(B - 1, 1)
            for p in range(2):
                sp.wait_ge(stored[p], 16 * (B // 2))
        W_FIRST, W_REST = 16 * 6, 16 * 21
        K_BANKS = (0, 1, 0, 1)
        QD, KD, QD3 = 3 * PAIRS // 2, 3 * PAIRS // 2, 3 * HH

        @block.tensor
        def _(pe):
            HEADS3 = [2 * pair + e for j in range(3) for pair in (j, j + 3) for e in range(2)]

            def unit_scores1(c_par, u):
                w, r = divmod(u, 3)
                for i in range(2):
                    last = nc.tensor.matmul(
                        ps[:, SC + u % 3, i * 256:(i + 1) * 256],
                        qst[c_par][:, 2 * r + i, w * 2 * QW:(w + 1) * 2 * QW],
                        kst[:, 2 * r + i, w * KW:(w + 1) * KW], start=True, stop=True)
                last.then_inc(s_done, 1)

            def unit_scores3(c_par, u):
                pair, e = divmod(HEADS3[u], 2)
                for i in range(2):
                    last = nc.tensor.matmul(
                        ps[:, SC + u % 3, i * 256:(i + 1) * 256],
                        qst3[c_par][:, pair, e, i * 128:(i + 1) * 128],
                        kst3[c_par][:, pair, :], start=True, stop=True)
                last.then_inc(s_done, 1)

            def unit_turn(u):
                for kc in range(2):
                    for i in range(2):
                        last = nc.tensor.transpose(
                            ps[:, TR, kc * 256 + i * 128:kc * 256 + (i + 1) * 128],
                            prob[:, u % 3, i * 256 + kc * 128:i * 256 + (kc + 1) * 128], eye[:])
                last.then_inc(t_done, 1)

            def unit_pv1(p, u):
                w, r = divmod(u, 3)
                for kc in range(2):
                    for j in range(4):
                        last = nc.tensor.matmul(
                            psO[32 * j:32 * j + 32, r * L + w * QW:r * L + (w + 1) * QW],
                            va[:, 2 * w + kc, 4 * r + j, :],
                            probT[:, u % 3, kc * 256 + j * QW:kc * 256 + (j + 1) * QW],
                            start=(kc == 0), stop=(kc == 1), tile_position=(0, 32 * j))
                last.then_inc(pv_done, 1)

            def unit_pv3(p, u):
                g, j = divmod(HEADS3[u], 4)
                for kc in range(2):
                    last = nc.tensor.matmul(
                        psO[32 * j:32 * j + 32, g * L:(g + 1) * L], va3[p][:, kc, HEADS3[u], :],
                        probT[:, u % 3, kc * 256:(kc + 1) * 256],
                        start=(kc == 0), stop=(kc == 1), tile_position=(0, 32 * j))
                last.then_inc(pv_done, 1)

            PARTS = ((0, 0), (0, 1), (1, 0))

            def qk_product(p, col, tb, bank, split):
                cols, toks = slice(col, col + HC), slice(tb * 512, (tb + 1) * 512)
                if not split:
                    for a in range(2):
                        last = nc.tensor.matmul(ps[0:HC, bank, :], wqkv[0:HC + a, a, cols], xT[p][0:HC + a, a, toks],
                                                start=(a == 0), stop=(a == 1))
                    return last
                for n, (u, v) in enumerate(PARTS):
                    for a in range(2):
                        last = nc.tensor.matmul(ps[0:HC, bank, :], whl[0:HC + a, u, a, cols],
                                                xhl[0:HC + a, v, a, toks],
                                                start=(n == 0 and a == 0), stop=(n == 2 and a == 1))
                return last

            def q_piece(p, k, bank, split):
                half, tb = divmod(k, 2)
                qk_product(p, half * HC, tb, bank, split).then_inc(q_done, 1)

            def k_piece(p, k, bank, split):
                tb, half = divmod(k, 2)
                qk_product(p, C + half * HC, tb, bank, split).then_inc(k_done, 1)

            def v_piece(p, k, bank):
                for i in range(2):
                    t = 2 * k + i
                    for a in range(2):
                        last = nc.tensor.matmul(ps[:, bank, i * C:(i + 1) * C],
                                                xT[p][0:HC + a, a, t * 128:(t + 1) * 128],
                                                wqkv[0:HC + a, a, 2 * C:3 * C],
                                                start=(a == 0), stop=(a == 1))
                last.then_inc(v_done, 1)
                return last

            def h_piece(t):
                for g in range(G3):
                    last = nc.tensor.matmul(psH, oT[:, g, t * 128:(t + 1) * 128], wo[:, g, :],
                                            start=(g == 0), stop=(g == G3 - 1))
                last.then_inc(h_done, 1)

            def project(c, p, k, first):
                if first and k == 1:
                    pe.wait_ge(x_loaded[0], 16)
                if not first and k == 0:
                    pe.wait_ge(x_low, c * 4)
                    pe.wait_ge(w_low, 1)
                if k < 2:
                    if not first:
                        pe.wait_ge(v_ready, c * 4 - 1 + k)
                elif k < 6:
                    pe.wait_ge(q_pooled, c * 4 + k - 1)
                elif k < 10:
                    pe.wait_ge(k_split, c * 4 + k - 5)
                else:
                    pe.wait_ge(v_ready, c * 4 + k - 9)
                if k < 4:
                    q_piece(p, k, k % 2, not first)
                elif k < 8:
                    k_piece(p, k - 4, k % 2, not first)
                else:
                    v_piece(p, k - 8, k % 2)
                if k == 11:
                    pe.wait_ge(v_done, c * 4 + 4)
                    pe.sem_inc(x_used, 1)

            def output1(b, t):
                if t == 0:
                    pe.wait_ge(ot_ready, b + 1)
                else:
                    pe.wait_ge(h_ready, b * 2 + 1)
                h_piece(t)

            def wait_q(c, p):
                pe.wait_ge(q_stacked[p], (c // 2 + 1) * 16 * QD if isinstance(c, int) else (c - p) * 8 * QD + 16 * QD)

            def stage1(b, p):
                last = isinstance(b, int) and b == B - 1
                first = isinstance(b, int) and b == 0
                for u in range(U):
                    if u < U - 2:
                        if not (first and u == 0):
                            pe.wait_ge(exp_done, b * U + u)
                        if u + 2 == U // 2:
                            pe.wait_ge(k_stacked[1], (b + 1) * 16 * KD)
                        unit_scores1(p, u + 2)
                    elif not last:
                        pe.wait_ge(exp_done, b * U + u)
                        if u == U - 2:
                            wait_q(b + 1, 1 - p)
                            pe.wait_ge(k_stacked[0], (b + 2) * 16 * KD)
                        unit_scores1(1 - p, u + 2 - U)
                    if not last:
                        project(b + 1, 1 - p, u, False)
                    pe.wait_ge(exp_done, b * U + u + 1)
                    if not (first and u == 0):
                        pe.wait_ge(pt_ready, b * U + u)
                    unit_turn(u)
                    if u == 0:
                        if not first:
                            unit_pv1(1 - p, U - 1)
                    else:
                        if u == 1:
                            pe.wait_ge(v_ready, b * 4 + 4)
                            if not first:
                                pe.wait_ge(o_read, b)
                        if u in (6, 9) and not first:
                            pe.wait_ge(h_ready, (b - 1) * 2 + u // 3 - 1)
                        unit_pv1(p, u - 1)
                    if u in (4, 7) and not first:
                        output1(b - 1, u // 7)

            pe.wait_ge(x_first, 32)
            pe.wait_ge(consts, 3)
            for k in range(U):
                if k == 4:
                    pe.wait_ge(w_first, W_FIRST)
                project(0, 0, k, True)
            wait_q(0, 0)
            pe.wait_ge(k_stacked[0], 16 * KD)
            unit_scores1(0, 0)
            unit_scores1(0, 1)
            over_batches(pe, stage1)
            pe.wait_ge(pt_ready, B * U)
            unit_pv1(1, U - 1)

            B2, B3 = TR2, TR2 + 1

            def turn_x(b, p):
                pe.wait_ge(xh_ready, b + 1)
                if not (isinstance(b, int) and b < 4):
                    pe.wait_ge(yhT_ready, b - 3)
                for half in range(2):
                    for t in range(T2):
                        last = nc.tensor.transpose(ps[0:HC, B2, half * L + t * 128:half * L + (t + 1) * 128],
                                                   xh[:, p, t, half * HC:(half + 1) * HC], eye[:])
                last.then_inc(xt_done, 1)

            def project_dt(b):
                if isinstance(b, int) and b == 0:
                    pe.wait_ge(h_ready, 2 * B)
                if not (isinstance(b, int) and b < 2):
                    pe.wait_ge(y_ready, b - 1)
                for t in range(T2):
                    for half in range(2):
                        last = nc.tensor.matmul(psDt[:, t * SH:(t + 1) * SH], xnT[:, half, t * 128:(t + 1) * 128],
                                                win[:, half, ZXD - SH:ZXD], start=(half == 0), stop=(half == 1))
                last.then_inc(dt_done, 1)

            def project_zx(b, k):
                if k == 0:
                    pe.wait_ge(xn_ready, b * 2 + 2)
                if not (isinstance(b, int) and b == 0 and k < 2):
                    pe.wait_ge(zx_read, b * 4 + k - 1)
                for i in range(2 if k < 3 else 1):
                    j = (XC + 2 * k + i) % (XC + TAPS)
                    for half in range(2):
                        last = nc.tensor.matmul(ps[:, k % 2, i * L:(i + 1) * L],
                                                win[:, half, j * 128:(j + 1) * 128], xnT[:, half, :],
                                                start=(half == 0), stop=(half == 1))
                last.then_inc(zx_done, 1)

            def turn_tok(b, p, t):
                for c in range(XC):
                    last = nc.tensor.transpose(ps[:, B3, c * 128:(c + 1) * 128],
                                               xc[:, p, c, t * 128:(t + 1) * 128], eye[:])
                last.then_inc(tok_done, 1)

            def decay(lhs, tile_):
                for i in range(2):
                    last = nc.tensor.matmul(ps[:, SC2 + i, 0:384], lhs,
                                            a1[:, tile_, 3 * i:3 * i + 3, :].rearrange("p h t -> p (h t)"),
                                            start=True, stop=True)
                last.then_inc(seg_done, 1)

            def mid_first(b, p):
                pe.wait_ge(xc_ready, b + 1)
                if not (isinstance(b, int) and b < 2):
                    pe.wait_ge(h2_ready, b - 1)
                turn_tok(b, p, 0)
                pe.wait_ge(a1_ready, b * 2 + 2)
                if not (isinstance(b, int) and b == 0):
                    pe.wait_ge(dec_ready, b * 3)
                decay(later[:], 0)
                if not (isinstance(b, int) and b == B - 1):
                    pe.wait_ge(dt_step, b * 9 + 10)
                elif b:
                    pe.wait_ge(y_ready, b)
                nc.tensor.matmul(psSuf, later[:], a2[:, p, 0, :], start=True, stop=True).then_inc(suf_done, 1)
                pe.wait_ge(xdt_ready, b * 3 + 1)
                turn_tok(b, p, 1)

            def mid_last(b):
                pe.wait_ge(dec_ready, b * 3 + 1)
                decay(later[:], 1)
                pe.wait_ge(xdt_ready, b * 3 + 2)
                nc.tensor.matmul(ps[:, B3, 0:256], bcT[:, 0, 0:128], bcT[:, 1, :], start=True, stop=True)
                nc.tensor.matmul(ps[:, B3, 256:384], bcT[:, 0, 128:256], bcT[:, 1, 128:256],
                                 start=True, stop=True).then_inc(g_done, 1)
                pe.wait_ge(dec_ready, b * 3 + 2)
                decay(ones[:], 1)

            def mix_y(b):
                pe.wait_ge(mix_ready, b * 3 + 3)
                if not (isinstance(b, int) and b == 0):
                    pe.wait_ge(y_ready, b)
                if not (isinstance(b, int) and b < 2):
                    pe.wait_ge(lg_ready, b - 1)
                for hp in range(XC):
                    for i in range(2):
                        h = 2 * hp + i
                        o = psY[64 * i:64 * i + 64, hp * L:(hp + 1) * L]
                        nc.tensor.matmul(o[:, 0:128], xdt[:, 0, h, :], mix[:, 0, h, :], start=True, stop=True,
                                         tile_position=(0, 64 * i))
                        nc.tensor.matmul(o[:, 128:256], xdt[:, 1, h, :], mix[:, 2, h, :], start=True, stop=False,
                                         tile_position=(0, 64 * i))
                        last = nc.tensor.matmul(o[:, 128:256], xdt[:, 2, h, :], mix[:, 1, h, :], start=False,
                                                stop=True, tile_position=(0, 64 * i))
                last.then_inc(y_done, 1)

            def output2(b):
                pe.wait_ge(gsq_ready, b + 1)
                pe.wait_ge(gm_ready, B if isinstance(b, int) and b == B - 1 else b + 2)
                for t in range(T2):
                    for c in range(XC):
                        nc.tensor.matmul(ps[:, B3, t * C:(t + 1) * C], gt[:, c, t * 128:(t + 1) * 128],
                                         wout[:, c, :], start=(c == 0), stop=(c == XC - 1))
                    for c in range(XC):
                        last = nc.tensor.matmul(ps[:, B3, 2 * C + t:2 * C + t + 1], gsq[:, c, t * 128:(t + 1) * 128],
                                                ones[:, 0:1], start=(c == 0), stop=(c == XC - 1))
                last.then_inc(o2_done, 1)

            def turn_y(b):
                pe.wait_ge(yh_ready, b + 1)
                for half in range(2):
                    for t in range(T2):
                        last = nc.tensor.transpose(ps[0:HC, B2, half * L + t * 128:half * L + (t + 1) * 128],
                                                   uu[:, t, half * HC:(half + 1) * HC], eye[:])
                last.then_inc(yt_done, 1)

            def route(b):
                pe.wait_ge(suf_ready, b + 3 if not isinstance(b, int) or b + 3 < B else B)
                pe.wait_ge(yhT_ready, b + 1)
                for t in range(T2):
                    for half in range(2):
                        last = nc.tensor.matmul(psLg[:, t * E:(t + 1) * E], yhT[:, half, t * 128:(t + 1) * 128],
                                                wr[:, half, :], start=(half == 0), stop=(half == 1))
                last.then_inc(lg_done, 1)

            def stage2(s, p):
                project, next_x, mixing, output, routing = parts2(s)
                if project:
                    project_zx(s, 0)
                    project_zx(s, 1)
                    project_dt(s)
                    project_zx(s, 2)
                if mixing:
                    mid_first(s - 1, 1 - p)
                if routing:
                    turn_y(s - 3)
                if project:
                    project_zx(s, 3)
                if mixing:
                    mid_last(s - 1)
                if routing:
                    route(s - 3)
                if next_x:
                    turn_x(s + 1, 1 - p)
                if output:
                    output2(s - 2)
                if mixing:
                    mix_y(s - 1)

            pe.wait_ge(w_rest, W_REST)
            turn_x(0, 0)
            output1(B - 1, 0)
            output1(B - 1, 1)
            over_stages2(pe, stage2)

            pe.wait_ge(ch_step, 6)
            for t in range(T2):
                last = nc.tensor.transpose(ps[0:32, 0, t * 128:(t + 1) * 128],
                                           pe_[:, t * B:(t + 1) * B, :].rearrange("p b e -> p (b e)"), eye[:])
            last.then_inc(pr_done, 1)

            def linear1(p, where, cols):
                for n, (u, v) in enumerate(PARTS):
                    for a in range(2):
                        last = nc.tensor.matmul(where, w1hl[0:HC + a, u, a, cols], yhl[p][0:HC + a, v, a, :],
                                                start=(n == 0 and a == 0), stop=(n == 2 and a == 1))
                return last

            def project3(c, k, bank, p):
                first = isinstance(c, int) and c == 0
                if k == 0:
                    pe.wait_ge(selb_ready, c + 1)
                    if isinstance(c, int) and c == 1:
                        pe.wait_ge(m3_read, 3)
                    elif not first:
                        pe.wait_ge(k3_split, c)
                    for half in range(2):
                        last = nc.tensor.matmul(ps[0:HC + 1, bank, half * L:(half + 1) * L],
                                                nest[:, half * (HC + 1):(half + 1) * (HC + 1)], selb[:],
                                                start=True, stop=True)
                    last.then_inc(m_done, 1)
                elif k in (1, 2):
                    pe.wait_ge(yhat_split, c + 1)
                    if not first:
                        pe.wait_ge(m3_read, c * 3 - 2 + k)
                    at = MLP + (k - 1) * C
                    for half in range(2):
                        last = linear1(p, ps[0:HC, bank, half * L:(half + 1) * L],
                                       slice(at + half * HC, at + (half + 1) * HC))
                    last.then_inc(q3_done if k == 1 else k3_done, 1)
                elif k == 3:
                    pe.wait_ge(q3_split, c + 1)
                    for t in range(T2):
                        for a in range(2):
                            last = nc.tensor.matmul(ps[:, bank, t * C:(t + 1) * C],
                                                    yhat[0:HC + a, a, t * 128:(t + 1) * 128],
                                                    w1[0:HC + a, a, MLP + 2 * C:MLP + 3 * C],
                                                    start=(a == 0), stop=(a == 1))
                    last.then_inc(v3_done, 1)
                else:
                    j = k - 4
                    if j == 0:
                        if first or isinstance(c, int) and c == B - 1:
                            pe.wait_ge(k3_split, c + 1)
                        else:
                            pe.wait_ge(yhat_ready, c + 2)
                    if j == 1:
                        pe.wait_ge(v3_ready, c + 1)
                        if not (isinstance(c, int) and c < 2):
                            pe.wait_ge(f_read, c * 2 - 2)
                    if j == 2:
                        pe.wait_ge(m3_read, c * 3 + 1)
                    for i in range(2):
                        m = 2 * j + i
                        last = linear1(p, ps[:, bank, i * L:(i + 1) * L], slice(m * 128, (m + 1) * 128))
                    last.then_inc(m3_done, 1)

            def output3(b, p, t, part):
                if part == 1:
                    if t == 0:
                        pe.wait_ge(ot_ready, B + b + 1)
                    for j in range(MJ - 2, MJ):
                        nc.tensor.matmul(ps[:, 0, 0:C], y2T[p][:, j, t * 128:(t + 1) * 128], w2[:, j, :],
                                         start=False, stop=False)
                    for g in range(G3):
                        nc.tensor.matmul(ps[:, 0, 0:C], oT[:, g, t * 128:(t + 1) * 128], w2[:, MJ + g, :],
                                         start=False, stop=(g == G3 - 1))
                    nc.tensor.matmul(ps[:, 0, C:2 * C], gselb[:, p, t * 128:(t + 1) * 128],
                                     nestf[:, 2 * (HC + 1):2 * (HC + 1) + C], start=True,
                                     stop=True).then_inc(f_done, 1)
                    return
                if t == 0:
                    if isinstance(b, int) and b + 2 >= B:
                        pe.wait_ge(m3_read, 3 * B)
                    else:
                        pe.wait_ge(v3_ready, b + 3)
                    pe.wait_ge(gelu_done, b + 1)
                    pe.wait_ge(gates_ready, b + 1)
                else:
                    pe.wait_ge(f_read, b * 2 + 1)
                for j in range(MJ - 2):
                    nc.tensor.matmul(ps[:, 0, 0:C], y2T[p][:, j, t * 128:(t + 1) * 128], w2[:, j, :],
                                     start=(j == 0), stop=False)

            PIECES = {0: (1, 0), 1: (2, 1), 3: (3, 0), 9: (4, 1), 10: (5, 0), 11: (6, 1)}

            def wait_qk3(c, p):
                each = 16 * (QD3 + KD)
                pe.wait_ge(qk3_stacked[p], (c + p) * (each // 2))

            def stage3(b, p):
                last = isinstance(b, int) and b == B - 1
                first = isinstance(b, int) and b == 0
                n0 = B * U + b * U
                for u in range(U):
                    pe.wait_ge(exp_done, n0 + u)
                    if u < U - 2:
                        if first and u in (2, 6):
                            pe.wait_ge(first3[(u + 2) // 4], 16 * 9)
                        unit_scores3(p, u + 2)
                    elif not last:
                        if u == U - 2:
                            wait_qk3(b + 1, 1 - p)
                        unit_scores3(1 - p, u + 2 - U)
                    if not last and u in PIECES:
                        project3(b + 1, *PIECES[u], 1 - p)
                    if u == 5 and not last and not (isinstance(b, int) and b == B - 2):
                        project3(b + 2, 0, 1, p)
                    pe.wait_ge(exp_done, n0 + u + 1)
                    pe.wait_ge(pt_ready, n0 + u)
                    unit_turn(u)
                    if u == 0:
                        if not first:
                            unit_pv3(1 - p, U - 1)
                    else:
                        if u == 1:
                            pe.wait_ge(v3_ready, b + 1)
                            pe.wait_ge(vones, 1)
                            pe.wait_ge(o_read, B + b)
                        unit_pv3(p, u - 1)
                    if u in (4, 5, 6, 7) and not first:
                        output3(b - 1, 1 - p, *divmod(u - 4, 2))

            pe.wait_ge(w1_low, 1)
            pe.wait_ge(w2_ready, 3)
            project3(0, 0, 1, 0)
            for k, bank in PIECES.values():
                project3(0, k, bank, 0)
            project3(1, 0, 1, 1)
            pe.wait_ge(first3[0], 16 * 9)
            unit_scores3(0, 0)
            unit_scores3(0, 1)
            over_split_batches(pe, stage3)
            pe.wait_ge(pt_ready, 2 * B * U)
            unit_pv3(1, U - 1)
            for t in range(T2):
                for part in range(2):
                    output3(B - 1, 1, t, part)

        @block.vector
        def _(dve):
            def unit_max(n, slot):
                dve.wait_ge(s_done, n + 1)
                if not isinstance(n, int) or n >= 4:
                    dve.wait_ge(exp_done, n - 3)
                nc.vector.tensor_reduce(nmax[:, slot % 4, :],
                                        ps[:, SC + slot % 3, :].rearrange("p (a n) -> p a n", a=2),
                                        AX.X, ALU.max, negate=True).then_inc(max_done, 1)

            def unit_copy(n, u):
                dve.wait_ge(t_done, n + 1)
                if not isinstance(n, int) or n >= 3:
                    dve.wait_ge(pv_done, n - 2)
                nc.vector.tensor_copy(probT[:, u % 3, :], ps[:, TR, :]).then_inc(pt_ready, 1)

            def sums_beside(b):
                dve.wait_ge(pv_done, b * U + U)
                nc.vector.transpose(otA[:], psO).then_inc(o_read, 1)

            def normalise(b, tokens_inner):
                dve.wait_ge(o_read, b + 1)
                blocks = otA[:].rearrange("p (k e) -> p k e", e=32)
                nc.vector.reciprocal(rsum[:], blocks[:, :, D]).then_inc(ot_sum, 1)
                dve.wait_ge(ot_sum, b + 1)
                nc.vector.tensor_tensor(blocks[:, :, 0:D], blocks[:, :, 0:D],
                                        rsum[:].unsqueeze(2).broadcast_to([128, G3 * L // 32, D]),
                                        ALU.mult).then_inc(ot_norm, 1)
                dve.wait_ge(ot_norm, b + 1)
                if tokens_inner:
                    nc.vector.transpose(oT[:].rearrange("p g n -> p (g n)"), otA[:]).then_inc(ot_ready, 1)
                else:
                    for g in range(G3):
                        last = nc.vector.transpose(
                            oT[:, g, :].rearrange("p (q w) -> p w q", w=W),
                            otA[:, g * L:(g + 1) * L].rearrange("p (w q) -> p w q", w=W))
                    last.then_inc(ot_ready, 1)

            def pool_q(c, k, bank):
                half, tb = divmod(k, 2)
                dve.wait_ge(q_done, c * 4 + k + 1)
                if not (isinstance(c, int) and c == 0):
                    dve.wait_ge(q_low, c * 2)
                nc.vector.tensor_reduce(
                    qp[:, half, tb * 128:(tb + 1) * 128].rearrange("p (w j) -> p w j", w=2),
                    ps[0:HC, bank, :].rearrange("p (w s j) -> p w j s", w=2, s=STRIDE),
                    AX.X, ALU.max).then_inc(q_pooled, 1)

            def low_q(c):
                dve.wait_ge(q_high, c + 1)
                flat = [a.rearrange("p a n -> p (a n)") for a in (qhl[:, 1], qp[:], qhl[:, 0])]
                nc.vector.tensor_tensor(flat[0], flat[1], flat[2].bitcast(F32), ALU.subtract).then_inc(q_low, 1)
                dve.wait_ge(q_low, c * 2 + 1)
                for half in range(2):
                    last = nc.vector.tensor_tensor(
                        qmhl[:, 1, half, :].rearrange("p (w e q) -> p w e q", w=W, e=2),
                        qhl[:, 1, half, :].bitcast(F32).rearrange("p (w q) -> p w q", w=W).unsqueeze(2)
                        .broadcast_to([HC, W, 2, QW]),
                        hm[:].unsqueeze(1).unsqueeze(3).broadcast_to([HC, W, 2, QW]), ALU.mult)
                last.then_inc(q_low, 1)

            def low_k(c, k, bank):
                tb, half = divmod(k, 2)
                dve.wait_ge(k_ready, c * 4 + k + 1)
                where = slice(tb * 512, (tb + 1) * 512)
                nc.vector.scalar_tensor_tensor(khl[:, 1, half, where], ps[0:HC, bank, :], SCALE,
                                               khl[:, 0, half, where].bitcast(F32), ALU.mult,
                                               ALU.subtract).then_inc(k_split, 1)

            def take_h(b, t):
                dve.wait_ge(h_done, b * 2 + t + 1)
                nc.vector.tensor_tensor(h_all[:, tile(b, t), :].rearrange("p a c -> p (a c)"), psH, bo[:],
                                        ALU.add).then_inc(h_ready, 1)

            def stats1(b):
                dve.wait_ge(consts, 1)
                dve.wait_ge(h_ready, b * 2 + 2)
                for t in range(T2):
                    last = nc.vector.bn_stats(st6[:, t, :], h_all[:, tile(b, t), :].rearrange("p a c -> p (a c)"))
                last.then_inc(bn_done, 1)
                dve.wait_ge(consts, 1)
                dve.wait_ge(bn_done, b + 1)
                if not (isinstance(b, int) and b == 0):
                    dve.wait_ge(stat_done, b)
                for t in range(T2):
                    last = nc.vector.bn_aggr(mv[:, t, :], st6[:, t, :])
                last.then_inc(mv_done, 1)
                dve.wait_ge(mv_done, b + 1)
                nc.vector.tensor_copy(mean_all[:, bass.ds(b * T2, T2)], mv[:, :, 0])
                nc.vector.tensor_scalar(ve[:], mv[:, :, 1], 1e-5, None, ALU.add).then_inc(ve_done, 1)

            def stage1(b, p):
                last = isinstance(b, int) and b == B - 1
                first = isinstance(b, int) and b == 0
                for u in range(U):
                    if u == 1 and not first:
                        sums_beside(b - 1)
                    if u == 2 and not first:
                        normalise(b - 1, False)
                    if u < U - 2 or not last:
                        unit_max(b * U + u + 2, u + 2)
                    if u < 4 and not last:
                        pool_q(b + 1, u, u % 2)
                    unit_copy(b * U + u, u)
                    if u == 4 and not last:
                        low_q(b + 1)
                    if 4 <= u < 8 and not last:
                        low_k(b + 1, u - 4, K_BANKS[u - 4])
                    if u in (4, 7) and not first:
                        take_h(b - 1, u // 7)
                    if u == 8 and not first:
                        stats1(b - 1)

            for k in range(4):
                pool_q(0, k, k % 2)
            low_q(0)
            for k in range(4):
                low_k(0, k, K_BANKS[k])
            unit_max(0, 0)
            unit_max(1, 1)
            over_batches(dve, stage1)
            def normal_x(b, p):
                dve.wait_ge(stat_done, b + 1)
                if not (isinstance(b, int) and b == 0):
                    dve.wait_ge(hu_done, b)
                for t in range(T2):
                    h = h_all[:, tile(b, t), :].rearrange("p a c -> p (a c)")
                    nc.vector.tensor_scalar(uu2[:, t, :], h, mean_all[:, tile(b, t)], r1_all[:, tile(b, t)],
                                            ALU.subtract, ALU.mult)
                    last = nc.vector.tensor_scalar(xh[:, p, t, :], h, mean_all[:, tile(b, t)], rr_all[:, tile(b, t)],
                                                   ALU.subtract, ALU.mult)
                last.then_inc(xh_ready, 1)

            k = [small[:, i, :] for i in range(9)]

            def step_sizes_v(b):
                v3 = small[:, 0, :].rearrange("p (t h) -> p t h", t=T2)
                dve.wait_ge(dt_done, b + 1)
                nc.vector.tensor_tensor(v3, psDt.rearrange("p (t h) -> p t h", t=T2),
                                        dtb[:].unsqueeze(1).broadcast_to([128, T2, SH]), ALU.add).then_inc(dt_step, 1)
                dve.wait_ge(dt_step, b * 9 + 1)
                nc.vector.scalar_tensor_tensor(k[1], k[0], -1.0, k[0], ALU.mult, ALU.max).then_inc(dt_step, 1)

            def step_sizes_e(b):
                at = b * 9
                dve.wait_ge(dt_exp, b + 1)
                nc.vector.tensor_scalar(k[3], k[2], 1.0, None, ALU.add).then_inc(dt_step, 1)
                dve.wait_ge(dt_step, at + 3)
                nc.vector.scalar_tensor_tensor(k[5], k[3], -1.0, k[2], ALU.add, ALU.subtract).then_inc(dt_step, 1)
                nc.vector.reciprocal(k[6], k[3]).then_inc(dt_step, 1)
                dve.wait_ge(dt_step, at + 5)
                nc.vector.tensor_tensor(k[7], k[5], k[6], ALU.mult).then_inc(dt_step, 1)

            def step_sizes_a(b, p):
                at = b * 9
                dve.wait_ge(dt_step, at + 6)
                dve.wait_ge(dt_log, b + 1)
                nc.vector.tensor_tensor(k[8], k[4], k[7], ALU.subtract).then_inc(dt_step, 1)
                dve.wait_ge(dt_step, at + 7)
                dtf = dt2[:, p].rearrange("p t h -> p (t h)")
                nc.vector.scalar_tensor_tensor(dtf, k[0], 0.0, k[8], ALU.max, ALU.add).then_inc(dt_step, 1)
                dve.wait_ge(dt_step, at + 8)
                nc.vector.tensor_tensor(a2[:, p], dt2[:, p], aneg[:].unsqueeze(1).broadcast_to([128, T2, SH]),
                                        ALU.mult).then_inc(dt_step, 1)

            def convolve(b, j):
                at = b * 16 + j * 8
                for k in range(TAPS):
                    for i in range(2):
                        c = 2 * j + i
                        if k == 0:
                            dve.wait_ge(xp_ready, b * 4 + 2 * j + 2)
                            if c == 0 and not (isinstance(b, int) and b == 0):
                                dve.wait_ge(xc_ready, b)
                            nc.vector.tensor_scalar(acc[:, c, :], xpad[:, c, 4:4 + L], cw[:, c, 3:4],
                                                    cb[:, c:c + 1], ALU.mult, ALU.add).then_inc(conv_step, 1)
                        else:
                            dve.wait_ge(conv_step, at + 2 * k + i - 1)
                            nc.vector.scalar_tensor_tensor(acc[:, c, :], xpad[:, c, k:k + L], cw[:, c, k - 1:k],
                                                           acc[:, c, :], ALU.mult, ALU.add).then_inc(conv_step, 1)

            def weigh_x(b, p, t):
                dve.wait_ge(tok_done, b * 2 + t + 1)
                if t == 0 and not (isinstance(b, int) and b == 0):
                    dve.wait_ge(y_done, b)
                nc.vector.tensor_tensor(xdt[:, 2 * t, :, :],
                                        ps[:, 3, 0:INNER].rearrange("p (h q) -> p h q", h=SH),
                                        dt2[:, p, t, :].unsqueeze(2).broadcast_to([128, SH, 64]),
                                        ALU.mult).then_inc(xdt_ready, 1)

            def decay_x(b):
                dve.wait_ge(suf_ready, b + 1)
                dve.wait_ge(xdt_ready, b * 3 + 1)
                nc.vector.tensor_tensor(xdt[:, 1, :, :], xdt[:, 0, :, :],
                                        esuf[:].unsqueeze(2).broadcast_to([128, SH, 64]),
                                        ALU.mult).then_inc(xdt_ready, 1)

            def mask_g(b):
                dve.wait_ge(g_done, b + 1)
                cut3 = ps[:, 3, 0:384].rearrange("p (a t) -> p a t", a=3)
                nc.vector.tensor_tensor(gmask[:, 0, :], cut3[:, 0, :], upto[:], ALU.mult)
                nc.vector.tensor_copy(gmask[:, 1, :], cut3[:, 1, :])
                nc.vector.tensor_tensor(gmask[:, 2, :], cut3[:, 2, :], upto[:], ALU.mult).then_inc(gm_ready, 1)
                dve.wait_ge(gm_ready, b + 1)

            def mix_decays(b, p):
                for i, g in enumerate((0, 2, 1)):
                    dve.wait_ge(dec_ready, b * 3 + i + 1)
                    nc.vector.tensor_tensor(mix[:, i], dec[(i + p) % 2],
                                            gmask[:, g, :].unsqueeze(1).broadcast_to([128, SH, 128]),
                                            ALU.mult).then_inc(mix_ready, 1)

            def take_y(b, p):
                dve.wait_ge(y_done, b + 1)
                if not (isinstance(b, int) and b == 0):
                    dve.wait_ge(gt_ready, b)
                for c in range(XC):
                    last = nc.vector.scalar_tensor_tensor(y2[:, c, :], xc[:, p, c, :], dd[:, c:c + 1],
                                                          psY[:, c * L:(c + 1) * L], ALU.mult, ALU.add)
                last.then_inc(y_ready, 1)

            def mean_square(b):
                dve.wait_ge(o2_done, b + 1)
                nc.vector.tensor_scalar(ms[:], ps[:, 3, 2 * C:2 * C + 2], 1.0 / INNER, 1e-5,
                                        ALU.mult, ALU.add).then_inc(ms_done, 1)

            def take_h2(b):
                dve.wait_ge(rt_done, b + 1)
                dve.wait_ge(hu_done, b + 1)
                if not (isinstance(b, int) and b == 0):
                    dve.wait_ge(h2_used, b)
                for t in range(T2):
                    last = nc.vector.scalar_tensor_tensor(h2[:, t, :], ps[:, 3, t * C:(t + 1) * C], rt[:, t:t + 1],
                                                          h_all[:, tile(b, t), :].rearrange("p a c -> p (a c)"),
                                                          ALU.mult, ALU.add)
                last.then_inc(h2_ready, 1)
                dve.wait_ge(h2_ready, b + 1)
                for t in range(T2):
                    last = nc.vector.bn_stats(st6[:, t, :], h2[:, t, :])
                last.then_inc(bn2_done, 1)
                dve.wait_ge(consts, 1)
                dve.wait_ge(bn2_done, b + 1)
                for t in range(T2):
                    last = nc.vector.bn_aggr(mv[:, t, :], st6[:, t, :])
                last.then_inc(mv2_done, 1)
                dve.wait_ge(mv2_done, b + 1)
                nc.vector.tensor_scalar(ve[:], mv[:, :, 1], 1e-5, None, ALU.add).then_inc(ve3_done, 1)

            def take_u3(b):
                dve.wait_ge(r3_done, b + 1)
                if not (isinstance(b, int) and b == 0):
                    dve.wait_ge(yt_done, b)
                for t in range(T2):
                    nc.vector.tensor_scalar(u3_all[:, tile(b, t), :].rearrange("p a c -> p (a c)"), h2[:, t, :],
                                            mv[:, t, 0:1], r1[:, t:t + 1], ALU.subtract, ALU.mult)
                    last = nc.vector.tensor_scalar(uu[:, t, :], h2[:, t, :], mv[:, t, 0:1], rr[:, t:t + 1],
                                                   ALU.subtract, ALU.mult)
                last.then_inc(yh_ready, 1)

            def take_yT(b):
                dve.wait_ge(yt_done, b + 1)
                if isinstance(b, int) and b:
                    dve.wait_ge(yT_ready, b)
                nc.vector.tensor_copy(yhT[:].rearrange("p a n -> p (a n)"), ps[0:HC, TR2, :]).then_inc(yhT_ready, 1)

            def take_logits(b):
                dve.wait_ge(lg_done, b + 1)
                for t in range(T2):
                    last = nc.vector.tensor_scalar(lg[:, t, bass.ds(b, 1), :].rearrange("p b e -> p (b e)"),
                                                   psLg[:, t * E:(t + 1) * E], s2[:, t:t + 1], None, ALU.mult)
                last.then_inc(lg_ready, 1)

            def stage2(s, p):
                project, next_x, mixing, output, routing = parts2(s)
                if output:
                    take_y(s - 2, p)
                if next_x:
                    normal_x(s + 1, 1 - p)
                if project:
                    convolve(s, 0)
                if routing:
                    take_u3(s - 3)
                if project:
                    step_sizes_v(s)
                if mixing:
                    weigh_x(s - 1, 1 - p, 0)
                if project:
                    convolve(s, 1)
                if mixing:
                    weigh_x(s - 1, 1 - p, 1)
                    decay_x(s - 1)
                if project:
                    step_sizes_e(s)
                if routing:
                    take_yT(s - 3)
                if mixing:
                    mask_g(s - 1)
                    mix_decays(s - 1, 1 - p)
                if routing:
                    take_logits(s - 3)
                if output:
                    mean_square(s - 2)
                if project:
                    step_sizes_a(s, p)
                if output:
                    take_h2(s - 2)

            sums_beside(B - 1)
            normalise(B - 1, False)
            dve.wait_ge(w_rest, W_REST)
            normal_x(0, 0)
            dve.wait_ge(w2x_loaded, 16)
            nc.vector.tensor_tensor(w2[:], w2[:], w2x, ALU.add).then_inc(w2_ready, 1)
            take_h(B - 1, 0)
            for c in range(XC):
                last = nc.vector.tensor_scalar(wout[:, c, :], wout[:, c, :], rms[:, c:c + 1], None, ALU.mult)
            last.then_inc(setup, 1)
            take_h(B - 1, 1)
            stats1(B - 1)
            dve.wait_ge(alog_exp, 1)
            nc.vector.tensor_scalar(aneg[:], small[:, 11, 0:SH], -1.0, None, ALU.mult).then_inc(setup, 1)
            dve.wait_ge(setup, 2)
            dve.wait_ge(fills, 1)
            over_stages2(dve, stage2)

            nc.vector.tensor_copy(nest[:], nestf[:, 0:2 * (HC + 1)]).then_inc(w2_ready, 1)
            nc.vector.tensor_tensor(b2[:], b2[:], b2x[:], ALU.add).then_inc(w2_ready, 1)
            lgf = lg[:].rearrange("p t b e -> p (t b) e")
            tb = [128, T2 * B, E]
            dve.wait_ge(lg_ready, B)
            nc.vector.tensor_reduce(lsm[:, 0, :], lgf, AX.X, ALU.max).then_inc(ch_step, 1)
            dve.wait_ge(ch_step, 1)
            nc.vector.tensor_tensor(lgf, lgf, lsm[:, 0, :].unsqueeze(2).broadcast_to(tb), ALU.subtract).then_inc(ch_step, 1)
            dve.wait_ge(ch_exp, 1)
            nc.vector.tensor_reduce(lsm[:, 1, :], pe_[:], AX.X, ALU.add).then_inc(ch_step, 1)
            dve.wait_ge(ch_step, 3)
            nc.vector.reciprocal(lsm[:, 2, :], lsm[:, 1, :]).then_inc(ch_step, 1)
            dve.wait_ge(ch_step, 4)
            nc.vector.tensor_tensor(pe_[:], pe_[:], lsm[:, 2, :].unsqueeze(2).broadcast_to(tb), ALU.mult).then_inc(ch_step, 2)
            dve.wait_ge(pr_done, 1)
            nc.vector.tensor_copy(pr[:], ps[0:32, 0, 0:L]).then_inc(ch_step, 1)
            src, n = pr[:], 7
            for i in range(CAP // 8):
                dve.wait_ge(ch_step, n)
                nc.vector.max(top8[:], src).then_inc(ch_step, 1)
                dve.wait_ge(ch_step, n + 1)
                nc.vector.match_replace(pick[:, i % 2, :], top8[:], src, -1.0).then_inc(ch_step, 1)
                src, n = pick[:, i % 2, :], n + 2
            dve.wait_ge(ch_step, n)
            nc.vector.tensor_scalar(sel[:], src, 0.0, None, ALU.is_lt).then_inc(sel_ready, 1)
            dve.wait_ge(sel_ready, 1)
            nc.vector.tensor_tensor(gsel[:], pr[:], sel[:], ALU.mult).then_inc(sel_ready, 1)

            def take_yhat(c):
                dve.wait_ge(m_done, c + 1)
                if not (isinstance(c, int) and c == 0):
                    dve.wait_ge(v3_done, c)
                nc.vector.tensor_tensor(yhat[:], yT_all[:, :, bass.ds(c * L, L)],
                                        ps[0:HC + 1, 1, :].rearrange("p (a n) -> p a n", a=2),
                                        ALU.mult).then_inc(yhat_ready, 1)

            def low_yhat(c, p):
                dve.wait_ge(yhat_high, c + 1)
                nc.vector.tensor_tensor(yhl[p][:, 1], yhat[:], yhl[p][:, 0].bitcast(F32),
                                        ALU.subtract).then_inc(yhat_split, 1)

            def low_q3(c):
                dve.wait_ge(q3_ready, c + 1)
                nc.vector.tensor_tensor(qhl[:, 1].rearrange("p a n -> p (a n)"), ps[0:HC, 0, :],
                                        qhl[:, 0].rearrange("p a n -> p (a n)").bitcast(F32),
                                        ALU.subtract).then_inc(q3_split, 1)

            def low_k3(c):
                dve.wait_ge(k3_ready, c + 1)
                nc.vector.scalar_tensor_tensor(khl3[:, 1].rearrange("p a n -> p (a n)"), ps[0:HC, 1, :], SCALE,
                                               khl3[:, 0].rearrange("p a n -> p (a n)").bitcast(F32),
                                               ALU.mult, ALU.subtract).then_inc(k3_split, 1)

            def take_mlp(c, p, j, bank):
                dve.wait_ge(m3_done, c * 3 + j + 1)
                if j == 0 and not (isinstance(c, int) and c < 2):
                    dve.wait_ge(f_done, c * 2 - 2)
                nc.vector.tensor_copy(y2T[p][:, 2 * j:2 * j + 2, :].rearrange("p j n -> p (j n)"),
                                      ps[:, bank, :]).then_inc(m3_read, 1)

            def take_out(b, t):
                dve.wait_ge(f_done, b * 2 + t + 1)
                if t == 0 and not (isinstance(b, int) and b == 0):
                    dve.wait_ge(res_ready, b)
                nc.vector.tensor_tensor(res[:, t, :], ps[:, 0, 0:C], b2[:], ALU.add).then_inc(res_step, 1)
                dve.wait_ge(res_step, b * 2 + t + 1)
                nc.vector.tensor_tensor(res[:, t, :], res[:, t, :], ps[:, 0, C:2 * C], ALU.mult).then_inc(f_read, 1)

            def stage3(b, p):
                last = isinstance(b, int) and b == B - 1
                first = isinstance(b, int) and b == 0
                n0 = B * U + b * U
                for u in range(U):
                    if u == 1 and not first:
                        sums_beside(B + b - 1)
                    if u == 4 and not first:
                        normalise(B + b - 1, True)
                    if u < U - 2 or not last:
                        unit_max(n0 + u + 2, u + 2)
                    unit_copy(n0 + u, u)
                    if u in (6, 8) and not last and not (isinstance(b, int) and b == B - 2):
                        if u == 6:
                            take_yhat(b + 2)
                        else:
                            low_yhat(b + 2, p)
                    if u in (9, 10, 11) and not last:
                        take_mlp(b + 1, 1 - p, (9, 10, 11).index(u), 0 if u == 10 else 1)
                    if u == 0 and not last:
                        low_q3(b + 1)
                    if u == 1 and not last:
                        low_k3(b + 1)
                    if u in (5, 7) and not first:
                        take_out(b - 1, (u - 5) // 2)

            take_yhat(0)
            low_yhat(0, 0)
            low_q3(0)
            low_k3(0)
            for j in range(3):
                take_mlp(0, 0, j, (1, 0, 1)[j])
            take_yhat(1)
            low_yhat(1, 1)
            unit_max(B * U, 0)
            unit_max(B * U + 1, 1)
            over_split_batches(dve, stage3)
            sums_beside(2 * B - 1)
            normalise(2 * B - 1, True)
            take_out(B - 1, 0)
            take_out(B - 1, 1)

        @block.scalar
        def _(act):
            def unit_exp(n, u):
                act.wait_ge(max_done, n + 1)
                if not isinstance(n, int) or n >= 3:
                    act.wait_ge(t_done, n - 2)
                for i in range(2):
                    last = nc.scalar.activation(prob[:, u % 3, i * 256:(i + 1) * 256],
                                                ps[:, SC + u % 3, i * 256:(i + 1) * 256], ACT.Exp,
                                                bias=nmax[:, u % 4, i:i + 1])
                last.then_inc(exp_done, 1)

            def take_k(c, p, k, bank):
                tb, half = divmod(k, 2)
                act.wait_ge(k_done, c * 4 + k + 1)
                if not (isinstance(c, int) and c == 0):
                    wait_k_stacked(c, tb)
                nc.scalar.activation(khl[:, 0, half, tb * 512:(tb + 1) * 512], ps[0:HC, bank, :],
                                     ACT.Copy, scale=SCALE).then_inc(k_ready, 1)

            def wait_k_stacked(c, tb):
                act.wait_ge(k_stacked[tb], c * 16 * KD)

            def take_v(c, p, k, bank):
                act.wait_ge(v_done, c * 4 + k + 1)
                if not (isinstance(c, int) and c == 0):
                    act.wait_ge(pv_done, (c - 1) * U + 3 * (k + 1))
                nc.scalar.activation(va[:, 2 * k:2 * k + 2, :, 0:D],
                                     ps[:, bank, 0:2 * C].rearrange("p (t h e) -> p t h e", t=2, e=D),
                                     ACT.Copy).then_inc(v_ready, 1)

            def high_q(c):
                act.wait_ge(q_pooled, c * 4 + 4)
                if not (isinstance(c, int) and c == 0):
                    act.wait_ge(q_split, c)
                nc.scalar.activation(qhl[:, 0].rearrange("p a n -> p (a n)"), qp[:].rearrange("p a n -> p (a n)"),
                                     ACT.Copy).then_inc(q_high, 1)

            def high_x(c, p):
                for half in range(2):
                    for tb in range(2):
                        if half == 0 and tb == 0:
                            act.wait_ge(x_loaded[p], (c // 2 + 1) * 16 if isinstance(c, int) else (c - p) * 8 + 16)
                            if not (isinstance(c, int) and c == 1):
                                act.wait_ge(k_done, c * 4)
                        where = slice(tb * 512, (tb + 1) * 512)
                        nc.scalar.activation(xhl[:, 0, half, where], xT[p][0:HC + 1, half, where], ACT.Copy).then_inc(x_high, 1)

            def stage1(b, p):
                last = isinstance(b, int) and b == B - 1
                first = isinstance(b, int) and b == 0
                for u in range(U):
                    if u == 0 and not first:
                        take_v(b, p, 3, 1)
                    if u < U - 1 or not last:
                        unit_exp(b * U + u + 1, (u + 1) % U)
                    if last:
                        continue
                    if u == 4:
                        high_q(b + 1)
                    if 4 <= u < 8:
                        take_k(b + 1, 1 - p, u - 4, K_BANKS[u - 4])
                    if 8 <= u < 11:
                        take_v(b + 1, 1 - p, u - 8, u % 2)
                    if u == 8 and not (isinstance(b, int) and b == B - 2):
                        high_x(b + 2, p)

            act.wait_ge(w_first, W_FIRST)
            act.wait_ge(x_first, 32)
            nc.scalar.activation(whl[:, 0], wqkv[:, :, 0:2 * C], ACT.Copy).then_inc(w_high, 1)
            high_q(0)
            for k in range(4):
                take_k(0, 0, k, K_BANKS[k])
            for k in range(4):
                take_v(0, 0, k, k % 2)
            act.wait_ge(consts, 2)
            high_x(1, 1)
            unit_exp(0, 0)
            over_split_batches(act, stage1)

            def square(b):
                act.wait_ge(gt_ready, b + 1)
                if not (isinstance(b, int) and b == 0):
                    act.wait_ge(o2_done, b)
                nc.scalar.activation(gsq_, g_,
                                     ACT.Square).then_inc(gsq_ready, 1)

            def decays(b, p, i):
                if i == 0:
                    act.wait_ge(suf_done, b + 1)
                    if not (isinstance(b, int) and b == 0):
                        act.wait_ge(mix_ready, b * 3)
                act.wait_ge(seg_done, b * 3 + i + 1)
                if i == 2:
                    act.wait_ge(mix_ready, b * 3 + 1)
                nc.scalar.activation(dec[(i + p) % 2][:].rearrange("p (a h) t -> p a (h t)", a=2),
                                     ps[:, SC2:SC2 + 2, 0:384], ACT.Exp).then_inc(dec_ready, 1)
                if i == 0:
                    nc.scalar.activation(esuf[:], psSuf, ACT.Exp).then_inc(suf_ready, 1)

            def take_xn(b):
                act.wait_ge(xt_done, b + 1)
                if not (isinstance(b, int) and b == 0):
                    act.wait_ge(zx_done, b * 4)
                for half in range(2):
                    nc.scalar.activation(xnT[:, half, :], ps[0:HC, TR2, half * L:(half + 1) * L], ACT.Identity,
                                         bias=lnb[:, half:half + 1], scale=lnw[:, half:half + 1]).then_inc(xn_ready, 1)

            def dt_e(b):
                act.wait_ge(dt_step, b * 9 + 2)
                nc.scalar.activation(small[:, 2, :], small[:, 1, :], ACT.Exp, scale=-1.0).then_inc(dt_exp, 1)

            def dt_ln(b):
                act.wait_ge(dt_step, b * 9 + 3)
                nc.scalar.activation(small[:, 4, :], small[:, 3, :], ACT.Ln).then_inc(dt_log, 1)

            def take_x(b):
                for k in range(2):
                    act.wait_ge(zx_done, b * 4 + k + 1)
                    if k == 0 and not (isinstance(b, int) and b == 0):
                        act.wait_ge(conv_step, b * 16)
                    nc.scalar.activation(xpad[:, 2 * k:2 * k + 2, 4:4 + L],
                                         ps[:, k, :].rearrange("p (c t) -> p c t", c=2), ACT.Copy).then_inc(xp_ready, 2)
                    act.wait_ge(xp_ready, b * 4 + 2 * k + 2)
                    act.sem_inc(zx_read, 1)

            def take_z(b, p):
                act.wait_ge(zx_done, b * 4 + 3)
                if not (isinstance(b, int) and b < 2):
                    act.wait_ge(gt_ready, b - 1)
                nc.scalar.activation(sz[:, p, 0:2, :].rearrange("p c t -> p (c t)"), ps[:, 0, :], ACT.Silu).then_inc(zx_read, 1)
                act.wait_ge(zx_done, b * 4 + 4)
                nc.scalar.activation(sz[:, p, 2, :], ps[:, 1, 0:L], ACT.Silu).then_inc(zx_read, 1)

            def convolved(b, p):
                for c in range(XC):
                    act.wait_ge(conv_step, b * 16 + (7, 8, 15)[c])
                    if c == 0 and not (isinstance(b, int) and b < 2):
                        act.wait_ge(y_ready, b - 1)
                    nc.scalar.activation(xc[:, p, c, :], acc[:, c, :], ACT.Silu)
                act.wait_ge(conv_step, b * 16 + 16)
                if not (isinstance(b, int) and b == 0):
                    act.wait_ge(g_done, b)
                for i in range(2):
                    last = nc.scalar.activation(bcT[:, i, :], acc[64 * i:64 * i + 64, 3, :], ACT.Silu)
                last.then_inc(xc_ready, 1)

            def take_y(b):
                act.wait_ge(yhT_ready, b + 1)
                for half in range(2):
                    last = nc.scalar.activation(yT_all[0:HC, half, bass.ds(b * L, L)],
                                                yhT[:, half, :], ACT.Identity,
                                                bias=bet[:, half:half + 1], scale=gam[:, half:half + 1])
                last.then_inc(yT_ready, 1)

            def stage2(s, p):
                project, next_x, mixing, output, routing = parts2(s)
                if project:
                    take_x(s)
                if next_x and not mixing:
                    take_xn(s + 1)
                if project:
                    dt_e(s)
                if mixing:
                    decays(s - 1, 1 - p, 0)
                if output:
                    square(s - 2)
                if mixing:
                    decays(s - 1, 1 - p, 1)
                    decays(s - 1, 1 - p, 2)
                if next_x and mixing:
                    take_xn(s + 1)
                if project:
                    dt_ln(s)
                    take_z(s, p)
                    convolved(s, p)
                if routing:
                    take_y(s - 3)

            act.wait_ge(w_rest, W_REST)
            nc.scalar.activation(small[:, 11, 0:SH], aneg[:], ACT.Exp).then_inc(alog_exp, 1)
            take_xn(0)
            over_stages2(act, stage2)

            act.wait_ge(ch_step, 2)
            nc.scalar.activation(pe_[:].rearrange("p a e -> p (a e)"), lg[:].rearrange("p t b e -> p (t b e)"),
                                 ACT.Exp).then_inc(ch_exp, 1)

            act.wait_ge(h2_used, B)
            act.wait_ge(lg_ready, B)
            nc.scalar.activation(w1hl[:, 0], w1[:, :, 0:MLP + 2 * C], ACT.Copy).then_inc(w1_high, 1)

            def high_yhat(c, p):
                act.wait_ge(yhat_ready, c + 1)
                nc.scalar.activation(yhl[p][:, 0], yhat[:], ACT.Copy).then_inc(yhat_high, 1)

            def take_q3(c):
                act.wait_ge(q3_done, c + 1)
                if isinstance(c, int) and c == 1:
                    for group in first3:
                        act.wait_ge(group, 16 * 9)
                nc.scalar.activation(qhl[:, 0].rearrange("p a n -> p (a n)"), ps[0:HC, 0, :],
                                     ACT.Copy).then_inc(q3_ready, 1)

            def take_k3(c, p):
                act.wait_ge(k3_done, c + 1)
                nc.scalar.activation(khl3[:, 0].rearrange("p a n -> p (a n)"), ps[0:HC, 1, :],
                                     ACT.Copy, scale=SCALE).then_inc(k3_ready, 1)

            def take_v3(c, p):
                act.wait_ge(v3_done, c + 1)
                if not (isinstance(c, int) and c < 2):
                    act.wait_ge(pv_done, B * U + (c - 1) * U)
                nc.scalar.activation(va3[p][:, :, :, 0:D], ps[:, 0, 0:T2 * C].rearrange("p (t h e) -> p t h e", t=T2, e=D),
                                     ACT.Copy).then_inc(v3_ready, 1)

            def gelu(c, p):
                act.wait_ge(m3_read, c * 3 + 3)
                y = y2T[p].rearrange("p j n -> p (j n)")
                nc.scalar.activation(y, y, ACT.Gelu).then_inc(gelu_done, 1)

            def stage3(b, p):
                last = isinstance(b, int) and b == B - 1
                for u in range(U):
                    if u < U - 1 or not last:
                        unit_exp(B * U + b * U + u + 1, (u + 1) % U)
                    if u == 8:
                        gelu(b, p)
                    if last:
                        continue
                    if u == 0:
                        take_q3(b + 1)
                    if u == 1:
                        take_k3(b + 1, 1 - p)
                    if u == 3:
                        take_v3(b + 1, 1 - p)
                    if u == 7 and not (isinstance(b, int) and b == B - 2):
                        high_yhat(b + 2, p)

            high_yhat(0, 0)
            take_q3(0)
            take_k3(0, 0)
            take_v3(0, 0)
            high_yhat(1, 1)
            unit_exp(B * U, 0)
            over_split_batches(act, stage3)

        @block.gpsimd
        def _(pool):
            filled = [(xT[0][HC:HC + 1, :, :], 1.0), (xT[1][HC:HC + 1, :, :], 1.0), (va_ones(areaV1[:, :], N // 128), 1.0),
                      (ones[:], 1.0), (mhalf[:], -0.5), (eps5[:], 1e-5), (eps6[:], 1e-6)]
            for i, (where, value) in enumerate(filled):
                if i:
                    pool.wait_ge(consts, i)
                nc.gpsimd.memset(where, value).then_inc(consts, 1)

            def spread_q(c):
                for half in range(2):
                    pool.wait_ge(q_high, c + 1)
                    if not (isinstance(c, int) and c == 0):
                        pool.wait_ge(s_done, (c - 1) * U + 1)
                    last = nc.gpsimd.tensor_tensor(
                        qmhl[:, 0, half, :].rearrange("p (w e q) -> p w e q", w=W, e=2),
                        qhl[:, 0, half, :].bitcast(F32).rearrange("p (w q) -> p w q", w=W).unsqueeze(2)
                        .broadcast_to([HC, W, 2, QW]),
                        hm[:].unsqueeze(1).unsqueeze(3).broadcast_to([HC, W, 2, QW]), ALU.mult)
                last.then_inc(q_split, 1)
                pool.wait_ge(q_split, c + 1)

            def low_x(c, p):
                for half in range(2):
                    for tb in range(2):
                        n = 2 * half + tb
                        where = slice(tb * 512, (tb + 1) * 512)
                        pool.wait_ge(x_high, (c - 1) * 4 + n + 1)
                        nc.gpsimd.tensor_tensor(xhl[:, 1, half, where], xT[p][0:HC + 1, half, where],
                                                xhl[:, 0, half, where].bitcast(F32), ALU.subtract).then_inc(x_low, 1)
                        pool.wait_ge(x_low, (c - 1) * 4 + n + 1)

            def factors(b):
                pool.wait_ge(consts, 7)
                pool.wait_ge(ve_done, b + 1)
                at = b * 4
                r = r1[:]
                nc.gpsimd.tensor_tensor(r1_all[:, bass.ds(b * T2, T2)], ve[:], mhalf[:], ALU.pow)
                nc.gpsimd.tensor_tensor(r, ve[:], mhalf[:], ALU.pow).then_inc(pow_step, 1)
                pool.wait_ge(pow_step, at + 1)
                nc.gpsimd.tensor_tensor(vu[:], mv[:, :, 1], r, ALU.mult).then_inc(pow_step, 1)
                pool.wait_ge(pow_step, at + 2)
                nc.gpsimd.tensor_tensor(vu[:], vu[:], r, ALU.mult).then_inc(pow_step, 1)
                pool.wait_ge(pow_step, at + 3)
                nc.gpsimd.tensor_tensor(ve2[:], vu[:], eps5[:], ALU.add).then_inc(pow_step, 1)
                pool.wait_ge(pow_step, at + 4)
                nc.gpsimd.tensor_tensor(vu[:], ve2[:], mhalf[:], ALU.pow).then_inc(r1_done, 1)
                pool.wait_ge(consts, 7)
                pool.wait_ge(r1_done, b + 1)
                nc.gpsimd.tensor_tensor(rr_all[:, bass.ds(b * T2, T2)], vu[:], r, ALU.mult).then_inc(stat_done, 1)

            def stage1(b, p):
                last = isinstance(b, int) and b == B - 1
                first = isinstance(b, int) and b == 0
                if not last:
                    spread_q(b + 1)
                if not last and not (isinstance(b, int) and b == B - 2):
                    low_x(b + 2, p)
                if not first:
                    factors(b - 1)

            pool.wait_ge(w_first, W_FIRST)
            pool.wait_ge(w_high, 1)
            nc.gpsimd.tensor_tensor(whl[:, 1], wqkv[:, :, 0:2 * C], whl[:, 0].bitcast(F32),
                                    ALU.subtract).then_inc(w_low, 1)
            pool.wait_ge(w_low, 1)
            spread_q(0)
            low_x(1, 1)
            over_split_batches(pool, stage1)

            pool.wait_ge(stat_done, B - 1)
            pool.wait_ge(pv_done, B * U)
            nc.gpsimd.memset(xpad[:, :, 0:4], 0.0).then_inc(fills, 1)
            pool.wait_ge(fills, 1)

            def add_u(b):
                pool.wait_ge(consts, 7)
                pool.wait_ge(xh_ready, b + 1)
                hb = h_all[:, bass.ds(b * T2, T2), :]
                nc.gpsimd.tensor_tensor(hb, hb, uu2[:], ALU.add).then_inc(hu_done, 1)

            def gate(b, p):
                pool.wait_ge(y_ready, b + 1)
                if not (isinstance(b, int) and b == 0):
                    pool.wait_ge(o2_done, b)
                    pool.wait_ge(gsq_ready, b)
                nc.gpsimd.tensor_tensor(g_, y_, sz[:, p].rearrange("p c t -> p (c t)"), ALU.mult).then_inc(gt_ready, 1)

            def factors2(b):
                pool.wait_ge(ms_done, b + 1)
                nc.gpsimd.tensor_tensor(rt[:], ms[:], mhalf[:], ALU.pow).then_inc(rt_done, 1)
                pool.wait_ge(ve3_done, b + 1)
                at = b * 6
                if not (isinstance(b, int) and b == 0):
                    pool.wait_ge(yh_ready, b)
                nc.gpsimd.tensor_tensor(r1[:], ve[:], mhalf[:], ALU.pow).then_inc(pow2_step, 1)
                pool.wait_ge(pow2_step, at + 1)
                nc.gpsimd.tensor_tensor(vu[:], mv[:, :, 1], r1[:], ALU.mult).then_inc(pow2_step, 1)
                pool.wait_ge(pow2_step, at + 2)
                nc.gpsimd.tensor_tensor(vu[:], vu[:], r1[:], ALU.mult).then_inc(pow2_step, 1)
                pool.wait_ge(pow2_step, at + 3)
                nc.gpsimd.tensor_tensor(ve2[:], vu[:], eps6[:], ALU.add).then_inc(pow2_step, 1)
                pool.wait_ge(pow2_step, at + 4)
                nc.gpsimd.tensor_tensor(r2[:], ve2[:], mhalf[:], ALU.pow).then_inc(pow2_step, 1)
                pool.wait_ge(pow2_step, at + 5)
                nc.gpsimd.tensor_tensor(rr[:], r1[:], r2[:], ALU.mult).then_inc(pow2_step, 1)
                if not (isinstance(b, int) and b == 0):
                    pool.wait_ge(lg_ready, b)
                nc.gpsimd.tensor_tensor(s2[:], ve2[:], r2[:], ALU.mult).then_inc(r3_done, 1)

            def residual3(b):
                pool.wait_ge(consts, 7)
                pool.wait_ge(yh_ready, b + 1)
                where = u3_all[:, bass.ds(b * T2, T2), :]
                nc.gpsimd.tensor_tensor(where, where, h2[:], ALU.add).then_inc(h2_used, 1)

            def spread_a(b, p):
                pool.wait_ge(dt_step, b * 9 + 9)
                for t in range(T2):
                    if not (isinstance(b, int) and b == 0):
                        pool.wait_ge(seg_done, b * 3)
                    nc.gpsimd.tensor_tensor(a1[:, t], a2[:, p, t, :].unsqueeze(2).broadcast_to([128, SH, 128]),
                                            upto[:].unsqueeze(1).broadcast_to([128, SH, 128]),
                                            ALU.mult).then_inc(a1_ready, 1)

            def stage2(s, p):
                project, next_x, mixing, output, routing = parts2(s)
                if output:
                    gate(s - 2, p)
                if next_x:
                    add_u(s + 1)
                if routing:
                    residual3(s - 3)
                if output:
                    factors2(s - 2)
                if project:
                    spread_a(s, p)

            add_u(0)
            pool.wait_ge(hu_done, 1)
            factors(B - 1)
            pool.wait_ge(w_rest, W_REST)
            pool.wait_ge(stat_done, B)
            over_stages2(pool, stage2)
            pool.wait_ge(lg_ready, B)
            pool.wait_ge(h2_used, B)
            nc.gpsimd.memset(yT_all[HC:HC + 1, :, :], 1.0).then_inc(consts, 1)
            pool.wait_ge(consts, 8)
            nc.gpsimd.memset(va_ones(areaV3[:].rearrange("p a n -> p (a n)"), 2 * T2), 1.0).then_inc(vones, 1)
            pool.wait_ge(vones, 1)
            nc.gpsimd.memset(qst3[0][:].bitcast(F32), 0.0).then_inc(zeros3, 1)
            pool.wait_ge(zeros3, 1)
            nc.gpsimd.memset(qst3[1][:].bitcast(F32), 0.0).then_inc(zeros3, 1)
            pool.wait_ge(w1_high, 1)
            pool.wait_ge(zeros3, 2)
            nc.gpsimd.tensor_tensor(w1hl[:, 1], w1[:, :, 0:MLP + 2 * C], w1hl[:, 0].bitcast(F32),
                                    ALU.subtract).then_inc(w1_low, 1)

            def take_sel(c):
                pool.wait_ge(consts, 8)
                if isinstance(c, int) and c == 0:
                    pool.wait_ge(sel_ready, 1)
                else:
                    pool.wait_ge(m_done, c)
                nc.gpsimd.tensor_tensor(selb[:], sel[:], rowm[:, bass.ds(c, 1)].broadcast_to([32, L]),
                                        ALU.mult).then_inc(selb_ready, 1)

            def take_gates(c, p):
                pool.wait_ge(consts, 8)
                if isinstance(c, int) and c == 0:
                    pool.wait_ge(sel_ready, 2)
                nc.gpsimd.tensor_tensor(gselb[:, p, :], gsel[:], rowm[:, bass.ds(c, 1)].broadcast_to([32, L]),
                                        ALU.mult).then_inc(gates_ready, 1)

            def add_u3(b):
                pool.wait_ge(f_read, b * 2 + 2)
                nc.gpsimd.tensor_tensor(res2[:], res[:], u3_all[:, bass.ds(b * T2, T2), :], ALU.add).then_inc(res_ready, 1)

            def stage3(b, p):
                last = isinstance(b, int) and b == B - 1
                first = isinstance(b, int) and b == 0
                if not last and not (isinstance(b, int) and b == B - 2):
                    take_sel(b + 2)
                if not first:
                    pool.wait_ge(consts, 8)
                    wait_stored(b - 1, 1 - p)
                    add_u3(b - 1)
                if not last:
                    take_gates(b + 1, 1 - p)

            def wait_stored(b, p):
                if isinstance(b, int) and b == 0:
                    return
                q = 1 - p
                pool.wait_ge(stored[q], (b - 1 - q) * 8 + 16)

            take_sel(0)
            take_gates(0, 0)
            take_sel(1)
            over_split_batches(pool, stage3)
            wait_stored(B - 1, 1)
            add_u3(B - 1)


def va_ones(area, tiles):
    return area.rearrange("p (t e) -> p t e", e=32)[:, 0:tiles * H, D:32]


def _layouts(v):
    f = np.float32

    def halves(a):
        got = np.zeros((HC + 1, 2, a.shape[1]), f)
        got[:HC, 0], got[:HC, 1] = a[:HC], a[HC:C]
        if a.shape[0] > C:
            got[HC, 1] = a[C]
        return got if a.shape[0] > C else np.ascontiguousarray(got[:HC])

    def heads(a):
        got = np.zeros((128, G3, a.shape[1]), f)
        for h in range(H):
            got[32 * (h % 4):32 * (h % 4) + D, h // 4] = a[h * D:(h + 1) * D]
        return got

    def chunks(a):
        return np.ascontiguousarray(a.reshape((-1, 128) + a.shape[1:]).swapaxes(0, 1))

    x = v["x"].reshape(B, STRIDE, QW, W, C)
    x = x.transpose(0, 4, 3, 1, 2).reshape(B, 2, HC, N).transpose(0, 2, 1, 3)
    w2 = v["L0_ffn_w2"].reshape(2, C, MLP + C).transpose(0, 2, 1)
    r, c = np.arange(128)[:, None], np.arange(128)[None, :]
    keeps = [C >> (E - 1 - e) for e in range(E)]
    inside = np.array([[ch < keeps[e % E] for ch in range(C)] for e in range(B * E)], f)
    nest = np.ones((B * E, 2 * (HC + 1) + C), f)
    nest[:, 0:HC], nest[:, HC + 1:2 * HC + 1], nest[:, 2 * HC + 2:] = inside[:, :HC], inside[:, HC:], inside
    return {
        "x": x,
        "wqkv": halves(np.concatenate([v["L0_tok_qkv_w"].T, v["L0_tok_qkv_b"][None]])),
        "wo": heads(v["L0_tok_proj_w"].T), "bo": v["L0_tok_proj_b"],
        "win": halves(v["L0_attn_W_in"]),
        "lnw": v["L0_attn_ln_w"].reshape(2, HC).T, "lnb": v["L0_attn_ln_b"].reshape(2, HC).T,
        "cw": chunks(v["L0_attn_conv_w"]), "cb": chunks(v["L0_attn_conv_b"]),
        "dtb": v["L0_attn_dt_bias"], "alog": v["L0_attn_A_log"],
        "dd": chunks(np.repeat(v["L0_attn_D"], 64)), "rms": chunks(v["L0_attn_rms_w"]),
        "wout": chunks(v["L0_attn_W_out"]), "wr": halves(v["L0_ffn_w_router"].T),
        "gam": v["L0_ffn_gamma1"].reshape(2, HC).T, "bet": v["L0_ffn_beta1"].reshape(2, HC).T,
        "w1": halves(np.concatenate([v["L0_ffn_w1"].T, v["L0_ffn_b1"][None]])),
        "w2": np.stack([np.concatenate([chunks(w[:MLP]), heads(w[MLP:])], 1) for w in w2]),
        "b2": v["L0_ffn_b2"].reshape(2, C),
        "hm": np.arange(HC)[:, None] // D % 2 == np.arange(2)[None, :],
        "later": r > c, "upto": r <= c, "eye": r == c,
        "nest": nest, "row": np.arange(B * E)[:, None] // E == np.arange(B)[None, :],
    }


def kernel(**inputs):
    import concourse.bacc as _bacc
    from concourse import mybir as _mybir
    from concourse.bass_utils import run_bass_kernel_spmd as _run

    nc = _bacc.Bacc("TRN2", target_bir_lowering=False, num_devices=1)
    laid = _layouts({k: np.asarray(a) for k, a in inputs.items()})
    arrays, args = {}, []
    for name, a in laid.items():
        a = np.ascontiguousarray(a, dtype=np.float32)
        arrays[f"in_{name}_dram"] = a
        args.append(nc.dram_tensor(f"in_{name}_dram", a.shape, _mybir.dt.float32, kind="ExternalInput").ap())
    out = nc.dram_tensor("out_dram", (B, L, C), _mybir.dt.float32, kind="ExternalOutput").ap()
    audio_tower(nc, *args, out)
    r = _run(nc, [arrays], core_ids=[0])
    return r.results[0]["out_dram"]
```
